# Optimizing a Trainium2 kernel written in Bass

```python
import numpy as np
import jax
import jax.numpy as jnp

def _softmax(x, axis=-1):
    return jax.nn.softmax(x, axis=axis)

def _gelu(x):
    return jax.nn.gelu(x, approximate=True)

def _silu(x):
    return jax.nn.silu(x)

def _sigmoid(x):
    return jax.nn.sigmoid(x)

def _layernorm(x, axis=-1, eps=1e-05):
    m = jnp.mean(x, axis=axis, keepdims=True)
    v = jnp.var(x, axis=axis, keepdims=True)
    return (x - m) / jnp.sqrt(v + eps)

def _scatter_add(tgt, idx, src, axis=0):
    return tgt.at[idx].add(src)

def _segment_sum(src, seg, n):
    return jax.ops.segment_sum(src, seg, n)
kernel_name = 'mk_decoder_postln_d1_seqx_r4_e46210'

def setup_inputs(seed: int=0):
    np.random.seed(seed)
    _w = jnp.asarray

    def _rec_inputs():
        import jax
        import jax.numpy as jnp
        _rk = jax.random.key(seed)
        x = 7.22e-05 + 1 * jax.random.normal(jax.random.fold_in(_rk, 1), (4, 512, 512), jnp.float32)
        _lenS = 512 - jax.random.randint(jax.random.fold_in(_rk, 7), (4,), 0, max(1, 512 // 4) + 1, jnp.int32)
        _lenS2 = 512 - jax.random.randint(jax.random.fold_in(_rk, 8), (4,), 0, max(1, 512 // 4) + 1, jnp.int32)
        _ctx_1024P = jax.random.normal(jax.random.fold_in(_rk, 11), (4, 16, 256), jnp.float32)
        _ctx_1024c = jax.random.dirichlet(jax.random.fold_in(_rk, 511), 0.3 * jnp.ones((16,), jnp.float32), (4, 512))
        _ctx_1024t = jnp.einsum('bsk,bkd->bsd', _ctx_1024c, _ctx_1024P)
        _ctx_1024t = _ctx_1024t * jax.lax.rsqrt(jnp.mean(jnp.square(_ctx_1024t)) + 1e-12) * 0.953939
        ctx_1024 = 2.81802e-05 + 1.00001 * (_ctx_1024t + 0.3 * jax.random.normal(jax.random.fold_in(_rk, 611), (4, 512, 256), jnp.float32))
        return (x, ctx_1024)
    x, ctx_1024 = _rec_inputs()

    def _L0_attn_setup():
        import jax, jax.numpy as jnp
        import numpy as np
        HIDDEN = 512
        NUM_HEADS = 16
        HEAD_SIZE = HIDDEN // NUM_HEADS
        SEQ = 512
        BATCH = 2

        def alibi_causal_bias(seq_len: int, num_heads: int) -> jnp.ndarray:
            i = jnp.arange(seq_len)[:, None]
            j = jnp.arange(seq_len)[None, :]
            dist = -(i - j).astype(jnp.float32)
            causal = jnp.where(j > i, -jnp.inf, 0.0)
            base = jnp.where(j > i, 0.0, dist) + causal
            if num_heads <= 8:
                slopes = jnp.asarray([1.0 / 2 ** k for k in range(num_heads)], jnp.float32)
            else:
                slopes = jnp.asarray([1.0 / 2 ** (k / 2) for k in range(num_heads)], jnp.float32)
            return slopes[None, :, None, None] * dist[None, None] * (j <= i)[None, None] + causal[None, None]
        key = jax.random.key(seed)
        ks = jax.random.split(key, 3)
        sd = 1.0 / np.sqrt(HIDDEN)
        return {'x': jax.random.normal(ks[0], (BATCH, SEQ, HIDDEN), jnp.float32), 'Wqkv': jax.random.normal(ks[1], (HIDDEN, 3 * HIDDEN), jnp.float32) * sd, 'bqkv': jnp.zeros((3 * HIDDEN,), jnp.float32), 'Wo': jax.random.normal(ks[2], (HIDDEN, HIDDEN), jnp.float32) * sd, 'bo': jnp.zeros((HIDDEN,), jnp.float32)}
    _L0_attn_all = _L0_attn_setup()
    _L0_attn_in = {k: v for k, v in _L0_attn_all.items() if k in ('Wqkv', 'bqkv', 'Wo', 'bo')}
    del _L0_attn_all

    def _L0_xattn_setup():
        import jax, jax.numpy as jnp
        import numpy as np
        key = jax.random.key(seed)
        ks = jax.random.split(key, 6)
        B, L, N, C, D = (8, 128, 512, 256, 128)
        return {'teacher_logits': jax.random.normal(ks[0], (B, L, N), dtype=jnp.float32), 'teacher_features': jax.random.normal(ks[1], (B, N, C), dtype=jnp.float32), 'Wq': jax.random.normal(ks[2], (D, C), dtype=jnp.float32) * (1.0 / np.sqrt(C)), 'bq': jnp.zeros((D,), dtype=jnp.float32), 'Wk': jax.random.normal(ks[3], (D, C), dtype=jnp.float32) * (1.0 / np.sqrt(C)), 'bk': jnp.zeros((D,), dtype=jnp.float32)}
    _L0_xattn_all = _L0_xattn_setup()
    _L0_xattn_in = {k: v for k, v in _L0_xattn_all.items() if k in ('Wq', 'bq', 'Wk', 'bk')}
    del _L0_xattn_all

    def _L0_ffn_setup():
        import jax, jax.numpy as jnp
        import numpy as np
        H = 512
        I = 2048
        NE = 8
        S = 2
        N = NE - S
        K = N
        E = I // NE
        C = 2
        RESIDUAL = True
        B, L = (2, 512)

        def _swiglu(h, W, b):
            return jax.nn.silu(h @ W + b) * h
        key = jax.random.key(seed)
        ks = jax.random.split(key, 16)
        s = 0.02
        inp = {'x': jax.random.normal(ks[0], (B, L, H), dtype=jnp.float32), 'Wg': jax.random.normal(ks[1], (C, H, NE)) * s, 'bg': jnp.zeros((C, NE)), 'Wup': jax.random.normal(ks[2], (N, H, E)) * s, 'bup': jnp.zeros((N, E)), 'Wsw': jax.random.normal(ks[3], (N, E, E)) * s, 'bsw': jnp.zeros((N, E)), 'Wdn': jax.random.normal(ks[4], (N, E, H)) * s, 'bdn': jnp.zeros((N, H)), 'Wsu': jax.random.normal(ks[5], (H, S * E)) * s, 'bsu': jnp.zeros((S * E,)), 'Wsa': jax.random.normal(ks[6], (E, E)) * s, 'bsa': jnp.zeros((E,)), 'Wsd': jax.random.normal(ks[7], (S * E, H)) * s, 'bsd': jnp.zeros((H,))}
        return inp
    _L0_ffn_all = _L0_ffn_setup()
    _L0_ffn_in = {k: v for k, v in _L0_ffn_all.items() if k in ('Wg', 'bg', 'Wup', 'bup', 'Wsw', 'bsw', 'Wdn', 'bdn', 'Wsu', 'bsu', 'Wsa', 'bsa', 'Wsd', 'bsd')}
    del _L0_ffn_all
    return {'x': x, 'ctx_1024': ctx_1024, 'L0_attn_Wqkv': _L0_attn_in['Wqkv'], 'L0_attn_bqkv': _L0_attn_in['bqkv'], 'L0_attn_Wo': _L0_attn_in['Wo'], 'L0_attn_bo': _L0_attn_in['bo'], 'L0_xattn_Wq': _L0_xattn_in['Wq'], 'L0_xattn_bq': _L0_xattn_in['bq'], 'L0_xattn_Wk': _L0_xattn_in['Wk'], 'L0_xattn_bk': _L0_xattn_in['bk'], 'L0_ffn_Wg': _L0_ffn_in['Wg'], 'L0_ffn_bg': _L0_ffn_in['bg'], 'L0_ffn_Wup': _L0_ffn_in['Wup'], 'L0_ffn_bup': _L0_ffn_in['bup'], 'L0_ffn_Wsw': _L0_ffn_in['Wsw'], 'L0_ffn_bsw': _L0_ffn_in['bsw'], 'L0_ffn_Wdn': _L0_ffn_in['Wdn'], 'L0_ffn_bdn': _L0_ffn_in['bdn'], 'L0_ffn_Wsu': _L0_ffn_in['Wsu'], 'L0_ffn_bsu': _L0_ffn_in['bsu'], 'L0_ffn_Wsa': _L0_ffn_in['Wsa'], 'L0_ffn_bsa': _L0_ffn_in['bsa'], 'L0_ffn_Wsd': _L0_ffn_in['Wsd'], 'L0_ffn_bsd': _L0_ffn_in['bsd']}

def reference(x, ctx_1024, L0_attn_Wqkv, L0_attn_bqkv, L0_attn_Wo, L0_attn_bo, L0_xattn_Wq, L0_xattn_bq, L0_xattn_Wk, L0_xattn_bk, L0_ffn_Wg, L0_ffn_bg, L0_ffn_Wup, L0_ffn_bup, L0_ffn_Wsw, L0_ffn_bsw, L0_ffn_Wdn, L0_ffn_bdn, L0_ffn_Wsu, L0_ffn_bsu, L0_ffn_Wsa, L0_ffn_bsa, L0_ffn_Wsd, L0_ffn_bsd):
    import jax
    import jax.numpy as jnp

    def _L0_attn_ref(x, Wqkv, bqkv, Wo, bo):
        import jax, jax.numpy as jnp
        import numpy as np
        HIDDEN = 512
        NUM_HEADS = 16
        HEAD_SIZE = HIDDEN // NUM_HEADS
        SEQ = 512
        BATCH = 2

        def alibi_causal_bias(seq_len: int, num_heads: int) -> jnp.ndarray:
            i = jnp.arange(seq_len)[:, None]
            j = jnp.arange(seq_len)[None, :]
            dist = -(i - j).astype(jnp.float32)
            causal = jnp.where(j > i, -jnp.inf, 0.0)
            base = jnp.where(j > i, 0.0, dist) + causal
            if num_heads <= 8:
                slopes = jnp.asarray([1.0 / 2 ** k for k in range(num_heads)], jnp.float32)
            else:
                slopes = jnp.asarray([1.0 / 2 ** (k / 2) for k in range(num_heads)], jnp.float32)
            return slopes[None, :, None, None] * dist[None, None] * (j <= i)[None, None] + causal[None, None]
        b, s, h = x.shape
        scale = 1.0 / np.sqrt(HEAD_SIZE)
        qkv = x @ Wqkv + bqkv
        q, k, v = jnp.split(qkv, 3, axis=-1)

        def heads(t):
            return t.reshape(b, s, NUM_HEADS, HEAD_SIZE).transpose(0, 2, 1, 3)
        q, k, v = (heads(q), heads(k), heads(v))
        scores = jnp.einsum('bhid,bhjd->bhij', q, k) * scale
        scores = scores + alibi_causal_bias(s, NUM_HEADS)
        attn = jax.nn.softmax(scores, axis=-1)
        out = jnp.einsum('bhij,bhjd->bhid', attn, v)
        out = out.transpose(0, 2, 1, 3).reshape(b, s, NUM_HEADS * HEAD_SIZE)
        return out @ Wo + bo

    def _L0_xattn_ref(teacher_logits, teacher_features, Wq, bq, Wk, bk):
        import jax, jax.numpy as jnp
        import numpy as np
        query = jnp.einsum('bnc,dc->bnd', teacher_features, Wq) + bq
        key = jnp.einsum('bnc,dc->bnd', teacher_features, Wk) + bk
        energy = jnp.einsum('bnd,bmd->bnm', query, key)
        attention = jax.nn.softmax(energy, axis=-1)
        x_m = jnp.einsum('bln,bmn->blm', teacher_logits, attention)
        return x_m

    def _L0_ffn_ref(x, Wg, bg, Wup, bup, Wsw, bsw, Wdn, bdn, Wsu, bsu, Wsa, bsa, Wsd, bsd):
        import jax, jax.numpy as jnp
        import numpy as np
        H = 512
        I = 2048
        NE = 8
        S = 2
        N = NE - S
        K = N
        E = I // NE
        C = 2
        RESIDUAL = True
        B, L = (2, 512)

        def _swiglu(h, W, b):
            return jax.nn.silu(h @ W + b) * h
        bsz, seq, _ = x.shape
        xt = x.reshape(-1, H)
        res = xt
        for j in range(C):
            gate = xt @ Wg[j] + bg[j]
            _, ids = jax.lax.top_k(gate, K)
            in_top = jax.nn.one_hot(ids, NE, dtype=gate.dtype).sum(-2) > 0
            w = jax.nn.softmax(jnp.where(in_top, gate, -jnp.inf), axis=-1)
            h = jnp.einsum('th,nhe->nte', xt, Wup) + bup[:, None, :]
            h = jax.nn.silu(jnp.einsum('nte,nef->ntf', h, Wsw) + bsw[:, None, :]) * h
            eo = jnp.einsum('nte,neh->nth', h, Wdn) + bdn[:, None, :]
            out = jnp.einsum('nth,tn->th', eo, w[:, :N])
            sh = (xt @ Wsu + bsu).reshape(-1, S, E)
            sh = _swiglu(sh, Wsa, bsa)
            out = out + sh.reshape(-1, S * E) @ Wsd + bsd
            xt = res + out if RESIDUAL else out
        return xt.reshape(bsz, seq, H)
    x = _layernorm(x + _L0_attn_ref(x, L0_attn_Wqkv, L0_attn_bqkv, L0_attn_Wo, L0_attn_bo), axis=-1)
    x = _layernorm(x + _L0_xattn_ref(x, ctx_1024, L0_xattn_Wq, L0_xattn_bq, L0_xattn_Wk, L0_xattn_bk), axis=-1)
    x = _layernorm(x + _L0_ffn_ref(x, L0_ffn_Wg, L0_ffn_bg, L0_ffn_Wup, L0_ffn_bup, L0_ffn_Wsw, L0_ffn_bsw, L0_ffn_Wdn, L0_ffn_bdn, L0_ffn_Wsu, L0_ffn_bsu, L0_ffn_Wsa, L0_ffn_bsa, L0_ffn_Wsd, L0_ffn_bsd), axis=-1)
    return x

_drawn_inputs = setup_inputs


def setup_inputs(seed=0):
    import zlib

    import numpy as np

    out = dict(_drawn_inputs(seed))
    spreads = {'L0_attn_bqkv': (0.0, 0.1),
     'L0_attn_bo': (0.0, 0.1),
     'L0_xattn_bq': (0.0, 0.1),
     'L0_xattn_bk': (0.0, 2.0),
     'L0_ffn_bg': (0.0, 0.8),
     'L0_ffn_bup': (0.0, 0.8),
     'L0_ffn_bsw': (0.0, 0.8),
     'L0_ffn_bdn': (0.0, 0.444),
     'L0_ffn_bsu': (0.0, 0.8),
     'L0_ffn_bsa': (0.0, 0.8),
     'L0_ffn_bsd': (0.0, 0.397)}
    factors = {'L0_ffn_Wg': 5.291,
     'L0_ffn_Wup': 8.0,
     'L0_ffn_Wsw': 8.0,
     'L0_ffn_Wdn': 8.0,
     'L0_ffn_Wsu': 5.978,
     'L0_ffn_Wsa': 7.094,
     'L0_ffn_Wsd': 5.944}
    for name, (base, spread) in spreads.items():
        noise = np.random.default_rng([zlib.crc32(name.encode()), seed]).standard_normal(out[name].shape)
        drawn = base * np.exp(spread * noise) if base else spread * noise
        out[name] = jnp.asarray(drawn.astype(out[name].dtype))
    for name, factor in factors.items():
        out[name] = (out[name] * factor).astype(out[name].dtype)
    return out
```

```python
import math
from contextlib import ExitStack

import concourse.bass as bass
from concourse import mybir

F32 = mybir.dt.float32
F32R = mybir.dt.float32r
ALU = mybir.AluOpType
ACT = mybir.ActivationFunctionType
AX = mybir.AxisListType

P = 128
B, S, H = 4, 512, 512
KT = H // P
TT = S // P
EPS = 1e-5
PARTS = [(0, 0), (0, 1), (1, 0)]
ATT_LINKS = 29
FFN_LINKS = 106


def apart(eng, sem, value, passed):
    eng.wait_ge(sem, value)
    eng.sem_inc(passed, 1)


def attention(nc, sems, io, x2_dram, x2t_dram):
    NH, D = 16, 32
    G = P // D
    NG = NH // G
    DX, CT = 128, 2
    LAG = 2
    SCALE = 1.0 / math.sqrt(D)
    MASKED = -1e30
    slope = [1.0 / 2 ** (n / 2) for n in range(NH)]
    SEEN = TT * (TT + 1) // 2 * P
    ROW = [t * (t + 1) // 2 * P for t in range(TT)]
    ORDER = [3, 2, 0, 1]
    COL = {0: 0, 1: TT * P, 3: TT * P + 3 * P, 2: TT * P + 4 * P}
    RING = 3
    with ExitStack() as ctx:
        def sb(name, shape, dt=F32):
            return ctx.enter_context(nc.sbuf_tensor("a_" + name, shape, dt))

        def sem(name):
            return sems.enter_context(nc.semaphore("a_" + name))

        def bank(name):
            return ctx.enter_context(nc.psum_tensor("a_" + name, [P, S], F32))

        HL = ("hi", "lo")
        w_qkv = [sb(f"w_qkv_{s}", [P, 3, KT, H], F32R) for s in HL]
        w_o = [sb(f"w_o_{s}", [P, KT, H], F32R) for s in HL]
        w_x = [sb(f"w_x_{s}", [P, 2, CT, DX], F32R) for s in HL]
        dist = sb("dist", [P, S])
        v_bias = sb("v_bias", [P, H])
        o_bias = sb("o_bias", [P, H])
        x_raw = sb("x_raw", [P, KT, S])
        xt = [sb(f"xt_{s}", [P, KT, S], F32R) for s in HL]
        raw = sb("raw", [P, 2, S])
        inv_sb = sb("inv_sb", [P, S])
        inv_wide = sb("inv_wide", [P, TT, G, D])
        nat = sb("nat", [P, 4, S], F32R)
        stack = [sb(f"stack_{s}", [P, G, S], F32R) for s in ("q", "k")]
        v = sb("v", [P, TT, H])
        probs = sb("probs", [P, RING, SEEN])
        probs_t = sb("probs_t", [P, G, SEEN])
        att = [sb(f"att_{s}", [P, KT, S], F32R) for s in HL]
        x = sb("x", [P, TT, H])
        ct = [sb(f"ct_{s}", [P, CT, S], F32R) for s in HL]
        ident = sb("ident", [P, P])
        q_scale = sb("q_scale", [P, NG])
        qk_bias = sb("qk_bias", [P, 2, NG])
        x_bias = sb("x_bias", [P, 2])
        top = sb("top", [P, 2, TT])
        ntop = sb("ntop", [P, 2, TT])
        total = sb("total", [P, G, TT])
        inv = sb("inv", [P, TT, G])
        stats = sb("stats", [P, TT, 6])
        mv = sb("mv", [P, TT, 2])
        var = sb("var", [P, TT])
        rstd = sb("rstd", [P, TT])
        half = sb("half", [P, 1])

        ab = [bank(f"proj{n}") for n in range(2)]
        s3, s20, s1 = bank("s3"), bank("s20"), bank("s1")
        tb = [bank(f"turn{n}") for n in range(2)]
        av = bank("av")
        scores = {3: s3[:, 0:4 * P], 2: s20[:, 0:3 * P], 0: s20[:, 3 * P:4 * P], 1: s1[:, 0:2 * P]}

        A = {}
        for key in [("q", 0), ("k", 0)] + [("v", t) for t in range(TT)]:
            A[key] = len(A)
        for step in range(NH + LAG + 1):
            if step % G < 2 and step // G + 1 < NG:
                A["qk"[step % G], step // G + 1] = len(A)
            if step >= LAG + 1 and (step - LAG - 1) % G == G - 1:
                A["inv", (step - LAG - 1) // G] = len(A)
        for key in [("xq", 0), ("xk", 0)] + [("energy", t) for t in range(TT)] + \
                [("wo", t) for t in range(TT)] + [("xm", t) for t in range(TT)]:
            A[key] = len(A)
        NA = len(A)
        T = {}
        for hd in range(NH):
            for n in range(3):
                T["p", hd, n] = len(T)
        for what in ("at", "x1t", "x2t"):
            for n in range(KT):
                T[what, n] = len(T)
        NT = len(T)
        assert NA % 2 == 0 and NT % 2 == 0

        s_win = [sem(f"win{n}") for n in range(5)]
        s_cst = sem("cst")
        s_prep = sem("prep")
        s_wq = sem("wq")
        s_link = sem("link")
        s_plink = sem("plink")
        s_xraw, s_craw, s_xin = sem("xraw"), sem("craw"), sem("xin")
        s_xhi, s_xlo = sem("xhi"), sem("xlo")
        s_chi, s_clo = sem("chi"), sem("clo")
        s_xb = sem("xb")
        s_a, s_t, s_s, s_av = sem("a"), sem("t"), sem("s"), sem("av")
        s_rawqk = sem("rawqk")
        s_nathi, s_nat = sem("nathi"), sem("nat")
        s_stack = [sem(f"stack{n}") for n in range(G)]
        s_v = sem("v")
        s_ttr = sem("ttr")
        s_ntop = sem("ntop")
        s_exp = sem("exp")
        s_inv = sem("inv")
        s_invc = sem("invc")
        s_pt0 = sem("pt0")
        s_pt1 = sem("pt1")
        s_atm = sem("atm")
        s_atl = sem("atl")
        s_en = sem("en")
        s_emax = sem("emax")
        s_px = sem("px")
        s_hi = sem("hi")
        s_lo = sem("lo")
        s_wo, s_xm = sem("wo"), sem("xm")
        s_var = sem("var")
        s_pow0, s_pow = sem("pow0"), sem("pow")
        s_stats = sem("stats")
        s_norm = sem("norm")
        s_x2out, s_x2tout = sem("x2out"), [sem("x2tout0"), sem("x2tout1")]

        def first(i, key):
            return i * NA + A[key] + 1

        def turned(i, key):
            return i * NT + T[key] + 1

        HI3 = {"at": 0, "x1t": 1, "x2t": 2}

        def split_tile(i, what, n):
            return i * 3 * KT + HI3[what] * KT + n + 1

        flat = probs[:].rearrange("p r n -> p (r n)")

        def v_staged():
            return flat[:, 0:KT * H].rearrange("p (k n) -> p k n", k=KT)

        def x_staged():
            return flat[:, KT * H:KT * H + 2 * CT * DX].rearrange("p (w c d) -> p w c d", w=2, c=CT)

        def cross(t):
            return flat[:, t * S:(t + 1) * S]

        def split_before(i, g, w):
            return (2 * NG + 2) * i + 2 * g + w + 1

        s_passed = {eng: sem(f"passed_{eng}") for eng in ("sp", "pool", "dve")}

        block = ctx.enter_context(nc.Block())

        @block.sync
        def _(sp):
            sp.dma_start(x_raw[:], io["xt"][0]).then_inc(s_xraw, 16)
            for w in range(2):
                sp.dma_start(probs_t[:, 2 * w:2 * w + 2, 0:2 * H],
                             io["w_qkv"][w].rearrange("p (a k) n -> p a (k n)", a=2)).then_inc(s_win[w], 16)
            for dst, src in [(qk_bias[:], io["qk_bias"]), (x_bias[:], io["x_bias"]),
                             (v_bias[:], io["v_bias"].unsqueeze(0).to_broadcast([P, H])),
                             (o_bias[:], io["bo"].unsqueeze(0).to_broadcast([P, H]))]:
                sp.dma_start(dst, src).then_inc(s_cst, 16)
            sp.dma_start(v_staged(), io["w_qkv"][2]).then_inc(s_win[2], 16)
            sp.dma_start(x_staged(), io["w_x"]).then_inc(s_win[4], 16)
            sp.dma_start(x[:], io["Wo"].rearrange("(k p) n -> p k n", p=P)).then_inc(s_win[3], 16)
            sp.dma_start(raw[:], io["ctxt"][0]).then_inc(s_craw, 16)
            sp.wait_ge(s_wq, 5)

            def entry(i, last):
                apart(sp, s_x2out, 16 * TT * i + 16, s_passed["sp"])
                sp.dma_start(x[:], io["x"][bass.ds(i * S, S), :].rearrange("(t p) n -> p t n", p=P)
                             ).then_inc(s_xin, 16)
                if not last:
                    apart(sp, s_xlo, KT * i + KT, s_passed["sp"])
                    sp.dma_start(x_raw[:], io["xt"][bass.ds(i + 1, 1)].rearrange("o p k n -> (o p) k n")
                                 ).then_inc(s_xraw, 16)
                for g in range(NG):
                    for hh in range(G):
                        if g:
                            apart(sp, s_s, 3 * (NH * i + G * (g - 1) + hh) + 3, s_passed["sp"])
                        for w in range(2):
                            if hh == 0:
                                apart(sp, s_nat, split_before(i, g, w), s_passed["sp"])
                            for r in range(4):
                                part = (r // 2) if w == 0 else (r % 2)
                                sp.dma_start(stack[w][D * r:D * (r + 1), hh, :].bitcast(F32),
                                             nat[D * hh:D * (hh + 1), 2 * w + part, :].bitcast(F32)
                                             ).then_inc(s_stack[hh], 16)
                if not last:
                    apart(sp, s_nat, split_before(i, NG, 1), s_passed["sp"])
                    sp.dma_start(raw[:], io["ctxt"][bass.ds(i + 1, 1)].rearrange("o p k n -> (o p) k n")
                                 ).then_inc(s_craw, 16)
                for t in range(TT):
                    apart(sp, s_norm, 2 * TT * i + TT + t + 1, s_passed["sp"])
                    sp.dma_start(x2_dram[bass.ds(i * S + t * P, P), :], x[:, t, :]).then_inc(s_x2out, 16)
                for part in range(2):
                    apart(sp, s_hi if part == 0 else s_lo, split_tile(i, "x2t", KT - 1), s_passed["sp"])
                    dst = x2t_dram[part, bass.ds(i, 1)].rearrange("o p k n -> (o p) k n")
                    sp.dma_start(dst.bitcast(F32), xt[part][:].bitcast(F32)).then_inc(s_x2tout[part], 16)

            with sp.Fori(0, B - 1) as i:
                entry(i, False)
            entry(B - 1, True)
            sp.wait_ge(s_x2out, 16 * TT * B + 16)
            for part in range(2):
                sp.wait_ge(s_x2tout[part], 16 * B + 16)

        @block.gpsimd
        def _(pool):
            done = [0]

            def step(ins):
                done[0] += 1
                ins.then_inc(s_plink, 1)
                pool.wait_ge(s_plink, done[0])

            step(pool.memset(half[:], -0.5))
            for g in range(NG):
                for r in range(G):
                    step(pool.memset(q_scale[D * r:D * (r + 1), g:g + 1], SCALE / slope[G * g + r]))
            pool.memset(ident[:], 0.0).then_inc(s_prep, 1)
            pool.wait_ge(s_prep, 1)
            pool.affine_select(out=ident[:], in_=ident[:], compare_op=ALU.not_equal, fill=1.0,
                               base=0, pattern=[[-1, P]], channel_multiplier=1).then_inc(s_prep, 1)
            scratch = v[:, 0, :].bitcast(mybir.dt.int32)
            step(pool.iota(scratch, pattern=[[1, S]], base=-(TT - 1) * P, channel_multiplier=-1))
            step(pool.tensor_copy(dist[:], scratch))
            pool.affine_select(out=dist[:], in_=dist[:], compare_op=ALU.is_ge, fill=MASKED,
                               base=(TT - 1) * P, pattern=[[-1, S]], channel_multiplier=1).then_inc(s_prep, 1)
            pool.wait_ge(s_cst, 16 * 4)
            with pool.Fori(0, B) as i:
                pool.wait_ge(s_xin, 16 * i + 16)
                for t in range(TT):
                    pool.tensor_tensor(x[:, t, :], x[:, t, :], o_bias[:], ALU.add).then_inc(s_xb, 1)
                for c in range(CT):
                    pool.wait_ge(s_chi, CT * i + c + 1)
                    pool.tensor_tensor(ct[1][:, c, :], raw[:, c, :], ct[0][:, c, :].bitcast(F32),
                                       ALU.subtract).then_inc(s_clo, 1)
                for ln in range(2):
                    apart(pool, s_var, 2 * i + ln + 1, s_passed["pool"])
                    pool.tensor_scalar(var[:], mv[:, :, 1], EPS, None, ALU.add).then_inc(s_pow0, 1)
                    pool.wait_ge(s_pow0, 2 * i + ln + 1)
                    pool.tensor_tensor(rstd[:], var[:], half[:].to_broadcast([P, TT]), ALU.pow).then_inc(s_pow, 1)

        @block.scalar
        def _(act):
            act.wait_ge(s_cst, 16 * 4)
            act.wait_ge(s_wq, 6)
            with act.Fori(0, B) as i:
                act.wait_ge(s_xraw, 16 * i + 16)
                for part in range(2):
                    act.wait_ge(s_x2tout[part], 16 * i + 16)
                for k in range(KT):
                    act.activation(xt[0][:, k, :], x_raw[:, k, :], ACT.Copy).then_inc(s_xhi, 1)

                def copy_qk(w, g):
                    act.wait_ge(s_a, first(i, ("qk"[w], g)))
                    if g:
                        act.wait_ge(s_nat, split_before(i, g - 1, w))
                    elif w == 0:
                        act.wait_ge(s_clo, CT * i + CT)
                    act.activation(raw[:, w, :], ab[A["qk"[w], g] % 2][:], ACT.Identity,
                                   bias=qk_bias[:, w, g:g + 1],
                                   scale=q_scale[:, g:g + 1] if w == 0 else 1.0).then_inc(s_rawqk, 1)

                copy_qk(0, 0)
                copy_qk(1, 0)
                for st in range(NH + LAG + 2):
                    if st < NH:
                        hd = st
                        act.wait_ge(s_ntop, NH * i + hd + 1)
                        if hd % G == 0:
                            if hd:
                                act.wait_ge(s_inv, NG * i + hd // G)
                        for t in ORDER:
                            at = probs[:, hd % RING, ROW[t]:ROW[t] + (t + 1) * P]
                            act.activation(at, at, ACT.Exp, bias=ntop[:, hd % 2, t:t + 1], scale=slope[hd],
                                           accum_out=total[:, hd % G, t:t + 1]).then_inc(s_exp, 1)
                    if st % G < 2 and st // G + 1 < NG:
                        copy_qk(st % G, st // G + 1)
                    if st >= LAG + 1 and (st - LAG - 1) % G == G - 1:
                        g = (st - LAG - 1) // G
                        act.wait_ge(s_a, first(i, ("inv", g)))
                        if g:
                            act.wait_ge(s_atl, NG * i + g)
                        act.activation(inv_sb[:], ab[A["inv", g] % 2][:], ACT.Copy).then_inc(s_invc, 1)
                    if LAG <= st < NH + LAG:
                        hd = st - LAG
                        for n, (at, width) in ((1, (COL[1], 4 * P)), (2, (COL[2], 2 * P))):
                            act.wait_ge(s_t, turned(i, ("p", hd, n)))
                            if hd % G == 0 and n == 1 and hd:
                                act.wait_ge(s_av, NG * i + hd // G)
                            act.activation(probs_t[:, hd % G, at:at + width], tb[T["p", hd, n] % 2][:, 0:width],
                                           ACT.Copy).then_inc(s_pt1, 1)
                for w in range(2):
                    act.wait_ge(s_a, first(i, (("xq", "xk")[w], 0)))
                    act.wait_ge(s_nat, split_before(i, NG - 1, w))
                    act.activation(raw[:, w, :], ab[A[("xq", "xk")[w], 0] % 2][:], ACT.Identity,
                                   bias=x_bias[:, w:w + 1]).then_inc(s_rawqk, 1)
                for t in range(TT):
                    act.wait_ge(s_emax, TT * i + t + 1)
                    act.activation(cross(t), ab[A["energy", t] % 2][:], ACT.Exp, bias=ntop[:, 0, t:t + 1],
                                   accum_out=total[:, 0, t:t + 1]).then_inc(s_en, 1)
                for what, dst in (("at", stack), ("x1t", att), ("x2t", xt)):
                    for n in range(KT):
                        act.wait_ge(s_t, turned(i, (what, n)))
                        act.activation(dst[0][:, n, :], tb[T[what, n] % 2][:], ACT.Copy).then_inc(s_hi, 1)

        @block.tensor
        def _(pe):
            def product(out, pairs):
                for n, (lhs, rhs) in enumerate(pairs):
                    mm = pe.matmul(out, lhs, rhs, start=(n == 0), stop=(n == len(pairs) - 1))
                return mm

            pe.wait_ge(s_wq, 2)
            pe.wait_ge(s_prep, 3)
            with pe.Fori(0, B) as i:
                def free_a(key):
                    n = A[key] - 2
                    if n < 0:
                        return
                    old = next(k for k, v_ in A.items() if v_ == n)
                    what, k = old
                    if what in ("q", "k"):
                        pe.wait_ge(s_rawqk, i * (2 * NG + 2) + 2 * k + "qk".index(what) + 1)
                    elif what in ("xq", "xk"):
                        pe.wait_ge(s_rawqk, i * (2 * NG + 2) + 2 * NG + ("xq", "xk").index(what) + 1)
                    else:
                        per = NG if what == "inv" else TT
                        pe.wait_ge({"v": s_v, "inv": s_invc, "energy": s_en, "wo": s_wo, "xm": s_xm}[what],
                                   per * i + k + 1)

                def free_t(key):
                    n = T[key] - 2
                    if n < 0:
                        return
                    old = next(k for k, v_ in T.items() if v_ == n)
                    if old[0] == "p":
                        if old[2] == 0:
                            pe.wait_ge(s_pt0, NH * i + old[1] + 1)
                        else:
                            pe.wait_ge(s_pt1, 2 * (NH * i + old[1]) + old[2])
                    else:
                        pe.wait_ge(s_lo, split_tile(i, old[0], old[1]))

                def project_qk(w, g):
                    key = ("qk"[w], g)
                    free_a(key)
                    mm = product(ab[A[key] % 2][:], [(w_qkv[a][:, w, k, g * P:(g + 1) * P], xt[b][:, k, :])
                                                     for k in range(KT) for a, b in PARTS])
                    mm.then_inc(s_a, 1)

                pe.wait_ge(s_xlo, KT * i + KT)
                project_qk(0, 0)
                project_qk(1, 0)
                pe.wait_ge(s_wq, 3)
                for t in range(TT):
                    free_a(("v", t))
                    product(ab[A["v", t] % 2][:], [(xt[b][:, k, t * P:(t + 1) * P], w_qkv[a][:, 2, k, :])
                                                   for k in range(KT) for a, b in PARTS]).then_inc(s_a, 1)
                for st in range(NH + LAG + 2):
                    if st < NH:
                        hd = st
                        pe.wait_ge(s_stack[hd % G], 16 * 8 * (NG * i + hd // G + 1))
                        for t in ORDER:
                            if hd:
                                pe.wait_ge(s_ttr, TT * (NH * i + hd - 1) + {3: 1, 2: 3, 0: 3, 1: 4}[t])
                            mm = pe.matmul(scores[t], stack[0][:, hd % G, t * P:(t + 1) * P],
                                           stack[1][:, hd % G, 0:(t + 1) * P], start=True, stop=True)
                            if t != 2:
                                mm.then_inc(s_s, 1)
                    if st % G < 2 and st // G + 1 < NG:
                        project_qk(st % G, st // G + 1)
                    if st >= LAG + 1 and (st - LAG - 1) % G == G - 1:
                        g = (st - LAG - 1) // G
                        free_a(("inv", g))
                        pe.wait_ge(s_inv, NG * i + g + 1)
                        for t in range(TT):
                            mm = pe.matmul(ab[A["inv", g] % 2][:, t * P:(t + 1) * P],
                                           inv_wide[:, t, :, :].rearrange("p g d -> p (g d)"), ident[:],
                                           start=True, stop=True)
                        mm.then_inc(s_a, 1)
                        pe.wait_ge(s_pt0, NH * i + G * g + G)
                        pe.wait_ge(s_pt1, 2 * (NH * i + G * g + G))
                        if g:
                            pe.wait_ge(s_atm, NG * i + g)
                        else:
                            pe.wait_ge(s_v, TT * i + TT)
                        for c in range(TT):
                            for hh in range(G):
                                mm = pe.matmul(av[D * hh:D * (hh + 1), c * P:S],
                                               v[:, c, (G * g + hh) * D:(G * g + hh + 1) * D],
                                               probs_t[:, hh, COL[c]:COL[c] + S - c * P],
                                               start=(c == 0), stop=(c == TT - 1), skip_group_check=True)
                        mm.then_inc(s_av, 1)
                    if LAG <= st < NH + LAG:
                        hd = st - LAG
                        pe.wait_ge(s_exp, TT * (NH * i + hd + 1))
                        for n, cols in enumerate(((0,), (1, 3), (2,))):
                            free_t(("p", hd, n))
                            out = tb[T["p", hd, n] % 2]
                            at = 0
                            for c in cols:
                                for t in range(c, TT):
                                    mm = pe.transpose(out[:, at:at + P],
                                                      probs[:, hd % RING, ROW[t] + c * P:ROW[t] + (c + 1) * P],
                                                      ident[:])
                                    at += P
                            mm.then_inc(s_t, 1)
                pe.wait_ge(s_wq, 5)
                for w in range(2):
                    key = (("xq", "xk")[w], 0)
                    free_a(key)
                    if w == 0:
                        pe.wait_ge(s_clo, CT * i + CT)
                    product(ab[A[key] % 2][:], [(w_x[a][:, w, c, :], ct[b][:, c, :])
                                                for c in range(CT) for a, b in PARTS]).then_inc(s_a, 1)
                for t in range(TT):
                    free_a(("energy", t))
                    if t == 0:
                        pe.wait_ge(s_nat, split_before(i, NG, 1))
                    product(ab[A["energy", t] % 2][:], [(nat[:, a, t * P:(t + 1) * P], nat[:, 2 + b, :])
                                                        for a, b in PARTS]).then_inc(s_a, 1)
                for t in range(TT):
                    free_a(("wo", t))
                    if t == 0:
                        pe.wait_ge(s_atl, NG * i + NG)
                    product(ab[A["wo", t] % 2][:], [(att[b][:, k, t * P:(t + 1) * P], w_o[a][:, k, :])
                                                    for k in range(KT) for a, b in PARTS]).then_inc(s_a, 1)

                def turn(what, src):
                    for n in range(KT):
                        free_t((what, n))
                        for t in range(TT):
                            mm = pe.transpose(tb[T[what, n] % 2][:, t * P:(t + 1) * P], src(t, n), ident[:])
                        mm.then_inc(s_t, 1)

                pe.wait_ge(s_px, TT * i + TT)
                turn("at", lambda t, n: cross(t)[:, n * P:(n + 1) * P])
                pe.wait_ge(s_norm, 2 * TT * i + TT)
                turn("x1t", lambda t, n: x[:, t, n * P:(n + 1) * P])
                pe.wait_ge(s_lo, split_tile(i, "x1t", KT - 1))
                for t in range(TT):
                    free_a(("xm", t))
                    product(ab[A["xm", t] % 2][:], [(att[b][:, k, t * P:(t + 1) * P], stack[a][:, k, :])
                                                    for k in range(KT) for a, b in PARTS]).then_inc(s_a, 1)
                pe.wait_ge(s_norm, 2 * TT * i + 2 * TT)
                turn("x2t", lambda t, n: x[:, t, n * P:(n + 1) * P])

        @block.vector
        def _(dve):
            count = [0]
            base = [0]

            def link(ins):
                count[0] += 1
                ins.then_inc(s_link, 1)
                dve.wait_ge(s_link, base[0] + count[0])

            def split_weight(parts, src, s):
                dve.wait_ge(s_win[s], 16)
                link(dve.tensor_copy(parts[0], src))
                dve.tensor_tensor(parts[1], src, parts[0].bitcast(F32), ALU.subtract).then_inc(s_wq, 1)

            for w in range(2):
                for a in range(2):
                    src = probs_t[:, 2 * w + a, 0:1024].rearrange("p (k n) -> p k n", k=2)
                    dst = [p_[:, w, 2 * a:2 * a + 2, :] for p_ in w_qkv]
                    if a == 0:
                        dve.wait_ge(s_win[w], 16)
                    link(dve.tensor_copy(dst[0], src))
                    ins = dve.tensor_tensor(dst[1], src, dst[0].bitcast(F32), ALU.subtract)
                    if a == 1:
                        ins.then_inc(s_wq, 1)
                    else:
                        link(ins)
            split_weight([p_[:, 2] for p_ in w_qkv], v_staged(), 2)
            split_weight([p_[:] for p_ in w_x], x_staged(), 4)
            split_weight([p_[:] for p_ in w_o], x[:], 3)
            dve.wait_ge(s_cst, 16 * 4)
            dve.wait_ge(s_prep, 1)
            dve.tensor_tensor(qk_bias[:, 0, :], qk_bias[:, 0, :], q_scale[:], ALU.mult).then_inc(s_wq, 1)
            link(dve.memset(stats[:], 0.0))
            dve.memset(mv[:, 0, :], 0.0).then_inc(s_x2out, 16)
            dve.memset(mv[:, 1, :], 0.0).then_inc(s_x2tout[0], 16)
            dve.memset(mv[:, 2, :], 0.0).then_inc(s_x2tout[1], 16)
            s0 = count[0]

            with dve.Fori(0, B) as i:
                base[0] = i * ATT_LINKS

                dve.wait_ge(s_x2tout[1], 16 * i + 16)
                for k in range(KT):
                    dve.wait_ge(s_xhi, KT * i + k + 1)
                    dve.tensor_tensor(xt[1][:, k, :], x_raw[:, k, :], xt[0][:, k, :].bitcast(F32),
                                      ALU.subtract).then_inc(s_xlo, 1)
                dve.wait_ge(s_craw, 16 * i + 16)
                for c in range(CT):
                    dve.tensor_copy(ct[0][:, c, :], raw[:, c, :]).then_inc(s_chi, 1)

                def split_qk(w, g):
                    n = (NG + 1) * 2 * i + 2 * g + w
                    dve.wait_ge(s_rawqk, n + 1)
                    if w == 0:
                        for hh in range(G):
                            if g:
                                dve.wait_ge(s_stack[hh], 16 * 8 * (NG * i + g))
                    link(dve.tensor_copy(nat[:, 2 * w, :], raw[:, w, :]))
                    dve.tensor_tensor(nat[:, 2 * w + 1, :], raw[:, w, :], nat[:, 2 * w, :].bitcast(F32),
                                      ALU.subtract).then_inc(s_nat, 1)

                split_qk(0, 0)
                split_qk(1, 0)
                for t in range(TT):
                    dve.wait_ge(s_a, first(i, ("v", t)))
                    dve.tensor_tensor(v[:, t, :], ab[A["v", t] % 2][:], v_bias[:], ALU.add).then_inc(s_v, 1)

                def divide_sums(g):
                    link(dve.reciprocal(inv[:].rearrange("p t g -> p g t"), total[:]))
                    dve.tensor_copy(inv_wide[:], inv[:].unsqueeze(3).to_broadcast([P, TT, G, D])).then_inc(s_inv, 1)

                for st in range(NH + LAG + 2):
                    if st and st % G == 0 and st <= NH:
                        dve.wait_ge(s_exp, TT * (NH * i + st))
                        divide_sums(st // G - 1)
                    if st < NH:
                        hd = st
                        if hd >= RING:
                            dve.wait_ge(s_t, turned(i, ("p", hd - RING, 2)))
                        if hd >= 2:
                            dve.wait_ge(s_exp, TT * (NH * i + hd - 1))
                        for t in ORDER:
                            if t != 0:
                                apart(dve, s_s, 3 * (NH * i + hd) + {3: 1, 2: 2, 1: 3}[t], s_passed["dve"])
                            dve.tensor_tensor_reduce(probs[:, hd % RING, ROW[t]:ROW[t] + (t + 1) * P],
                                                     scores[t], dist[:, S - (t + 1) * P:S], 1.0, -3e38,
                                                     ALU.add, ALU.max, top[:, hd % 2, t:t + 1]).then_inc(s_ttr, 1)
                        dve.wait_ge(s_ttr, TT * (NH * i + hd + 1))
                        dve.tensor_scalar(ntop[:, hd % 2, :], top[:, hd % 2, :], -slope[hd], None,
                                          ALU.mult).then_inc(s_ntop, 1)
                    if st % G < 2 and st // G + 1 < NG:
                        split_qk(st % G, st // G + 1)
                    if LAG <= st < NH + LAG:
                        hd = st - LAG
                        dve.wait_ge(s_t, turned(i, ("p", hd, 0)))
                        if hd % G == 0 and hd:
                            dve.wait_ge(s_av, NG * i + hd // G)
                        dve.tensor_copy(probs_t[:, hd % G, 0:S], tb[T["p", hd, 0] % 2][:]).then_inc(s_pt0, 1)
                    if st >= LAG + 1 and (st - LAG - 1) % G == G - 1:
                        g = (st - LAG - 1) // G
                        dve.wait_ge(s_av, NG * i + g + 1)
                        dve.wait_ge(s_invc, NG * i + g + 1)
                        dve.tensor_tensor(inv_sb[:], av[:], inv_sb[:], ALU.mult).then_inc(s_atm, 1)
                        dve.wait_ge(s_atm, NG * i + g + 1)
                        link(dve.tensor_copy(att[0][:, g, :], inv_sb[:]))
                        dve.tensor_tensor(att[1][:, g, :], inv_sb[:], att[0][:, g, :].bitcast(F32),
                                          ALU.subtract).then_inc(s_atl, 1)
                for w in range(2):
                    if w == 0:
                        for hh in range(G):
                            dve.wait_ge(s_stack[hh], 16 * 8 * (NG * i + NG))
                    dve.wait_ge(s_rawqk, (2 * NG + 2) * i + 2 * NG + w + 1)
                    link(dve.tensor_copy(nat[:, 2 * w, :], raw[:, w, :]))
                    dve.tensor_tensor(nat[:, 2 * w + 1, :], raw[:, w, :], nat[:, 2 * w, :].bitcast(F32),
                                      ALU.subtract).then_inc(s_nat, 1)
                for t in range(TT):
                    dve.wait_ge(s_a, first(i, ("energy", t)))
                    link(dve.tensor_reduce(top[:, 0, t:t + 1], ab[A["energy", t] % 2][:], AX.X, ALU.max))
                    dve.tensor_scalar(ntop[:, 0, t:t + 1], top[:, 0, t:t + 1], -1.0, None,
                                      ALU.mult).then_inc(s_emax, 1)
                dve.wait_ge(s_en, TT * i + TT)
                link(dve.reciprocal(inv[:, :, 0], total[:, 0, :]))
                for t in range(TT):
                    dve.tensor_scalar(cross(t), cross(t), inv[:, t, 0:1], None, ALU.mult).then_inc(s_px, 1)

                def add(what, t, s):
                    dve.wait_ge(s_a, first(i, (what, t)))
                    dve.tensor_tensor(x[:, t, :], x[:, t, :], ab[A[what, t] % 2][:], ALU.add).then_inc(s, 1)
                    dve.wait_ge(s, TT * i + t + 1)
                    dve.bn_stats(stats[:, t, :], x[:, t, :]).then_inc(s_stats, 1)
                    apart(dve, s_stats, 2 * TT * i + (TT if what == "xm" else 0) + t + 1, s_passed["dve"])
                    ins = dve.bn_aggr(mv[:, t, :], stats[:, t, :])
                    ins.then_inc(s_var, 1) if t == TT - 1 else link(ins)

                def norm(n):
                    dve.wait_ge(s_pow, 2 * i + n + 1)
                    for t in range(TT):
                        dve.tensor_scalar(x[:, t, :], x[:, t, :], mv[:, t, 0:1], rstd[:, t:t + 1],
                                          ALU.subtract, ALU.mult).then_inc(s_norm, 1)

                def lows(what, dst):
                    for n in range(KT):
                        dve.wait_ge(s_hi, split_tile(i, what, n))
                        dve.tensor_tensor(dst[1][:, n, :], tb[T[what, n] % 2][:], dst[0][:, n, :].bitcast(F32),
                                          ALU.subtract).then_inc(s_lo, 1)

                dve.wait_ge(s_xb, TT * i + TT)
                for t in range(TT):
                    add("wo", t, s_wo)
                lows("at", stack)
                norm(0)
                lows("x1t", att)
                for t in range(TT):
                    add("xm", t, s_xm)
                norm(1)
                lows("x2t", xt)
                assert count[0] == ATT_LINKS + s0, count[0] - s0


def feed_forward(nc, sems, io, x2_dram, x2t_dram):
    N, C, E, NE = 6, 2, 256, 8
    SH = 2
    UNITS = SH + N
    TOP = N
    ET = E // P
    PIECE = 512
    STAGES = 2
    ctx = ExitStack()
    with ctx:
        def sb(name, shape, dt=F32):
            return ctx.enter_context(nc.sbuf_tensor(name, shape, dt))

        def sem(name):
            return sems.enter_context(nc.semaphore("f_" + name))

        w_up = [sb(f"w_up_{s}", [P, UNITS, KT, E], F32R) for s in ("hi", "lo")]
        w_sw = [sb(f"w_sw_{s}", [P, 1 + N, ET, E], F32R) for s in ("hi", "lo")]
        w_dn = [sb(f"w_dn_{s}", [P, UNITS, ET, H], F32R) for s in ("hi", "lo")]
        w_gate = sb("w_gate", [P, KT * C * 16 + 112], F32R)
        rows = sb("rows", [64, N * P], F32R)
        wt = sb("wt", [64, S], F32R)
        xt = [sb(f"xt_{s}", [P, KT, S], F32R) for s in ("hi", "lo")]
        h = sb("h", [P, ET, S])
        hp = [sb(f"h_{s}", [P, ET, S], F32R) for s in ("hi", "lo")]
        gp = [sb(f"g_{s}", [P, ET, S], F32R) for s in ("hi", "lo")]
        stage = sb("stage", [P, STAGES, PIECE])
        ident = sb("ident", [P, P])
        gate_t = sb("gate_t", [16, S])
        fold = sb("fold", [16, 8])
        b_up = sb("b_up", [P, UNITS, ET])
        b_sw = sb("b_sw", [P, 1 + N, ET])
        b_gate = sb("b_gate", [P, C, NE])
        before = sb("before", [P, NE, NE])
        lg = sb("lg", [P, TT, NE])
        cmp_gt = sb("cmp_gt", [P, TT, NE, NE])
        rank = sb("rank", [P, TT, NE])
        top = sb("top", [P, TT])
        ex = sb("ex", [P, TT, NE])
        gw = sb("gw", [P, TT, 32])
        stats = sb("stats", [P, 2, 6])
        mv = sb("mv", [P, 2, 2])
        rstd = sb("rstd", [P, 2, 2])
        half = sb("half", [P, 1])
        pick = sb("pick", [64, 2])

        acc = [ctx.enter_context(nc.psum_tensor(f"acc{m}", [P, S], F32)) for m in range(KT)]
        ring = [ctx.enter_context(nc.psum_tensor(f"ring{m}", [P, S], F32)) for m in range(4)]

        SLOT = {"gate": 0}
        n_slots = 1
        for u in range(UNITS):
            if u == SH:
                SLOT["wt"] = n_slots
                n_slots += 1
            for what in ("h0", "h1", *(("wb",) if u >= SH else ()), "z0", "z1"):
                SLOT[what, u] = n_slots
                n_slots += 1
        assert n_slots % len(ring) == 0

        def bank(key):
            return ring[SLOT[key] % len(ring)]

        def filled(i, j, key):
            return i * (C * n_slots) + j * n_slots + SLOT[key] + 1

        def units(i, j, u):
            return i * (C * UNITS) + j * UNITS + u

        s_const = sem("s_const")
        s_prep = sem("s_prep")
        s_staged = [sem(f"s_staged{k}") for k in range(STAGES)]
        s_wsplit = sem("s_wsplit")
        s_whi = sem("s_whi")
        s_small = sem("s_small")
        s_slot = sem("s_slot")
        s_tok = sem("s_tok")
        s_dn = sem("s_dn")
        s_acc = sem("s_acc")
        s_gatecopy = sem("s_gatecopy")
        s_exp = sem("s_exp")
        s_wt = sem("s_wt")
        s_h = sem("s_h")
        s_silu = sem("s_silu")
        s_lg = sem("s_lg")
        s_dif = sem("s_dif")
        s_gw = sem("s_gw")
        s_hsplit = sem("s_hsplit")
        s_wb = sem("s_wb")
        s_zread = sem("s_zread")
        s_gsplit = sem("s_gsplit")
        s_xt = sem("s_xt")
        s_accfree = sem("s_accfree")
        s_xload = [sem("s_xload_hi"), sem("s_xload_lo")]
        s_res = [sem("s_res0"), sem("s_res1")]
        s_stats = sem("s_stats")
        s_var = sem("s_var")
        s_pow0 = sem("s_pow0")
        s_pow = sem("s_pow")
        s_y = sem("s_y")
        s_out = [sem("s_out0"), sem("s_out1")]
        s_link = sem("s_link")
        s_pl = sem("s_pl")

        LINKS = 0

        pieces, need = [], {}
        for u in range(UNITS):
            e = u - SH
            up_src = io["Wsu"][:, u * E:(u + 1) * E] if u < SH else io["Wup"][e]
            sw_src = io["Wsa"] if u < SH else io["Wsw"][e]
            dn_src = io["Wsd"][u * E:(u + 1) * E, :] if u < SH else io["Wdn"][e]
            for k in range(0, KT, 2):
                pieces.append(([w[:, u, k:k + 2, :] for w in w_up],
                               up_src[k * P:(k + 2) * P, :].rearrange("(k p) e -> p k e", p=P), 2))
            need["up", u] = len(pieces)
            if u != 1:
                s = max(u - 1, 0)
                pieces.append(([w[:, s, :, :] for w in w_sw], sw_src.rearrange("(k p) e -> p k e", p=P), 2))
            need["sw", u] = len(pieces)
            for k in range(ET):
                pieces.append(([w[:, u, k:k + 1, :] for w in w_dn],
                               dn_src[k * P:(k + 1) * P, :].rearrange("(k p) e -> p k e", p=P), 1))
            need["dn", u] = len(pieces)

        def sw_of(u):
            return max(u - 1, 0)

        s_passed = {eng: sem(f"passed_{eng}") for eng in ("sp", "pool", "dve")}

        block = ctx.enter_context(nc.Block())

        @block.sync
        def _(sp):
            def load_x(i):
                for part in range(2):
                    sp.dma_start(xt[part][:].bitcast(F32),
                                 x2t_dram[part, i].bitcast(F32)).then_inc(s_xload[part], 16)

            load_x(0)
            small = [
                (b_up[:], io["b_up"]), (b_sw[:], io["b_sw"]),
                (b_gate[:], io["bg"].unsqueeze(0).to_broadcast([P, C, NE])),
                (h[:, 0, 0:C * KT * NE], io["w_gate"]),
            ] + [(h[32 + NE * c:32 + NE * (c + 1), 1, :], io["b_out"]) for c in range(4)]
            for dst, src in small:
                sp.dma_start(dst, src).then_inc(s_const, 16)
            for n, (_, src, k) in enumerate(pieces):
                if n >= STAGES:
                    sp.wait_ge(s_wsplit, n - STAGES + 1)
                sp.dma_start(stage[:, n % STAGES, :].rearrange("p (k e) -> p k e", k=k),
                             src).then_inc(s_staged[n % STAGES], 16)
            sp.wait_ge(s_wsplit, len(pieces))

            def chunk(i, last):
                if not last:
                    apart(sp, s_slot, filled(i, C - 1, ("h1", UNITS - 1)), s_passed["sp"])
                    load_x(i + 1)
                for t in range(TT):
                    k = t % STAGES
                    per = TT // STAGES
                    apart(sp, s_out[k], 16 * (i * per + t // STAGES) + 16, s_passed["sp"])
                    sp.dma_start(stage[:, k, :], x2_dram[bass.ds(i * S + t * P, P), :]).then_inc(s_res[k], 16)
                    if t >= 1:
                        store(i, t - 1)
                store(i, TT - 1)

            def store(i, t):
                k = t % STAGES
                apart(sp, s_y, i * TT + t + 1, s_passed["sp"])
                sp.dma_start(io["out"][bass.ds(i * S + t * P, P), :], stage[:, k, :]).then_inc(s_out[k], 16)

            with sp.Fori(0, B - 1) as i:
                chunk(i, False)
            chunk(B - 1, True)
            for k in range(STAGES):
                sp.wait_ge(s_out[k], 16 * (1 + B * TT // STAGES))

        @block.gpsimd
        def _(pool):
            done = [0]

            def step(ins):
                done[0] += 1
                ins.then_inc(s_pl, 1)
                pool.wait_ge(s_pl, done[0])

            def mark(t, op, base, pattern, channel):
                step(pool.affine_select(out=t, in_=t, compare_op=op, fill=1.0, base=base,
                                        pattern=pattern, channel_multiplier=channel))

            for t in (half, ident, fold, before, pick, gate_t):
                step(pool.memset(t[:], -0.5 if t is half else 0.0))
            mark(ident[:], ALU.not_equal, 0, [[-1, P]], 1)
            mark(fold[:], ALU.not_equal, 0, [[-1, NE]], 1)
            mark(fold[:], ALU.not_equal, -NE, [[-1, NE]], 1)
            mark(before[:], ALU.is_ge, 0, [[-1, NE], [1, NE]], 0)
            mark(pick[:, 0:1], ALU.is_ge, -48, [[0, 1]], 1)
            sel = cmp_gt[0:32, :, :, :].rearrange("p a b c -> p (a b c)")[:, 0:P]
            for n in range(N):
                if n:
                    pool.wait_ge(s_small, n)
                step(pool.memset(sel, 0.0))
                mark(sel, ALU.not_equal, -n, [[0, P]], 1)
                mark(sel, ALU.not_equal, -(n + NE), [[0, P]], 1)
                pool.memset(half[:], -0.5).then_inc(s_prep, 1)
            for n, (dst, _, k) in enumerate(pieces):
                pool.wait_ge(s_staged[n % STAGES], 16 * (n // STAGES + 1))
                src = stage[:, n % STAGES, :].rearrange("p (k e) -> p k e", k=k)
                pool.tensor_copy(dst[0], src).then_inc(s_whi, 1)
                pool.wait_ge(s_whi, n + 1)
                pool.tensor_tensor(dst[1], src, dst[0].bitcast(F32), ALU.subtract).then_inc(s_wsplit, 1)
            with pool.Fori(0, B) as i:
                for t in range(TT):
                    k = t % STAGES
                    apart(pool, s_var, i * TT + t + 1, s_passed["pool"])
                    pool.tensor_scalar(rstd[:, k, 0:1], mv[:, k, 1:2], EPS, None, ALU.add).then_inc(s_pow0, 1)
                    pool.wait_ge(s_pow0, i * TT + t + 1)
                    pool.tensor_tensor(rstd[:, k, 1:2], rstd[:, k, 0:1], half[:], ALU.pow).then_inc(s_pow, 1)

        @block.scalar
        def _(act):
            act.wait_ge(s_const, 16 * 8)
            act.wait_ge(s_small, N + 3)
            with act.Fori(0, B) as i:
                for j in range(C):
                    act.wait_ge(s_slot, filled(i, j, "gate"))
                    act.activation(gate_t[:], bank("gate")[0:16, :], ACT.Copy).then_inc(s_gatecopy, 1)
                    for u in range(UNITS):
                        if u == SH:
                            act.wait_ge(s_slot, filled(i, j, "wt"))
                            act.activation(wt[0:32, :], bank("wt")[0:32, :], ACT.Copy)
                            act.activation(wt[32:64, :], bank("wt")[0:32, :], ACT.Copy).then_inc(s_wt, 1)
                        for m in range(ET):
                            act.wait_ge(s_slot, filled(i, j, (f"h{m}", u)))
                            if u:
                                act.wait_ge(s_gsplit, ET * units(i, j, u - 1) + m + 1)
                            act.activation(h[:, m, :], bank((f"h{m}", u))[:], ACT.Identity,
                                           bias=b_up[:, u, m:m + 1]).then_inc(s_h, 1)
                        if u == 0:
                            act.wait_ge(s_dif, i * C + j + 1)
                            act.activation(ex[:], lg[:], ACT.Exp).then_inc(s_exp, 1)
                        for m in range(ET):
                            z = bank((f"z{m}", u))
                            act.wait_ge(s_slot, filled(i, j, (f"z{m}", u)))
                            act.activation(z[:], z[:], ACT.Silu,
                                           bias=b_sw[:, sw_of(u), m:m + 1]).then_inc(s_silu, 1)

        @block.tensor
        def _(pe):
            def product(out, pairs):
                for n, (lhs, rhs) in enumerate(pairs):
                    mm = pe.matmul(out, lhs, rhs, start=(n == 0), stop=(n == len(pairs) - 1))
                return mm

            pe.wait_ge(s_small, N + 3)
            with pe.Fori(0, B) as i:
                for j in range(C):
                    def up(u):
                        pe.wait_ge(s_wsplit, need["up", u])
                        for m in range(ET):
                            out = bank((f"h{m}", u))
                            s = SLOT[f"h{m}", u] - len(ring)
                            if u >= 1:
                                free(s)
                            product(out[:], [(w_up[a][:, u, k, m * P:(m + 1) * P], xt[b][:, k, :])
                                             for k in range(KT) for a, b in PARTS]).then_inc(s_slot, 1)

                    def free(s):
                        key = next(k for k, v in SLOT.items() if v == s)
                        if key == "gate":
                            pe.wait_ge(s_lg, i * C + j + 1)
                        elif key == "wt":
                            pe.wait_ge(s_wt, i * C + j + 1)
                        elif key[0][0] == "h":
                            pe.wait_ge(s_h, ET * units(i, j, key[1]) + int(key[0][1]) + 1)
                        elif key[0] == "wb":
                            pe.wait_ge(s_wb, (i * C + j) * N + key[1] - SH + 1)
                        else:
                            pe.wait_ge(s_zread, ET * units(i, j, key[1]) + int(key[0][1]) + 1)

                    def gate_weights_by_token():
                        pe.wait_ge(s_gatecopy, i * C + j + 1)
                        for t in range(TT):
                            mm = pe.matmul(bank("gate")[:, t * NE:(t + 1) * NE], gate_t[:, t * P:(t + 1) * P],
                                           fold[:], start=True, stop=True)
                        mm.then_inc(s_tok, 1)

                    def broadcast(u):
                        free(SLOT["wb", u] - len(ring))
                        if u == SH:
                            pe.wait_ge(s_wt, i * C + j + 1)
                        pe.matmul(bank(("wb", u))[:], rows[0:32, (u - SH) * P:(u - SH + 1) * P], wt[0:32, :],
                                  start=True, stop=True).then_inc(s_slot, 1)

                    def sw(u):
                        pe.wait_ge(s_wsplit, need["sw", u])
                        for m in range(ET):
                            s = SLOT[f"z{m}", u] - len(ring)
                            if s >= 0:
                                free(s)
                            pe.wait_ge(s_hsplit, ET * units(i, j, u) + (m + 1 if m == 0 else ET))
                            pairs = []
                            for k in range(ET):
                                for a, b in PARTS:
                                    pairs.append((w_sw[a][:, sw_of(u), k, m * P:(m + 1) * P], hp[b][:, k, :]))
                            for n, (lhs, rhs) in enumerate(pairs):
                                if m == 0 and n == len(PARTS):
                                    pe.wait_ge(s_hsplit, ET * units(i, j, u) + ET)
                                mm = pe.matmul(bank((f"z{m}", u))[:], lhs, rhs, start=(n == 0),
                                               stop=(n == len(pairs) - 1))
                            mm.then_inc(s_slot, 1)

                    def dn(u):
                        pe.wait_ge(s_wsplit, need["dn", u])
                        for k in range(ET):
                            pe.wait_ge(s_gsplit, ET * units(i, j, u) + k + 1)
                            for m in range(KT):
                                if j == 0 and u == 0 and k == 0:
                                    pe.wait_ge(s_accfree, i * KT + m + 1)
                                for a, b in PARTS:
                                    if j == 0:
                                        lhs, rhs = w_dn[a][:, u, k, m * P:(m + 1) * P], gp[b][:, k, :]
                                    else:
                                        lhs, rhs = gp[b][:, k, m * P:(m + 1) * P], w_dn[a][:, u, k, :]
                                    mm = pe.matmul(acc[m][:], lhs, rhs,
                                                   start=(u == 0 and k == 0 and (a, b) == (0, 0)), stop=False)
                        mm.then_inc(s_dn, 1)

                    def out_bias():
                        for m in range(KT):
                            if j == 0:
                                lhs, rhs = rows[32:64, m * P:(m + 1) * P], wt[32:64, :]
                            else:
                                lhs, rhs = wt[32:64, m * P:(m + 1) * P], rows[32:64, 0:H]
                            pe.matmul(acc[m][:], lhs, rhs, start=False, stop=True).then_inc(s_acc, 1)

                    if j == 0:
                        for part in range(2):
                            pe.wait_ge(s_xload[part], 16 * i + 16)
                    gate_pairs = []
                    for k in range(KT):
                        if j == 1:
                            pe.wait_ge(s_xt, i * KT + k + 1)
                        at = (j * KT + k) * 16
                        for b in range(2):
                            mm = pe.matmul(bank("gate")[:], w_gate[:, at:at + P], xt[b][:, k, :],
                                           start=(k == 0 and b == 0), stop=(k == KT - 1 and b == 1))
                    mm.then_inc(s_slot, 1)
                    for u in range(UNITS):
                        up(u)
                        if u == 0:
                            gate_weights_by_token()
                        if u == SH:
                            pass
                        if u:
                            dn(u - 1)
                        if u >= SH:
                            broadcast(u)
                        sw(u)
                        if u == SH - 1:
                            free(SLOT["wt"] - len(ring))
                            pe.wait_ge(s_gw, i * C + j + 1)
                            for t in range(TT):
                                mm = pe.transpose(bank("wt")[0:32, t * P:(t + 1) * P], gw[:, t, :], ident[:])
                            mm.then_inc(s_slot, 1)
                    dn(UNITS - 1)
                    out_bias()

        @block.vector
        def _(dve):
            count = [0]
            base = [0]

            def link(ins):
                count[0] += 1
                ins.then_inc(s_link, 1)
                dve.wait_ge(s_link, base[0] + count[0])

            link(dve.memset(w_gate[:].bitcast(mybir.dt.uint32), 0))
            dve.wait_ge(s_const, 16 * 8)
            wg = w_gate[:, 0:C * KT * 16].rearrange("p (a n) -> p a n", n=16)
            raw = h[:, 0, 0:C * KT * NE].rearrange("p (a n) -> p a n", n=NE)
            link(dve.tensor_copy(wg[:, :, 0:NE], raw))
            link(dve.tensor_tensor(wg[:, :, NE:16], raw, wg[:, :, 0:NE].bitcast(F32), ALU.subtract))
            for n in range(N):
                dve.wait_ge(s_prep, n + 1)
                dve.tensor_copy(rows[0:32, n * P:(n + 1) * P],
                                cmp_gt[0:32, :, :, :].rearrange("p a b c -> p (a b c)")[:, 0:P]).then_inc(s_small, 1)
            bd = rows[32:64, 0:H]
            raw = h[32:64, 1, :]
            low = h[32:64, 0, :]
            link(dve.tensor_copy(bd, raw))
            link(dve.tensor_tensor(low, raw, bd.bitcast(F32), ALU.subtract))
            link(dve.tensor_scalar(pick[32:64, 1:2], pick[32:64, 0:1], -1.0, 1.0, ALU.mult, ALU.add))
            link(dve.tensor_scalar(low, low, pick[32:64, 1:2], None, ALU.mult))
            link(dve.scalar_tensor_tensor(out=bd, in0=bd.bitcast(F32), scalar=pick[32:64, 0:1], in1=low,
                                          op0=ALU.mult, op1=ALU.add))
            dve.memset(gw[:], 0.0).then_inc(s_small, 1)
            dve.memset(stats[:], 0.0).then_inc(s_small, 1)
            dve.memset(mv[:], 0.0).then_inc(s_small, 1)
            link(dve.memset(top[:], 0.0))
            dve.memset(rank[:], 0.0).then_inc(s_accfree, KT)
            dve.memset(rstd[:, 0, :], 0.0).then_inc(s_out[0], 16)
            dve.memset(rstd[:, 1, :], 0.0).then_inc(s_out[1], 16)
            s0 = count[0]

            with dve.Fori(0, B) as i:
                base[0] = i * FFN_LINKS
                for j in range(C):
                    def split_h(u):
                        for m in range(ET):
                            dve.wait_ge(s_h, ET * units(i, j, u) + m + 1)
                            link(dve.tensor_copy(hp[0][:, m, :], h[:, m, :]))
                            dve.tensor_tensor(hp[1][:, m, :], h[:, m, :], hp[0][:, m, :].bitcast(F32),
                                              ALU.subtract).then_inc(s_hsplit, 1)

                    def gated(u):
                        if u >= SH:
                            dve.wait_ge(s_slot, filled(i, j, ("wb", u)))
                            for m in range(ET):
                                ins = dve.tensor_tensor(h[:, m, :], h[:, m, :], bank(("wb", u))[:], ALU.mult)
                                if m == ET - 1:
                                    ins.then_inc(s_wb, 1)
                            dve.wait_ge(s_wb, (i * C + j) * N + u - SH + 1)
                        for m in range(ET):
                            dve.wait_ge(s_silu, ET * units(i, j, u) + m + 1)
                            dve.tensor_tensor(h[:, m, :], h[:, m, :], bank((f"z{m}", u))[:],
                                              ALU.mult).then_inc(s_zread, 1)
                            dve.wait_ge(s_zread, ET * units(i, j, u) + m + 1)
                            if u and m == 0:
                                dve.wait_ge(s_dn, units(i, j, u))
                            link(dve.tensor_copy(gp[0][:, m, :], h[:, m, :]))
                            dve.tensor_tensor(gp[1][:, m, :], h[:, m, :], gp[0][:, m, :].bitcast(F32),
                                              ALU.subtract).then_inc(s_gsplit, 1)

                    def logits():
                        dve.wait_ge(s_tok, i * C + j + 1)
                        dve.tensor_tensor(lg[:], bank("gate")[:, 0:TT * NE].rearrange("p (t n) -> p t n", t=TT),
                                          b_gate[:, j, :].unsqueeze(1).to_broadcast([P, TT, NE]),
                                          ALU.add).then_inc(s_lg, 1)
                        dve.wait_ge(s_lg, i * C + j + 1)
                        own = lg[:].unsqueeze(3).to_broadcast([P, TT, NE, NE])
                        other = lg[:].unsqueeze(2).to_broadcast([P, TT, NE, NE])
                        link(dve.tensor_tensor(cmp_gt[:], other, own, ALU.is_equal))
                        link(dve.tensor_tensor(cmp_gt[:], cmp_gt[:],
                                               before[:].unsqueeze(1).to_broadcast([P, TT, NE, NE]), ALU.mult))
                        link(dve.tensor_reduce(rank[:], cmp_gt[:], AX.X, ALU.add))
                        link(dve.tensor_tensor(cmp_gt[:], other, own, ALU.is_gt))
                        link(dve.tensor_reduce(ex[:], cmp_gt[:], AX.X, ALU.add))
                        link(dve.tensor_tensor(rank[:], rank[:], ex[:], ALU.add))
                        link(dve.tensor_reduce(top[:], lg[:], AX.X, ALU.max))
                        dve.tensor_tensor(lg[:], lg[:], top[:].unsqueeze(2).to_broadcast([P, TT, NE]),
                                          ALU.subtract).then_inc(s_dif, 1)

                    def gate_softmax():
                        dve.wait_ge(s_exp, i * C + j + 1)
                        link(dve.scalar_tensor_tensor(out=ex[:], in0=rank[:], scalar=TOP - 0.5, in1=ex[:],
                                                      op0=ALU.is_lt, op1=ALU.mult))
                        link(dve.tensor_reduce(top[:], ex[:], AX.X, ALU.add))
                        link(dve.reciprocal(top[:], top[:]))
                        link(dve.tensor_tensor(ex[:], ex[:], top[:].unsqueeze(2).to_broadcast([P, TT, NE]),
                                               ALU.mult))
                        link(dve.memset(ex[:, :, N:N + 1], 1.0))
                        link(dve.memset(ex[:, :, N + 1:NE], 0.0))
                        link(dve.tensor_copy(gw[:, :, 0:NE].bitcast(F32R), ex[:]))
                        link(dve.tensor_tensor(gw[:, :, NE:2 * NE], ex[:], gw[:, :, 0:NE], ALU.subtract))
                        dve.tensor_copy(gw[:, :, 16:32], gw[:, :, 0:16]).then_inc(s_gw, 1)

                    for u in range(UNITS):
                        split_h(u)
                        if u == 0:
                            logits()
                        gated(u)
                        if u == 0:
                            gate_softmax()

                    if j == 0:
                        for m in range(KT):
                            dve.wait_ge(s_acc, (i * C + j) * KT + m + 1)
                            tmp = h[:, m % ET, :]
                            link(dve.tensor_tensor(tmp, xt[0][:, m, :].bitcast(F32), acc[m][:], ALU.add))
                            link(dve.tensor_tensor(tmp, tmp, xt[1][:, m, :].bitcast(F32), ALU.add))
                            link(dve.tensor_copy(xt[0][:, m, :], tmp))
                            dve.tensor_tensor(xt[1][:, m, :], tmp, xt[0][:, m, :].bitcast(F32),
                                              ALU.subtract).then_inc(s_xt, 1)
                        dve.wait_ge(s_xt, i * KT + KT)
                    else:
                        def add(t):
                            k = t % STAGES
                            dve.wait_ge(s_acc, (i * C + j) * KT + t + 1)
                            dve.wait_ge(s_res[k], 16 * (i * (TT // STAGES) + t // STAGES + 1))
                            dve.tensor_tensor(stage[:, k, :], stage[:, k, :], acc[t][:],
                                              ALU.add).then_inc(s_accfree, 1)
                            dve.wait_ge(s_accfree, KT + i * TT + t + 1)
                            dve.bn_stats(stats[:, k, :], stage[:, k, :]).then_inc(s_stats, 1)
                            apart(dve, s_stats, i * TT + t + 1, s_passed["dve"])
                            dve.bn_aggr(mv[:, k, :], stats[:, k, :]).then_inc(s_var, 1)

                        def norm(t):
                            k = t % STAGES
                            dve.wait_ge(s_var, i * TT + t + 1)
                            dve.wait_ge(s_pow, i * TT + t + 1)
                            dve.tensor_scalar(stage[:, k, :], stage[:, k, :], mv[:, k, 0:1], rstd[:, k, 1:2],
                                              ALU.subtract, ALU.mult).then_inc(s_y, 1)

                        for t in range(TT):
                            add(t)
                            if t:
                                norm(t - 1)
                        norm(TT - 1)
                assert count[0] == FFN_LINKS + s0, count[0] - s0


def lay_out_attention(x, ctx, Wqkv, bqkv, Wo, bo, Wq, bq, Wk, bk):
    import numpy as np
    tiles = lambda a: np.ascontiguousarray(a.reshape(a.shape[0], a.shape[1], -1, P).transpose(0, 3, 2, 1))
    return dict(
        x=x.reshape(-1, H), xt=tiles(x), ctxt=tiles(ctx),
        w_qkv=np.ascontiguousarray(Wqkv.reshape(KT, P, 3, H).transpose(2, 1, 0, 3)),
        qk_bias=np.ascontiguousarray(bqkv[:2 * H].reshape(2, KT, P).transpose(2, 0, 1)),
        v_bias=bqkv[2 * H:], Wo=Wo, bo=bo,
        w_x=np.ascontiguousarray(np.stack([Wq, Wk]).reshape(2, 128, -1, P).transpose(3, 0, 2, 1)),
        x_bias=np.ascontiguousarray(np.stack([bq, bk], 1)))


def lay_out_ffn(Wg, bg, Wup, bup, Wsw, bsw, Wdn, bdn, Wsu, bsu, Wsa, bsa, Wsd, bsd):
    import numpy as np
    cols = lambda *v: np.ascontiguousarray(
        np.concatenate([a.reshape(-1, 2, P) for a in v]).transpose(2, 0, 1))
    return dict(
        b_up=cols(bsu, bup), b_sw=cols(bsa, bsw), bg=bg,
        w_gate=np.ascontiguousarray(Wg.reshape(2, 4, P, 8).transpose(2, 0, 1, 3).reshape(P, 64)),
        b_out=np.concatenate([bdn, bsd[None], np.zeros_like(bsd)[None]]),
        Wup=Wup, Wsw=Wsw, Wdn=Wdn, Wsu=Wsu, Wsa=Wsa, Wsd=Wsd)


def decoder_layer(nc, io, out):
    x2 = nc.dram_tensor("x2_rows", [B * S, H], F32).ap()
    x2t = nc.dram_tensor("x2_transposed", [2, B, P, KT, S], F32R).ap()
    with ExitStack() as sems:
        attention(nc, sems, io, x2, x2t)
        feed_forward(nc, sems, io | {"out": out}, x2, x2t)


def kernel(x, ctx_1024, L0_attn_Wqkv, L0_attn_bqkv, L0_attn_Wo, L0_attn_bo, L0_xattn_Wq, L0_xattn_bq,
           L0_xattn_Wk, L0_xattn_bk, L0_ffn_Wg, L0_ffn_bg, L0_ffn_Wup, L0_ffn_bup, L0_ffn_Wsw, L0_ffn_bsw,
           L0_ffn_Wdn, L0_ffn_bdn, L0_ffn_Wsu, L0_ffn_bsu, L0_ffn_Wsa, L0_ffn_bsa, L0_ffn_Wsd, L0_ffn_bsd):
    import numpy as np
    import concourse.bacc as bacc
    from concourse.bass_utils import run_bass_kernel_spmd

    attn = [np.asarray(a) for a in (x, ctx_1024, L0_attn_Wqkv, L0_attn_bqkv, L0_attn_Wo, L0_attn_bo,
                                    L0_xattn_Wq, L0_xattn_bq, L0_xattn_Wk, L0_xattn_bk)]
    ffn = [np.asarray(a) for a in (L0_ffn_Wg, L0_ffn_bg, L0_ffn_Wup, L0_ffn_bup, L0_ffn_Wsw, L0_ffn_bsw,
                                   L0_ffn_Wdn, L0_ffn_bdn, L0_ffn_Wsu, L0_ffn_bsu, L0_ffn_Wsa, L0_ffn_bsa,
                                   L0_ffn_Wsd, L0_ffn_bsd)]
    laid = lay_out_attention(*attn) | lay_out_ffn(*ffn)
    nc = bacc.Bacc("TRN2", target_bir_lowering=False, num_devices=1)
    arrays, io = {}, {}
    for name, a in laid.items():
        arrays["in_" + name] = np.ascontiguousarray(a)
        io[name] = nc.dram_tensor("in_" + name, a.shape, mybir.dt.from_np(a.dtype), kind="ExternalInput").ap()
    out = nc.dram_tensor("out_rows", [B * S, H], F32, kind="ExternalOutput").ap()
    decoder_layer(nc, io, out)
    result = run_bass_kernel_spmd(nc, [arrays], core_ids=[0])
    return result.results[0]["out_rows"].reshape(B, S, H)
```

```python
import math
from contextlib import ExitStack

import concourse.bass as bass
from concourse import mybir

F32 = mybir.dt.float32
F32R = mybir.dt.float32r
ALU = mybir.AluOpType
ACT = mybir.ActivationFunctionType
AX = mybir.AxisListType

P = 128
B, S, H = 4, 512, 512
KT = H // P
TT = S // P
EPS = 1e-5
PARTS = [(0, 0), (0, 1), (1, 0)]
ATT_LINKS = 11
FFN_LINKS = 106


def apart(eng, sem, value, passed):
    eng.wait_ge(sem, value)
    eng.sem_inc(passed, 1)


def attention(nc, sems, io, x2_dram, x2t_dram):
    NH, D = 16, 32
    G = P // D
    NG = NH // G
    DX, CT = 128, 2
    LAG = 2
    SCALE = 1.0 / math.sqrt(D)
    MASKED = -1e30
    slope = [1.0 / 2 ** (n / 2) for n in range(NH)]
    SEEN = TT * (TT + 1) // 2 * P
    ROW = [t * (t + 1) // 2 * P for t in range(TT)]
    ORDER = [3, 2, 0, 1]
    COL = {0: 0, 1: TT * P, 3: TT * P + 3 * P, 2: TT * P + 4 * P}
    RING = 4
    NP = 3
    with ExitStack() as ctx:
        def sb(name, shape, dt=F32):
            return ctx.enter_context(nc.sbuf_tensor("a_" + name, shape, dt))

        def sem(name):
            return sems.enter_context(nc.semaphore("a_" + name))

        def bank(name):
            return ctx.enter_context(nc.psum_tensor("a_" + name, [P, S], F32))

        HL = ("hi", "lo")
        w_qkv = [sb(f"w_qkv_{s}", [P, 3, KT, H], F32R) for s in HL]
        w_o = [sb(f"w_o_{s}", [P, KT, H], F32R) for s in HL]
        w_x = [sb(f"w_x_{s}", [P, 2, CT, DX], F32R) for s in HL]
        dist = sb("dist", [P, S])
        o_bias = sb("o_bias", [P, H])
        xt = [sb(f"xt_{s}", [P, KT, S], F32R) for s in HL]
        raw = sb("raw", [P, 2, S])
        inv_sb = sb("inv_sb", [P, S])
        inv_wide = inv_sb[:].rearrange("p (t g d) -> p t g d", t=TT, g=G)
        nat = sb("nat", [P, 4, S], F32R)
        stack = [[sb(f"stack{n}_{s}", [P, G, S], F32R) for s in ("q", "k")] for n in range(2)]
        ct = [stack[0][0][:, CT * a:CT * (a + 1), :] for a in range(2)]
        crosst = stack[1]
        v = sb("v", [P, TT, H])
        probs = sb("probs", [P, RING, SEEN])
        probs_t = sb("probs_t", [P, G, SEEN])
        att = [sb(f"att_{s}", [P, KT, S], F32R) for s in HL]
        x = sb("x", [P, TT, H])
        ident = sb("ident", [P, P])
        q_scale = sb("q_scale", [P, NG])
        qk_bias = sb("qk_bias", [P, 2, NG])
        v_bias = sb("v_bias", [P, KT])
        x_bias = sb("x_bias", [P, 2])
        top = sb("top", [P, 2, TT])
        ntop = sb("ntop", [P, 2, TT])
        total = sb("total", [P, G, TT])
        inv = sb("inv", [P, TT, G])
        stats = sb("stats", [P, TT, 6])
        mv = sb("mv", [P, TT, 2])
        var = sb("var", [P, TT])
        rstd = sb("rstd", [P, TT])
        half = sb("half", [P, 1])
        parts_dram = nc.dram_tensor("qk_parts", [2, P, 4, S], F32).ap()

        ab = [bank(f"proj{n}") for n in range(2)]
        s3, s20, s1 = bank("s3"), bank("s20"), bank("s1")
        tb = [bank(f"turn{n}") for n in range(2)]
        av = bank("av")
        scores = {3: s3[:, 0:4 * P], 2: s20[:, 0:3 * P], 0: s20[:, 3 * P:4 * P], 1: s1[:, 0:2 * P]}

        STEPS = range(NH + LAG + 2)
        QK_AT = {0: [(0, 2, 0), (0, 2, 1), (0, 2, 2), (0, 2, 3)], 1: [(1, 2, 0), (1, 2, 1), (1, 2, 2), (1, 2, 3)],
                 2: [(0, 3, 0), (0, 3, 1)], 3: [(0, 3, 2), (0, 3, 3)],
                 4: [(1, 3, 0), (1, 3, 1), (1, 3, 2), (1, 3, 3)]}
        COPY_QK_AT = {st: (w, g) for st, tiles in QK_AT.items() for w, g, k in tiles if k == KT - 1}
        SPLIT_QK_AT = {1: (0, 2), 2: (1, 2), 4: (0, 3), 5: (1, 3), 15: (0, NG), 16: (1, NG)}
        SPLIT_CONTEXT_AT, XQK_AT = 12, {14: 0, 15: 1}
        SUMS_AT = {G * (g + 1): g for g in range(NG)}
        SPREAD_AT = {G * (g + 1) + 1: g for g in range(NG)}
        USE_AT = {G * g + G - 1 + LAG + 1: g for g in range(NG)}
        ATT_AT = {st + 1: g for st, g in USE_AT.items()}

        def slots(last):
            keys = []
            for st in STEPS:
                if st in COPY_QK_AT:
                    w, g = COPY_QK_AT[st]
                    keys.append(("qk"[w], g))
                if st in XQK_AT:
                    keys.append(("x", XQK_AT[st]))
                if st in SPREAD_AT:
                    keys.append(("inv", SPREAD_AT[st]))
            keys += [("energy", t) for t in range(TT)] + [("wo", t) for t in range(TT)]
            keys += [] if last else [("next", w, g) for g in range(2) for w in "qk"]
            keys += [("xm", t) for t in range(TT)]
            keys += [] if last else [("next", "v", t) for t in range(TT)]
            return keys

        AHEAD = [("next", w, g) for g in range(2) for w in "qk"] + [("next", "v", t) for t in range(TT)]
        NA = len(slots(False))
        NEXT_QK = [(w, g) for g in range(2) for w in range(2)]
        T = {}
        for hd in range(NH):
            for n in range(3):
                T["p", hd, n] = len(T)
        for what in ("at", "x1t", "x2t"):
            for n in range(KT):
                T[what, n] = len(T)
        NT = len(T)
        assert (NA - slots(False).index(("energy", 0))) % 2 == 0 and NT % 2 == 0 and len(AHEAD) % 2 == 0

        HEADS = slots(True).index(("energy", 0))

        class Slots:

            def __init__(self, i, last=False):
                self.i = i
                self.keys = AHEAD if i is None else slots(last)
                self.heads = 0 if i is None else HEADS

            def bank(self, key):
                n = self.keys.index(key) - self.heads
                return ab[0] if n < 0 else ab[(n + 1) % 2]

            def filled(self, key):
                n = self.keys.index(key) + 1
                return n if self.i is None else len(AHEAD) + self.i * NA + n

            def before(self, key):
                n = self.keys.index(key)
                if n < self.heads:
                    return self.keys[n - 1] if n else ("v", TT - 1)
                if self.heads and n == self.heads:
                    return ("p", NH - 1)
                n = max(n - 2, self.heads - 1)
                return self.keys[n] if n >= 0 else None

        s_win = [sem(f"win{n}") for n in range(5)]
        s_cst = sem("cst")
        s_prep = sem("prep")
        s_wq = sem("wq")
        s_vb, s_vwo = sem("vb"), sem("vwo")
        s_link, s_plink = sem("link"), sem("plink")
        s_xraw, s_craw, s_xin = sem("xraw"), sem("craw"), sem("xin")
        s_xhi, s_xlo = sem("xhi"), sem("xlo")
        s_chi, s_clo = sem("chi"), sem("clo")
        s_xb = sem("xb")
        s_a, s_t, s_s, s_av = sem("a"), sem("t"), sem("s"), sem("av")
        s_rawqk = sem("rawqk")
        s_nathi, s_nat = sem("nathi"), sem("nat")
        s_natout = [sem("natout_q"), sem("natout_k")]
        s_stack = [sem(f"stack{n}") for n in range(2)]
        s_v = sem("v")
        s_ttr = sem("ttr")
        s_ntop = sem("ntop")
        s_exp = sem("exp")
        s_rcp = sem("rcp")
        s_inv = sem("inv")
        s_invc = sem("invc")
        s_pt0 = sem("pt0")
        s_pt1 = sem("pt1")
        s_atm, s_ath, s_atl = sem("atm"), sem("ath"), sem("atl")
        s_emax = sem("emax")
        s_en = sem("en")
        s_px = sem("px")
        s_hi = sem("hi")
        s_lo = sem("lo")
        s_wo, s_xm = sem("wo"), sem("xm")
        s_stats = sem("stats")
        s_var = sem("var")
        s_pow0, s_pow = sem("pow0"), sem("pow")
        s_norm = sem("norm")
        s_x2out, s_x2tout = sem("x2out"), [sem("x2tout0"), sem("x2tout1")]
        s_passed = {eng: sem(f"passed_{eng}") for eng in ("sp", "pool", "dve")}

        LOADS = 16 * 2 * NP

        def turn_bank(key):
            if key[0] == "p":
                return (tb[0][:], tb[1][:], ab[1][:])[key[2]]
            return (tb[0], tb[1], s3, s20)[key[1]][:]

        def turned(i, key):
            return i * NT + T[key] + 1

        def split_tile(i, what, n):
            return i * 3 * KT + {"at": 0, "x1t": 1, "x2t": 2}[what] * KT + n + 1

        def qk_tile(e, g, w):
            return (2 * NG + 2) * e + 2 * g + w + 1

        def in_stack(e, g):
            return LOADS * (2 * e + g // 2 + 1)

        flat = probs[:].rearrange("p r n -> p (r n)")
        flat_t = probs_t[:].rearrange("p g n -> p (g n)")
        x_staged = flat_t[:, 0:KT * S].rearrange("p (k n) -> p k n", k=KT)
        wq_staged = flat_t[:, KT * S:2 * KT * S].rearrange("p (k n) -> p k n", k=KT)
        wv_staged = flat[:, 0:KT * H].rearrange("p (k n) -> p k n", k=KT)
        wx_staged = flat[:, KT * H:KT * H + 2 * CT * DX].rearrange("p (w c d) -> p w c d", w=2, c=CT)

        def cross(t):
            return flat[:, t * S:(t + 1) * S]

        block = ctx.enter_context(nc.Block())

        @block.sync
        def _(sp):
            sp.dma_start(wq_staged, io["w_qkv"][0]).then_inc(s_win[0], 16)
            sp.dma_start(x_staged, io["xt"][0]).then_inc(s_xraw, 16)
            for dst, src in [(qk_bias[:], io["qk_bias"]), (x_bias[:], io["x_bias"]), (v_bias[:], io["v_bias"]),
                             (o_bias[:], io["bo"].unsqueeze(0).to_broadcast([P, H]))]:
                sp.dma_start(dst, src).then_inc(s_cst, 16)
            sp.dma_start(v[:], io["w_qkv"][1]).then_inc(s_win[1], 16)
            sp.dma_start(wv_staged, io["w_qkv"][2]).then_inc(s_win[2], 16)
            sp.dma_start(wx_staged, io["w_x"]).then_inc(s_win[3], 16)
            sp.dma_start(x[:], io["Wo"].rearrange("(k p) n -> p k n", p=P)).then_inc(s_win[4], 16)

            def store_parts(e, g, w, first=False):
                apart(sp, s_nat, qk_tile(e, g, w), s_passed["sp"])
                if not first:
                    apart(sp, s_stack[g % 2], in_stack(e, g) - LOADS, s_passed["sp"])
                sp.dma_start(parts_dram[g % 2, :, 2 * w:2 * w + 2, :],
                             nat[:, 2 * w:2 * w + 2, :].bitcast(F32)).then_inc(s_natout[w], 16)

            def load_parts(e, g, w):
                apart(sp, s_natout[w], 16 * (NG * e + g + 1), s_passed["sp"])
                for r in range(NP):
                    part = ((0, 0, 1), (0, 1, 0))[w][r]
                    sp.dma_start(stack[g % 2][w][D * r:D * (r + 1), :, :].bitcast(F32),
                                 parts_dram[g % 2, :, 2 * w + part, :].rearrange("(h d) n -> d h n", d=D)
                                 ).then_inc(s_stack[g % 2], 16)

            for g in range(2):
                for w in range(2):
                    store_parts(0, g, w, first=True)
                for w in range(2):
                    load_parts(0, g, w)
            sp.wait_ge(s_wq, 7)

            def entry(i, last):
                apart(sp, s_x2out, 16 * TT * i + 16, s_passed["sp"])
                sp.dma_start(x[:], io["x"][bass.ds(i * S, S), :].rearrange("(t p) n -> p t n", p=P)
                             ).then_inc(s_xin, 16)
                for g in range(2, NG):
                    for w in range(2):
                        store_parts(i, g, w)
                    apart(sp, s_s, 3 * (NH * i + G * (g - 1)), s_passed["sp"])
                    for w in range(2):
                        load_parts(i, g, w)
                sp.dma_start(raw[:], io["ctxt"][bass.ds(i, 1)].rearrange("o p k n -> (o p) k n")
                             ).then_inc(s_craw, 16)
                if not last:
                    apart(sp, s_av, NG * i + NG, s_passed["sp"])
                    sp.dma_start(x_staged, io["xt"][bass.ds(i + 1, 1)].rearrange("o p k n -> (o p) k n")
                                 ).then_inc(s_xraw, 16)
                    slots = Slots(i)
                    for w in range(2):
                        store_parts(i + 1, 0, w)
                    apart(sp, s_a, slots.filled(("x", 1)), s_passed["sp"])
                    for w in range(2):
                        load_parts(i + 1, 0, w)
                    for w in range(2):
                        store_parts(i + 1, 1, w)
                    apart(sp, s_a, slots.filled(("xm", TT - 1)), s_passed["sp"])
                    for w in range(2):
                        load_parts(i + 1, 1, w)
                for t in range(TT):
                    apart(sp, s_norm, 2 * TT * i + TT + t + 1, s_passed["sp"])
                    sp.dma_start(x2_dram[bass.ds(i * S + t * P, P), :], x[:, t, :]).then_inc(s_x2out, 16)
                for part in range(2):
                    apart(sp, (s_hi, s_lo)[part], split_tile(i, "x2t", KT - 1) + part, s_passed["sp"])
                    dst = x2t_dram[part, bass.ds(i, 1)].rearrange("o p k n -> (o p) k n")
                    sp.dma_start(dst.bitcast(F32), att[part][:].bitcast(F32)).then_inc(s_x2tout[part], 16)

            with sp.Fori(0, B - 1) as i:
                entry(i, False)
            entry(B - 1, True)
            sp.wait_ge(s_x2out, 16 * TT * B + 16)
            for part in range(2):
                sp.wait_ge(s_x2tout[part], 16 * B + 16)

        @block.gpsimd
        def _(pool):
            done = [0]

            def step(ins):
                done[0] += 1
                ins.then_inc(s_plink, 1)
                pool.wait_ge(s_plink, done[0])

            for g in range(NG):
                for r in range(G):
                    ins = pool.memset(q_scale[D * r:D * (r + 1), g:g + 1], SCALE / slope[G * g + r])
                    if (g, r) == (NG - 1, G - 1):
                        ins.then_inc(s_prep, 1)
                        pool.wait_ge(s_prep, 1)
                    else:
                        step(ins)
            step(pool.memset(half[:], -0.5))
            step(pool.memset(ident[:], 0.0))
            pool.affine_select(out=ident[:], in_=ident[:], compare_op=ALU.not_equal, fill=1.0,
                               base=0, pattern=[[-1, P]], channel_multiplier=1).then_inc(s_prep, 1)
            pool.wait_ge(s_prep, 2)
            scratch = inv_sb[:].bitcast(mybir.dt.int32)
            step(pool.iota(scratch, pattern=[[1, S]], base=-(TT - 1) * P, channel_multiplier=-1))
            step(pool.tensor_copy(dist[:], scratch))
            pool.affine_select(out=dist[:], in_=dist[:], compare_op=ALU.is_ge, fill=MASKED,
                               base=(TT - 1) * P, pattern=[[-1, S]], channel_multiplier=1).then_inc(s_prep, 1)
            pool.wait_ge(s_prep, 3)

            def low_qk(e, g, w):
                pool.wait_ge(s_nathi, qk_tile(e, g, w))
                pool.tensor_tensor(nat[:, 2 * w + 1, :], raw[:, w, :], nat[:, 2 * w, :].bitcast(F32),
                                   ALU.subtract).then_inc(s_nat, 1)

            def rstds(n):
                apart(pool, s_var, n + 1, s_passed["pool"])
                pool.tensor_scalar(var[:], mv[:, :, 1], EPS, None, ALU.add).then_inc(s_pow0, 1)
                pool.wait_ge(s_pow0, n + 1)
                pool.tensor_tensor(rstd[:], var[:], half[:].to_broadcast([P, TT]), ALU.pow).then_inc(s_pow, 1)

            def entry(i, last):
                for st in STEPS:
                    if st in SPLIT_QK_AT:
                        w, g = SPLIT_QK_AT[st]
                        low_qk(i, g, w)
                    if st == G + 2:
                        pool.wait_ge(s_xin, 16 * i + 16)
                        for t in range(TT):
                            pool.tensor_tensor(x[:, t, :], x[:, t, :], o_bias[:], ALU.add).then_inc(s_xb, 1)
                    if st == SPLIT_CONTEXT_AT:
                        for c in range(CT):
                            pool.wait_ge(s_chi, CT * i + c + 1)
                            pool.tensor_tensor(ct[1][:, c, :], raw[:, c, :], ct[0][:, c, :].bitcast(F32),
                                               ALU.subtract).then_inc(s_clo, 1)
                    if st in ATT_AT:
                        g = ATT_AT[st]
                        if g == 0:
                            pool.wait_ge(s_x2tout[1], 16 * i + 16)
                        pool.wait_ge(s_ath, NG * i + g + 1)
                        pool.tensor_tensor(att[1][:, g, :], inv_sb[:], att[0][:, g, :].bitcast(F32),
                                           ALU.subtract).then_inc(s_atl, 1)
                rstds(2 * i)
                if not last:
                    for g in range(2):
                        for w in range(2):
                            low_qk(i + 1, g, w)
                rstds(2 * i + 1)

            for g in range(2):
                for w in range(2):
                    low_qk(0, g, w)
            pool.wait_ge(s_wq, 7)
            with pool.Fori(0, B - 1) as i:
                entry(i, False)
            entry(B - 1, True)

        @block.scalar
        def _(act):
            def split_x(e):
                act.wait_ge(s_xraw, 16 * e + 16)
                for k in range(KT):
                    act.activation(xt[0][:, k, :], x_staged[:, k, :], ACT.Copy).then_inc(s_xhi, 1)

            def copy_qk(e, g, w, slots, key):
                act.wait_ge(s_a, slots.filled(key))
                if g == NG:
                    act.wait_ge(s_clo, CT * e + CT)
                    bias, scale = x_bias[:, w:w + 1], 1.0
                else:
                    if not (slots.i is None and g == 0):
                        act.wait_ge(s_nat, qk_tile(e, g, w) - 2)
                    bias, scale = qk_bias[:, w, g:g + 1], q_scale[:, g:g + 1] if w == 0 else 1.0
                act.activation(raw[:, w, :], slots.bank(key)[:], ACT.Identity, bias=bias,
                               scale=scale).then_inc(s_rawqk, 1)

            def copy_v(slots, tiles):
                for t in tiles:
                    act.wait_ge(s_a, slots.filled(("next", "v", t)))
                    act.activation(v[:, t, :], slots.bank(("next", "v", t))[:], ACT.Copy).then_inc(s_v, 1)

            def entry(i, last):
                slots = Slots(i, last)

                def high(what, dst):
                    for n in range(KT):
                        act.wait_ge(s_t, turned(i, (what, n)))
                        act.activation(dst[0][:, n, :], turn_bank((what, n)), ACT.Copy).then_inc(s_hi, 1)

                def exponentials(hd):
                    act.wait_ge(s_ntop, NH * i + hd + 1)
                    if hd % G == 0 and hd:
                        act.wait_ge(s_rcp, NG * i + hd // G)
                    for t in ORDER:
                        at = probs[:, hd % RING, ROW[t]:ROW[t] + (t + 1) * P]
                        act.activation(at, at, ACT.Exp, bias=ntop[:, hd % 2, t:t + 1], scale=slope[hd],
                                       accum_out=total[:, hd % G, t:t + 1]).then_inc(s_exp, 1)

                def copy_turned(hd, n):
                    at, width = ((COL[1], 4 * P), (COL[2], 2 * P))[n - 1]
                    act.wait_ge(s_t, turned(i, ("p", hd, n)))
                    if hd == 0 and n == 1:
                        act.wait_ge(s_xlo, KT * i + KT)
                    elif hd % G == 0 and n == 1:
                        act.wait_ge(s_av, NG * i + hd // G)
                    act.activation(probs_t[:, hd % G, at:at + width], turn_bank(("p", hd, n))[:, 0:width],
                                   ACT.Copy).then_inc(s_pt1, 1)

                for st in STEPS:
                    turns = LAG <= st < NH + LAG
                    if turns and st not in USE_AT:
                        copy_turned(st - LAG, 1)
                        copy_turned(st - LAG, 2)
                    if st < NH:
                        exponentials(st)
                    if turns and st in USE_AT:
                        copy_turned(st - LAG, 1)
                        copy_turned(st - LAG, 2)
                    if st in SUMS_AT:
                        act.wait_ge(s_rcp, NG * i + SUMS_AT[st] + 1)
                        if SUMS_AT[st]:
                            act.wait_ge(s_atl, NG * i + SUMS_AT[st])
                        act.activation(inv_wide, inv[:].unsqueeze(3).to_broadcast([P, TT, G, D]),
                                       ACT.Copy).then_inc(s_inv, 1)
                    if st in COPY_QK_AT:
                        w, g = COPY_QK_AT[st]
                        copy_qk(i, g, w, slots, ("qk"[w], g))
                    if st in XQK_AT:
                        copy_qk(i, NG, XQK_AT[st], slots, ("x", XQK_AT[st]))
                    if st in SPREAD_AT:
                        g = SPREAD_AT[st]
                        act.wait_ge(s_a, slots.filled(("inv", g)))
                        act.activation(inv_sb[:], slots.bank(("inv", g))[:], ACT.Copy).then_inc(s_invc, 1)
                for t in range(TT):
                    act.wait_ge(s_emax, TT * i + t + 1)
                    act.activation(cross(t), slots.bank(("energy", t))[:], ACT.Exp, bias=ntop[:, 0, t:t + 1],
                                   accum_out=total[:, 0, t:t + 1]).then_inc(s_en, 1)
                if not last:
                    split_x(i + 1)
                    copy_qk(i + 1, 0, 0, slots, ("next", "q", 0))
                high("at", crosst)
                if not last:
                    for w, g in NEXT_QK[1:]:
                        copy_qk(i + 1, g, w, slots, ("next", "qk"[w], g))
                high("x1t", att)
                if not last:
                    copy_v(slots, range(TT - 1))
                high("x2t", att)
                if not last:
                    copy_v(slots, range(TT - 1, TT))

            split_x(0)
            act.wait_ge(s_wq, 1)
            slots = Slots(None)
            for g in range(2):
                for w in range(2):
                    copy_qk(0, g, w, slots, ("next", "qk"[w], g))
            copy_v(slots, range(TT))
            with act.Fori(0, B - 1) as i:
                entry(i, False)
            entry(B - 1, True)

        @block.tensor
        def _(pe):
            def product(out, pairs):
                for n, (lhs, rhs) in enumerate(pairs):
                    mm = pe.matmul(out, lhs, rhs, start=(n == 0), stop=(n == len(pairs) - 1))
                return mm

            def free_a(slots, key):
                old = slots.before(key)
                if old is None:
                    return
                e = 0 if slots.i is None else slots.i
                ahead = 0 if slots.i is None else 1
                what, n = old[0], old[-1]
                if what == "next" and old[1] == "v":
                    pe.wait_ge(s_v, TT * (e + ahead) + n + 1)
                elif what == "next":
                    pe.wait_ge(s_rawqk, qk_tile(e + ahead, n, "qk".index(old[1])))
                elif what in ("q", "k"):
                    pe.wait_ge(s_rawqk, qk_tile(e, n, "qk".index(what)))
                elif what == "x":
                    pe.wait_ge(s_rawqk, qk_tile(e, NG, n))
                elif what == "p":
                    pe.wait_ge(s_pt1, 2 * (NH * e + NH))
                else:
                    per = NG if what == "inv" else TT
                    pe.wait_ge({"v": s_v, "inv": s_invc, "energy": s_en, "wo": s_wo, "xm": s_xm}[what],
                               per * e + n + 1)

            def project_qk_tile(slots, key, w, g, k):
                if k == 0:
                    free_a(slots, key)
                for n, (a, b) in enumerate(PARTS):
                    mm = pe.matmul(slots.bank(key)[:], w_qkv[a][:, w, k, g * P:(g + 1) * P], xt[b][:, k, :],
                                   start=(k == 0 and n == 0), stop=(k == KT - 1 and n == len(PARTS) - 1))
                if k == KT - 1:
                    mm.then_inc(s_a, 1)

            def project_next_qk(e, slots, tiles):
                for w, g in tiles:
                    if slots.i is None and g == 0:
                        pe.wait_ge(s_wq, 2 + w)
                    for k in range(KT):
                        if (w, g) == (0, 0):
                            pe.wait_ge(s_xlo, KT * e + k + 1)
                        project_qk_tile(slots, ("next", "qk"[w], g), w, g, k)

            def project_v(slots, tiles):
                for t in tiles:
                    key = ("next", "v", t)
                    free_a(slots, key)
                    product(slots.bank(key)[:], [(xt[b][:, k, t * P:(t + 1) * P], w_qkv[a][:, 2, k, :])
                                                 for k in range(KT) for a, b in PARTS]).then_inc(s_a, 1)

            def entry(i, last):
                slots = Slots(i, last)

                def free_t(key):
                    what, n = key[0], key[-1]
                    heads = key[1] if what == "p" else NH
                    if what == "p" and heads == 0:
                        if n == 2:
                            pe.wait_ge(s_v, TT * i + TT - 1)
                        return
                    if what in ("x1t", "x2t"):
                        pe.wait_ge(s_lo, split_tile(i, what, n) - KT + 1)
                    elif what == "at" and n > 1:
                        pe.wait_ge(s_ttr, TT * (NH * i + NH))
                    elif n == 0:
                        pe.wait_ge(s_pt0, NH * i + heads)
                    else:
                        pe.wait_ge(s_pt1, 2 * (NH * i + heads - 1) + n)

                def turn_probs(hd, n):
                    if n == 0:
                        pe.wait_ge(s_exp, TT * (NH * i + hd + 1))
                    free_t(("p", hd, n))
                    out = turn_bank(("p", hd, n))
                    at = 0
                    for c in ((0,), (1, 3), (2,))[n]:
                        for t in range(c, TT):
                            mm = pe.transpose(out[:, at:at + P],
                                              probs[:, hd % RING, ROW[t] + c * P:ROW[t] + (c + 1) * P], ident[:])
                            at += P
                    mm.then_inc(s_t, 1)

                def turn(what, src):
                    for n in range(KT):
                        free_t((what, n))
                        for t in range(TT):
                            mm = pe.transpose(turn_bank((what, n))[:, t * P:(t + 1) * P], src(t, n), ident[:])
                        mm.then_inc(s_t, 1)

                for st in STEPS:
                    if st < NH:
                        hd, g = st, st // G
                        if hd % G == 0:
                            pe.wait_ge(s_stack[g % 2], in_stack(i, g))
                        if hd == 0:
                            pe.wait_ge(s_lo, 3 * KT * i + 1)
                        for t in ORDER:
                            if hd:
                                pe.wait_ge(s_ttr, TT * (NH * i + hd - 1) + {3: 1, 2: 3, 0: 3, 1: 4}[t])
                            mm = pe.matmul(scores[t], stack[g % 2][0][0:NP * D, hd % G, t * P:(t + 1) * P],
                                           stack[g % 2][1][0:NP * D, hd % G, 0:(t + 1) * P], start=True, stop=True)
                            if t != 2:
                                mm.then_inc(s_s, 1)
                    if st in USE_AT:
                        g = USE_AT[st]
                        pe.wait_ge(s_pt0, NH * i + G * g + G)
                        pe.wait_ge(s_pt1, 2 * (NH * i + G * g + G))
                        if g:
                            pe.wait_ge(s_atm, NG * i + g)
                        else:
                            pe.wait_ge(s_v, TT * i + TT)
                        for c in range(TT):
                            for hh in range(G):
                                mm = pe.matmul(av[D * hh:D * (hh + 1), c * P:S],
                                               v[:, c, (G * g + hh) * D:(G * g + hh + 1) * D],
                                               probs_t[:, hh, COL[c]:COL[c] + S - c * P],
                                               start=(c == 0), stop=(c == TT - 1), skip_group_check=True)
                        mm.then_inc(s_av, 1)
                    if LAG <= st < NH + LAG:
                        turn_probs(st - LAG, 0)
                        turn_probs(st - LAG, 1)
                    if LAG <= st < NH + LAG:
                        turn_probs(st - LAG, 2)
                    for w, g, k in QK_AT.get(st, ()):
                        project_qk_tile(slots, ("qk"[w], g), w, g, k)
                    if st in XQK_AT:
                        w = XQK_AT[st]
                        free_a(slots, ("x", w))
                        if w == 0:
                            pe.wait_ge(s_clo, CT * i + CT)
                        product(slots.bank(("x", w))[:], [(w_x[a][:, w, c, :], ct[b][:, c, :])
                                                          for c in range(CT) for a, b in PARTS]).then_inc(s_a, 1)
                    if st in SPREAD_AT:
                        g = SPREAD_AT[st]
                        free_a(slots, ("inv", g))
                        pe.wait_ge(s_inv, NG * i + g + 1)
                        for t in range(TT):
                            mm = pe.matmul(slots.bank(("inv", g))[:, t * P:(t + 1) * P],
                                           inv_sb[:, t * P:(t + 1) * P], ident[:],
                                           start=True, stop=True)
                        mm.then_inc(s_a, 1)
                for t in range(TT):
                    free_a(slots, ("energy", t))
                    if t == 0:
                        pe.wait_ge(s_nat, qk_tile(i, NG, 1))
                    product(slots.bank(("energy", t))[:], [(nat[:, a, t * P:(t + 1) * P], nat[:, 2 + b, :])
                                                           for a, b in PARTS]).then_inc(s_a, 1)
                for t in range(TT):
                    free_a(slots, ("wo", t))
                    if t == 0:
                        pe.wait_ge(s_atl, NG * i + NG)
                    product(slots.bank(("wo", t))[:], [(att[b][:, k, t * P:(t + 1) * P], w_o[a][:, k, :])
                                                       for k in range(KT) for a, b in PARTS]).then_inc(s_a, 1)
                if not last:
                    project_next_qk(i + 1, slots, NEXT_QK[:1])
                pe.wait_ge(s_px, TT * i + TT)
                turn("at", lambda t, n: cross(t)[:, n * P:(n + 1) * P])
                if not last:
                    project_next_qk(i + 1, slots, NEXT_QK[1:])
                pe.wait_ge(s_norm, 2 * TT * i + TT)
                turn("x1t", lambda t, n: x[:, t, n * P:(n + 1) * P])
                for t in range(TT):
                    free_a(slots, ("xm", t))
                    for k in range(KT):
                        if t == 0:
                            pe.wait_ge(s_lo, split_tile(i, "x1t", k) + 1)
                        for n, (a, b) in enumerate(PARTS):
                            mm = pe.matmul(slots.bank(("xm", t))[:], att[b][:, k, t * P:(t + 1) * P],
                                           crosst[a][:, k, :], start=(k == 0 and n == 0),
                                           stop=(k == KT - 1 and n == len(PARTS) - 1))
                    mm.then_inc(s_a, 1)
                if not last:
                    project_v(slots, range(TT - 1))
                pe.wait_ge(s_norm, 2 * TT * i + 2 * TT)
                turn("x2t", lambda t, n: x[:, t, n * P:(n + 1) * P])
                if not last:
                    project_v(slots, range(TT - 1, TT))

            slots = Slots(None)
            project_next_qk(0, slots, NEXT_QK)
            pe.wait_ge(s_wq, 4)
            project_v(slots, range(TT))
            pe.wait_ge(s_prep, 3)
            pe.wait_ge(s_vb, 1)
            pe.wait_ge(s_win[4], 16)
            for k in range(KT):
                mm = pe.matmul(av[:], inv_sb[:, k * P:(k + 1) * P], x[:, k, :], start=(k == 0), stop=(k == KT - 1))
            mm.then_inc(s_vwo, 1)
            pe.wait_ge(s_wq, 7)
            with pe.Fori(0, B - 1) as i:
                entry(i, False)
            entry(B - 1, True)

        @block.vector
        def _(dve):
            count = [0]
            base = [0]

            def link(ins):
                count[0] += 1
                ins.then_inc(s_link, 1)
                dve.wait_ge(s_link, base[0] + count[0])

            def split_weight(parts, src, s):
                dve.wait_ge(s_win[s], 16)
                link(dve.tensor_copy(parts[0], src))
                dve.tensor_tensor(parts[1], src, parts[0].bitcast(F32), ALU.subtract).then_inc(s_wq, 1)

            def split_x(e):
                for k in range(KT):
                    dve.wait_ge(s_xhi, KT * e + k + 1)
                    dve.tensor_tensor(xt[1][:, k, :], x_staged[:, k, :], xt[0][:, k, :].bitcast(F32),
                                      ALU.subtract).then_inc(s_xlo, 1)

            def high_qk(e, g, w):
                dve.wait_ge(s_rawqk, qk_tile(e, g, w))
                if g:
                    dve.wait_ge(s_natout[w], 16 * (NG * e + g))
                dve.tensor_copy(nat[:, 2 * w, :], raw[:, w, :]).then_inc(s_nathi, 1)

            def entry(i, last):
                slots = Slots(i, last)
                base[0] = i * ATT_LINKS
                count[0] = s0

                for st in STEPS:
                    if st < NH:
                        hd = st
                        if hd >= RING:
                            dve.wait_ge(s_t, turned(i, ("p", hd - RING, 2)))
                        if hd >= 2:
                            dve.wait_ge(s_exp, TT * (NH * i + hd - 1))
                        for t in ORDER:
                            if t != 0:
                                apart(dve, s_s, 3 * (NH * i + hd) + {3: 1, 2: 2, 1: 3}[t], s_passed["dve"])
                            dve.tensor_tensor_reduce(probs[:, hd % RING, ROW[t]:ROW[t] + (t + 1) * P],
                                                     scores[t], dist[:, S - (t + 1) * P:S], 1.0, -3e38,
                                                     ALU.add, ALU.max, top[:, hd % 2, t:t + 1]).then_inc(s_ttr, 1)
                        dve.wait_ge(s_ttr, TT * (NH * i + hd + 1))
                        dve.tensor_scalar(ntop[:, hd % 2, :], top[:, hd % 2, :], -slope[hd], None,
                                          ALU.mult).then_inc(s_ntop, 1)
                    if st in SUMS_AT:
                        g = SUMS_AT[st]
                        dve.wait_ge(s_exp, TT * (NH * i + G * g + G))
                        if g:
                            dve.wait_ge(s_inv, NG * i + g)
                        dve.reciprocal(inv[:].rearrange("p t g -> p g t"), total[:]).then_inc(s_rcp, 1)
                    if LAG <= st < NH + LAG:
                        hd = st - LAG
                        dve.wait_ge(s_t, turned(i, ("p", hd, 0)))
                        if hd % G == 0 and hd:
                            dve.wait_ge(s_av, NG * i + hd // G)
                        dve.tensor_copy(probs_t[:, hd % G, 0:S], turn_bank(("p", hd, 0))).then_inc(s_pt0, 1)
                    if st in ATT_AT:
                        g = ATT_AT[st]
                        if g == 0:
                            dve.wait_ge(s_x2tout[0], 16 * i + 16)
                        dve.wait_ge(s_av, NG * i + g + 1)
                        dve.wait_ge(s_invc, NG * i + g + 1)
                        dve.tensor_tensor(inv_sb[:], av[:], inv_sb[:], ALU.mult).then_inc(s_atm, 1)
                        dve.wait_ge(s_atm, NG * i + g + 1)
                        dve.tensor_copy(att[0][:, g, :], inv_sb[:]).then_inc(s_ath, 1)
                    if st == SPLIT_CONTEXT_AT:
                        dve.wait_ge(s_s, 3 * (NH * i + 3 * G))
                        dve.wait_ge(s_craw, 16 * i + 16)
                        for c in range(CT):
                            dve.tensor_copy(ct[0][:, c, :], raw[:, c, :]).then_inc(s_chi, 1)
                    if st in SPLIT_QK_AT:
                        w, g = SPLIT_QK_AT[st]
                        high_qk(i, g, w)

                for t in range(TT):
                    dve.wait_ge(s_a, slots.filled(("energy", t)))
                    link(dve.tensor_reduce(top[:, 0, t:t + 1], slots.bank(("energy", t))[:], AX.X, ALU.max))
                    dve.tensor_scalar(ntop[:, 0, t:t + 1], top[:, 0, t:t + 1], -1.0, None,
                                      ALU.mult).then_inc(s_emax, 1)
                dve.wait_ge(s_en, TT * i + TT)
                dve.wait_ge(s_inv, NG * i + NG)
                link(dve.reciprocal(inv[:, :, 0], total[:, 0, :]))
                for t in range(TT):
                    dve.tensor_scalar(cross(t), cross(t), inv[:, t, 0:1], None, ALU.mult).then_inc(s_px, 1)

                def add(what, t, s):
                    dve.wait_ge(s_a, slots.filled((what, t)))
                    dve.tensor_tensor(x[:, t, :], x[:, t, :], slots.bank((what, t))[:], ALU.add).then_inc(s, 1)
                    dve.wait_ge(s, TT * i + t + 1)
                    dve.bn_stats(stats[:, t, :], x[:, t, :]).then_inc(s_stats, 1)
                    apart(dve, s_stats, 2 * TT * i + (TT if what == "xm" else 0) + t + 1, s_passed["dve"])
                    ins = dve.bn_aggr(mv[:, t, :], stats[:, t, :])
                    ins.then_inc(s_var, 1) if t == TT - 1 else link(ins)

                def norm(n):
                    dve.wait_ge(s_pow, 2 * i + n + 1)
                    for t in range(TT):
                        dve.tensor_scalar(x[:, t, :], x[:, t, :], mv[:, t, 0:1], rstd[:, t:t + 1],
                                          ALU.subtract, ALU.mult).then_inc(s_norm, 1)

                def lows(what, dst):
                    for n in range(KT):
                        dve.wait_ge(s_hi, split_tile(i, what, n))
                        dve.tensor_tensor(dst[1][:, n, :], turn_bank((what, n)), dst[0][:, n, :].bitcast(F32),
                                          ALU.subtract).then_inc(s_lo, 1)

                dve.wait_ge(s_xb, TT * i + TT)
                for t in range(TT):
                    add("wo", t, s_wo)
                    if t == 1 and not last:
                        split_x(i + 1)
                norm(0)
                if not last:
                    high_qk(i + 1, 0, 0)
                lows("at", crosst)
                if not last:
                    for w, g in NEXT_QK[1:]:
                        high_qk(i + 1, g, w)
                lows("x1t", att)
                for t in range(TT):
                    add("xm", t, s_xm)
                norm(1)
                lows("x2t", att)
                if not last:
                    assert count[0] == ATT_LINKS + s0, count[0] - s0

            dve.wait_ge(s_prep, 1)
            dve.wait_ge(s_cst, 16 * 4)
            dve.tensor_tensor(qk_bias[:, 0, :], qk_bias[:, 0, :], q_scale[:], ALU.mult).then_inc(s_wq, 1)
            dve.wait_ge(s_prep, 3)
            dve.tensor_copy(inv_sb[:].rearrange("p (k n) -> p k n", k=KT),
                            v_bias[:].unsqueeze(2).to_broadcast([P, KT, P])).then_inc(s_vb, 1)
            split_weight([part[:, 0] for part in w_qkv], wq_staged, 0)
            split_x(0)
            split_weight([part[:, 1] for part in w_qkv], v[:], 1)
            for w in range(2):
                high_qk(0, 0, w)
            split_weight([part[:, 2] for part in w_qkv], wv_staged, 2)
            for w in range(2):
                high_qk(0, 1, w)
            split_weight([part[:] for part in w_x], wx_staged, 3)
            split_weight([part[:] for part in w_o], x[:], 4)
            dve.wait_ge(s_vwo, 1)
            dve.tensor_tensor(o_bias[:], o_bias[:], av[:], ALU.add).then_inc(s_wq, 1)
            link(dve.memset(stats[:], 0.0))
            dve.memset(mv[:, 0, :], 0.0).then_inc(s_x2out, 16)
            dve.memset(mv[:, 1, :], 0.0).then_inc(s_x2tout[0], 16)
            dve.memset(mv[:, 2, :], 0.0).then_inc(s_x2tout[1], 16)
            dve.memset(mv[:, 3, :], 0.0).then_inc(s_lo, 1)
            s0 = count[0]
            with dve.Fori(0, B - 1) as i:
                entry(i, False)
            entry(B - 1, True)


def feed_forward(nc, sems, io, x2_dram, x2t_dram):
    N, C, E, NE = 6, 2, 256, 8
    SH = 2
    UNITS = SH + N
    TOP = N
    ET = E // P
    PIECE = 512
    STAGES = 2
    ctx = ExitStack()
    with ctx:
        def sb(name, shape, dt=F32):
            return ctx.enter_context(nc.sbuf_tensor(name, shape, dt))

        def sem(name):
            return sems.enter_context(nc.semaphore("f_" + name))

        w_up = [sb(f"w_up_{s}", [P, UNITS, KT, E], F32R) for s in ("hi", "lo")]
        w_sw = [sb(f"w_sw_{s}", [P, 1 + N, ET, E], F32R) for s in ("hi", "lo")]
        w_dn = [sb(f"w_dn_{s}", [P, UNITS, ET, H], F32R) for s in ("hi", "lo")]
        w_gate = sb("w_gate", [P, KT * C * 16 + 112], F32R)
        rows = sb("rows", [64, N * P], F32R)
        wt = sb("wt", [64, S], F32R)
        xt = [sb(f"xt_{s}", [P, KT, S], F32R) for s in ("hi", "lo")]
        h = sb("h", [P, ET, S])
        hp = [sb(f"h_{s}", [P, ET, S], F32R) for s in ("hi", "lo")]
        gp = [sb(f"g_{s}", [P, ET, S], F32R) for s in ("hi", "lo")]
        stage = sb("stage", [P, STAGES, PIECE])
        ident = sb("ident", [P, P])
        gate_t = sb("gate_t", [16, S])
        fold = sb("fold", [16, 8])
        b_up = sb("b_up", [P, UNITS, ET])
        b_sw = sb("b_sw", [P, 1 + N, ET])
        b_gate = sb("b_gate", [P, C, NE])
        before = sb("before", [P, NE, NE])
        lg = sb("lg", [P, TT, NE])
        cmp_gt = sb("cmp_gt", [P, TT, NE, NE])
        rank = sb("rank", [P, TT, NE])
        top = sb("top", [P, TT])
        ex = sb("ex", [P, TT, NE])
        gw = sb("gw", [P, TT, 32])
        stats = sb("stats", [P, 2, 6])
        mv = sb("mv", [P, 2, 2])
        rstd = sb("rstd", [P, 2, 2])
        half = sb("half", [P, 1])
        pick = sb("pick", [64, 2])

        acc = [ctx.enter_context(nc.psum_tensor(f"acc{m}", [P, S], F32)) for m in range(KT)]
        ring = [ctx.enter_context(nc.psum_tensor(f"ring{m}", [P, S], F32)) for m in range(4)]

        SLOT = {"gate": 0}
        n_slots = 1
        for u in range(UNITS):
            if u == SH:
                SLOT["wt"] = n_slots
                n_slots += 1
            for what in ("h0", "h1", *(("wb",) if u >= SH else ()), "z0", "z1"):
                SLOT[what, u] = n_slots
                n_slots += 1
        assert n_slots % len(ring) == 0

        def bank(key):
            return ring[SLOT[key] % len(ring)]

        def filled(i, j, key):
            return i * (C * n_slots) + j * n_slots + SLOT[key] + 1

        def units(i, j, u):
            return i * (C * UNITS) + j * UNITS + u

        s_const = sem("s_const")
        s_prep = sem("s_prep")
        s_staged = [sem(f"s_staged{k}") for k in range(STAGES)]
        s_wsplit = sem("s_wsplit")
        s_whi = sem("s_whi")
        s_small = sem("s_small")
        s_slot = sem("s_slot")
        s_tok = sem("s_tok")
        s_dn = sem("s_dn")
        s_acc = sem("s_acc")
        s_gatecopy = sem("s_gatecopy")
        s_exp = sem("s_exp")
        s_wt = sem("s_wt")
        s_h = sem("s_h")
        s_silu = sem("s_silu")
        s_lg = sem("s_lg")
        s_dif = sem("s_dif")
        s_gw = sem("s_gw")
        s_hsplit = sem("s_hsplit")
        s_wb = sem("s_wb")
        s_zread = sem("s_zread")
        s_gsplit = sem("s_gsplit")
        s_xt = sem("s_xt")
        s_accfree = sem("s_accfree")
        s_xload = [sem("s_xload_hi"), sem("s_xload_lo")]
        s_res = [sem("s_res0"), sem("s_res1")]
        s_stats = sem("s_stats")
        s_var = sem("s_var")
        s_pow0 = sem("s_pow0")
        s_pow = sem("s_pow")
        s_y = sem("s_y")
        s_out = [sem("s_out0"), sem("s_out1")]
        s_link = sem("s_link")
        s_pl = sem("s_pl")

        LINKS = 0

        pieces, need = [], {}
        for u in range(UNITS):
            e = u - SH
            up_src = io["Wsu"][:, u * E:(u + 1) * E] if u < SH else io["Wup"][e]
            sw_src = io["Wsa"] if u < SH else io["Wsw"][e]
            dn_src = io["Wsd"][u * E:(u + 1) * E, :] if u < SH else io["Wdn"][e]
            for k in range(0, KT, 2):
                pieces.append(([w[:, u, k:k + 2, :] for w in w_up],
                               up_src[k * P:(k + 2) * P, :].rearrange("(k p) e -> p k e", p=P), 2))
            need["up", u] = len(pieces)
            if u != 1:
                s = max(u - 1, 0)
                pieces.append(([w[:, s, :, :] for w in w_sw], sw_src.rearrange("(k p) e -> p k e", p=P), 2))
            need["sw", u] = len(pieces)
            for k in range(ET):
                pieces.append(([w[:, u, k:k + 1, :] for w in w_dn],
                               dn_src[k * P:(k + 1) * P, :].rearrange("(k p) e -> p k e", p=P), 1))
            need["dn", u] = len(pieces)

        def sw_of(u):
            return max(u - 1, 0)

        s_passed = {eng: sem(f"passed_{eng}") for eng in ("sp", "pool", "dve")}

        block = ctx.enter_context(nc.Block())

        @block.sync
        def _(sp):
            def load_x(i):
                for part in range(2):
                    sp.dma_start(xt[part][:].bitcast(F32),
                                 x2t_dram[part, i].bitcast(F32)).then_inc(s_xload[part], 16)

            load_x(0)
            small = [
                (b_up[:], io["b_up"]), (b_sw[:], io["b_sw"]),
                (b_gate[:], io["bg"].unsqueeze(0).to_broadcast([P, C, NE])),
                (h[:, 0, 0:C * KT * NE], io["w_gate"]),
            ] + [(h[32 + NE * c:32 + NE * (c + 1), 1, :], io["b_out"]) for c in range(4)]
            for dst, src in small:
                sp.dma_start(dst, src).then_inc(s_const, 16)
            for n, (_, src, k) in enumerate(pieces):
                if n >= STAGES:
                    sp.wait_ge(s_wsplit, n - STAGES + 1)
                sp.dma_start(stage[:, n % STAGES, :].rearrange("p (k e) -> p k e", k=k),
                             src).then_inc(s_staged[n % STAGES], 16)
            sp.wait_ge(s_wsplit, len(pieces))

            def chunk(i, last):
                if not last:
                    apart(sp, s_slot, filled(i, C - 1, ("h1", UNITS - 1)), s_passed["sp"])
                    load_x(i + 1)
                for t in range(TT):
                    k = t % STAGES
                    per = TT // STAGES
                    apart(sp, s_out[k], 16 * (i * per + t // STAGES) + 16, s_passed["sp"])
                    sp.dma_start(stage[:, k, :], x2_dram[bass.ds(i * S + t * P, P), :]).then_inc(s_res[k], 16)
                    if t >= 1:
                        store(i, t - 1)
                store(i, TT - 1)

            def store(i, t):
                k = t % STAGES
                apart(sp, s_y, i * TT + t + 1, s_passed["sp"])
                sp.dma_start(io["out"][bass.ds(i * S + t * P, P), :], stage[:, k, :]).then_inc(s_out[k], 16)

            with sp.Fori(0, B - 1) as i:
                chunk(i, False)
            chunk(B - 1, True)
            for k in range(STAGES):
                sp.wait_ge(s_out[k], 16 * (1 + B * TT // STAGES))

        @block.gpsimd
        def _(pool):
            done = [0]

            def step(ins):
                done[0] += 1
                ins.then_inc(s_pl, 1)
                pool.wait_ge(s_pl, done[0])

            def mark(t, op, base, pattern, channel):
                step(pool.affine_select(out=t, in_=t, compare_op=op, fill=1.0, base=base,
                                        pattern=pattern, channel_multiplier=channel))

            for t in (half, ident, fold, before, pick, gate_t):
                step(pool.memset(t[:], -0.5 if t is half else 0.0))
            mark(ident[:], ALU.not_equal, 0, [[-1, P]], 1)
            mark(fold[:], ALU.not_equal, 0, [[-1, NE]], 1)
            mark(fold[:], ALU.not_equal, -NE, [[-1, NE]], 1)
            mark(before[:], ALU.is_ge, 0, [[-1, NE], [1, NE]], 0)
            mark(pick[:, 0:1], ALU.is_ge, -48, [[0, 1]], 1)
            sel = cmp_gt[0:32, :, :, :].rearrange("p a b c -> p (a b c)")[:, 0:P]
            for n in range(N):
                if n:
                    pool.wait_ge(s_small, n)
                step(pool.memset(sel, 0.0))
                mark(sel, ALU.not_equal, -n, [[0, P]], 1)
                mark(sel, ALU.not_equal, -(n + NE), [[0, P]], 1)
                pool.memset(half[:], -0.5).then_inc(s_prep, 1)
            for n, (dst, _, k) in enumerate(pieces):
                pool.wait_ge(s_staged[n % STAGES], 16 * (n // STAGES + 1))
                src = stage[:, n % STAGES, :].rearrange("p (k e) -> p k e", k=k)
                pool.tensor_copy(dst[0], src).then_inc(s_whi, 1)
                pool.wait_ge(s_whi, n + 1)
                pool.tensor_tensor(dst[1], src, dst[0].bitcast(F32), ALU.subtract).then_inc(s_wsplit, 1)
            with pool.Fori(0, B) as i:
                for t in range(TT):
                    k = t % STAGES
                    apart(pool, s_var, i * TT + t + 1, s_passed["pool"])
                    pool.tensor_scalar(rstd[:, k, 0:1], mv[:, k, 1:2], EPS, None, ALU.add).then_inc(s_pow0, 1)
                    pool.wait_ge(s_pow0, i * TT + t + 1)
                    pool.tensor_tensor(rstd[:, k, 1:2], rstd[:, k, 0:1], half[:], ALU.pow).then_inc(s_pow, 1)

        @block.scalar
        def _(act):
            act.wait_ge(s_const, 16 * 8)
            act.wait_ge(s_small, N + 3)
            with act.Fori(0, B) as i:
                for j in range(C):
                    act.wait_ge(s_slot, filled(i, j, "gate"))
                    act.activation(gate_t[:], bank("gate")[0:16, :], ACT.Copy).then_inc(s_gatecopy, 1)
                    for u in range(UNITS):
                        if u == SH:
                            act.wait_ge(s_slot, filled(i, j, "wt"))
                            act.activation(wt[0:32, :], bank("wt")[0:32, :], ACT.Copy)
                            act.activation(wt[32:64, :], bank("wt")[0:32, :], ACT.Copy).then_inc(s_wt, 1)
                        for m in range(ET):
                            act.wait_ge(s_slot, filled(i, j, (f"h{m}", u)))
                            if u:
                                act.wait_ge(s_gsplit, ET * units(i, j, u - 1) + m + 1)
                            act.activation(h[:, m, :], bank((f"h{m}", u))[:], ACT.Identity,
                                           bias=b_up[:, u, m:m + 1]).then_inc(s_h, 1)
                        if u == 0:
                            act.wait_ge(s_dif, i * C + j + 1)
                            act.activation(ex[:], lg[:], ACT.Exp).then_inc(s_exp, 1)
                        for m in range(ET):
                            z = bank((f"z{m}", u))
                            act.wait_ge(s_slot, filled(i, j, (f"z{m}", u)))
                            act.activation(z[:], z[:], ACT.Silu,
                                           bias=b_sw[:, sw_of(u), m:m + 1]).then_inc(s_silu, 1)

        @block.tensor
        def _(pe):
            def product(out, pairs):
                for n, (lhs, rhs) in enumerate(pairs):
                    mm = pe.matmul(out, lhs, rhs, start=(n == 0), stop=(n == len(pairs) - 1))
                return mm

            pe.wait_ge(s_small, N + 3)
            with pe.Fori(0, B) as i:
                for j in range(C):
                    def up(u):
                        pe.wait_ge(s_wsplit, need["up", u])
                        for m in range(ET):
                            out = bank((f"h{m}", u))
                            s = SLOT[f"h{m}", u] - len(ring)
                            if u >= 1:
                                free(s)
                            product(out[:], [(w_up[a][:, u, k, m * P:(m + 1) * P], xt[b][:, k, :])
                                             for k in range(KT) for a, b in PARTS]).then_inc(s_slot, 1)

                    def free(s):
                        key = next(k for k, v in SLOT.items() if v == s)
                        if key == "gate":
                            pe.wait_ge(s_lg, i * C + j + 1)
                        elif key == "wt":
                            pe.wait_ge(s_wt, i * C + j + 1)
                        elif key[0][0] == "h":
                            pe.wait_ge(s_h, ET * units(i, j, key[1]) + int(key[0][1]) + 1)
                        elif key[0] == "wb":
                            pe.wait_ge(s_wb, (i * C + j) * N + key[1] - SH + 1)
                        else:
                            pe.wait_ge(s_zread, ET * units(i, j, key[1]) + int(key[0][1]) + 1)

                    def gate_weights_by_token():
                        pe.wait_ge(s_gatecopy, i * C + j + 1)
                        for t in range(TT):
                            mm = pe.matmul(bank("gate")[:, t * NE:(t + 1) * NE], gate_t[:, t * P:(t + 1) * P],
                                           fold[:], start=True, stop=True)
                        mm.then_inc(s_tok, 1)

                    def broadcast(u):
                        free(SLOT["wb", u] - len(ring))
                        if u == SH:
                            pe.wait_ge(s_wt, i * C + j + 1)
                        pe.matmul(bank(("wb", u))[:], rows[0:32, (u - SH) * P:(u - SH + 1) * P], wt[0:32, :],
                                  start=True, stop=True).then_inc(s_slot, 1)

                    def sw(u):
                        pe.wait_ge(s_wsplit, need["sw", u])
                        for m in range(ET):
                            s = SLOT[f"z{m}", u] - len(ring)
                            if s >= 0:
                                free(s)
                            pe.wait_ge(s_hsplit, ET * units(i, j, u) + (m + 1 if m == 0 else ET))
                            pairs = []
                            for k in range(ET):
                                for a, b in PARTS:
                                    pairs.append((w_sw[a][:, sw_of(u), k, m * P:(m + 1) * P], hp[b][:, k, :]))
                            for n, (lhs, rhs) in enumerate(pairs):
                                if m == 0 and n == len(PARTS):
                                    pe.wait_ge(s_hsplit, ET * units(i, j, u) + ET)
                                mm = pe.matmul(bank((f"z{m}", u))[:], lhs, rhs, start=(n == 0),
                                               stop=(n == len(pairs) - 1))
                            mm.then_inc(s_slot, 1)

                    def dn(u):
                        pe.wait_ge(s_wsplit, need["dn", u])
                        for k in range(ET):
                            pe.wait_ge(s_gsplit, ET * units(i, j, u) + k + 1)
                            for m in range(KT):
                                if j == 0 and u == 0 and k == 0:
                                    pe.wait_ge(s_accfree, i * KT + m + 1)
                                for a, b in PARTS:
                                    if j == 0:
                                        lhs, rhs = w_dn[a][:, u, k, m * P:(m + 1) * P], gp[b][:, k, :]
                                    else:
                                        lhs, rhs = gp[b][:, k, m * P:(m + 1) * P], w_dn[a][:, u, k, :]
                                    mm = pe.matmul(acc[m][:], lhs, rhs,
                                                   start=(u == 0 and k == 0 and (a, b) == (0, 0)), stop=False)
                        mm.then_inc(s_dn, 1)

                    def out_bias():
                        for m in range(KT):
                            if j == 0:
                                lhs, rhs = rows[32:64, m * P:(m + 1) * P], wt[32:64, :]
                            else:
                                lhs, rhs = wt[32:64, m * P:(m + 1) * P], rows[32:64, 0:H]
                            pe.matmul(acc[m][:], lhs, rhs, start=False, stop=True).then_inc(s_acc, 1)

                    if j == 0:
                        for part in range(2):
                            pe.wait_ge(s_xload[part], 16 * i + 16)
                    gate_pairs = []
                    for k in range(KT):
                        if j == 1:
                            pe.wait_ge(s_xt, i * KT + k + 1)
                        at = (j * KT + k) * 16
                        for b in range(2):
                            mm = pe.matmul(bank("gate")[:], w_gate[:, at:at + P], xt[b][:, k, :],
                                           start=(k == 0 and b == 0), stop=(k == KT - 1 and b == 1))
                    mm.then_inc(s_slot, 1)
                    for u in range(UNITS):
                        up(u)
                        if u == 0:
                            gate_weights_by_token()
                        if u == SH:
                            pass
                        if u:
                            dn(u - 1)
                        if u >= SH:
                            broadcast(u)
                        sw(u)
                        if u == SH - 1:
                            free(SLOT["wt"] - len(ring))
                            pe.wait_ge(s_gw, i * C + j + 1)
                            for t in range(TT):
                                mm = pe.transpose(bank("wt")[0:32, t * P:(t + 1) * P], gw[:, t, :], ident[:])
                            mm.then_inc(s_slot, 1)
                    dn(UNITS - 1)
                    out_bias()

        @block.vector
        def _(dve):
            count = [0]
            base = [0]

            def link(ins):
                count[0] += 1
                ins.then_inc(s_link, 1)
                dve.wait_ge(s_link, base[0] + count[0])

            link(dve.memset(w_gate[:].bitcast(mybir.dt.uint32), 0))
            dve.wait_ge(s_const, 16 * 8)
            wg = w_gate[:, 0:C * KT * 16].rearrange("p (a n) -> p a n", n=16)
            raw = h[:, 0, 0:C * KT * NE].rearrange("p (a n) -> p a n", n=NE)
            link(dve.tensor_copy(wg[:, :, 0:NE], raw))
            link(dve.tensor_tensor(wg[:, :, NE:16], raw, wg[:, :, 0:NE].bitcast(F32), ALU.subtract))
            for n in range(N):
                dve.wait_ge(s_prep, n + 1)
                dve.tensor_copy(rows[0:32, n * P:(n + 1) * P],
                                cmp_gt[0:32, :, :, :].rearrange("p a b c -> p (a b c)")[:, 0:P]).then_inc(s_small, 1)
            bd = rows[32:64, 0:H]
            raw = h[32:64, 1, :]
            low = h[32:64, 0, :]
            link(dve.tensor_copy(bd, raw))
            link(dve.tensor_tensor(low, raw, bd.bitcast(F32), ALU.subtract))
            link(dve.tensor_scalar(pick[32:64, 1:2], pick[32:64, 0:1], -1.0, 1.0, ALU.mult, ALU.add))
            link(dve.tensor_scalar(low, low, pick[32:64, 1:2], None, ALU.mult))
            link(dve.scalar_tensor_tensor(out=bd, in0=bd.bitcast(F32), scalar=pick[32:64, 0:1], in1=low,
                                          op0=ALU.mult, op1=ALU.add))
            dve.memset(gw[:], 0.0).then_inc(s_small, 1)
            dve.memset(stats[:], 0.0).then_inc(s_small, 1)
            dve.memset(mv[:], 0.0).then_inc(s_small, 1)
            link(dve.memset(top[:], 0.0))
            dve.memset(rank[:], 0.0).then_inc(s_accfree, KT)
            dve.memset(rstd[:, 0, :], 0.0).then_inc(s_out[0], 16)
            dve.memset(rstd[:, 1, :], 0.0).then_inc(s_out[1], 16)
            s0 = count[0]

            with dve.Fori(0, B) as i:
                base[0] = i * FFN_LINKS
                for j in range(C):
                    def split_h(u):
                        for m in range(ET):
                            dve.wait_ge(s_h, ET * units(i, j, u) + m + 1)
                            link(dve.tensor_copy(hp[0][:, m, :], h[:, m, :]))
                            dve.tensor_tensor(hp[1][:, m, :], h[:, m, :], hp[0][:, m, :].bitcast(F32),
                                              ALU.subtract).then_inc(s_hsplit, 1)

                    def gated(u):
                        if u >= SH:
                            dve.wait_ge(s_slot, filled(i, j, ("wb", u)))
                            for m in range(ET):
                                ins = dve.tensor_tensor(h[:, m, :], h[:, m, :], bank(("wb", u))[:], ALU.mult)
                                if m == ET - 1:
                                    ins.then_inc(s_wb, 1)
                            dve.wait_ge(s_wb, (i * C + j) * N + u - SH + 1)
                        for m in range(ET):
                            dve.wait_ge(s_silu, ET * units(i, j, u) + m + 1)
                            dve.tensor_tensor(h[:, m, :], h[:, m, :], bank((f"z{m}", u))[:],
                                              ALU.mult).then_inc(s_zread, 1)
                            dve.wait_ge(s_zread, ET * units(i, j, u) + m + 1)
                            if u and m == 0:
                                dve.wait_ge(s_dn, units(i, j, u))
                            link(dve.tensor_copy(gp[0][:, m, :], h[:, m, :]))
                            dve.tensor_tensor(gp[1][:, m, :], h[:, m, :], gp[0][:, m, :].bitcast(F32),
                                              ALU.subtract).then_inc(s_gsplit, 1)

                    def logits():
                        dve.wait_ge(s_tok, i * C + j + 1)
                        dve.tensor_tensor(lg[:], bank("gate")[:, 0:TT * NE].rearrange("p (t n) -> p t n", t=TT),
                                          b_gate[:, j, :].unsqueeze(1).to_broadcast([P, TT, NE]),
                                          ALU.add).then_inc(s_lg, 1)
                        dve.wait_ge(s_lg, i * C + j + 1)
                        own = lg[:].unsqueeze(3).to_broadcast([P, TT, NE, NE])
                        other = lg[:].unsqueeze(2).to_broadcast([P, TT, NE, NE])
                        link(dve.tensor_tensor(cmp_gt[:], other, own, ALU.is_equal))
                        link(dve.tensor_tensor(cmp_gt[:], cmp_gt[:],
                                               before[:].unsqueeze(1).to_broadcast([P, TT, NE, NE]), ALU.mult))
                        link(dve.tensor_reduce(rank[:], cmp_gt[:], AX.X, ALU.add))
                        link(dve.tensor_tensor(cmp_gt[:], other, own, ALU.is_gt))
                        link(dve.tensor_reduce(ex[:], cmp_gt[:], AX.X, ALU.add))
                        link(dve.tensor_tensor(rank[:], rank[:], ex[:], ALU.add))
                        link(dve.tensor_reduce(top[:], lg[:], AX.X, ALU.max))
                        dve.tensor_tensor(lg[:], lg[:], top[:].unsqueeze(2).to_broadcast([P, TT, NE]),
                                          ALU.subtract).then_inc(s_dif, 1)

                    def gate_softmax():
                        dve.wait_ge(s_exp, i * C + j + 1)
                        link(dve.scalar_tensor_tensor(out=ex[:], in0=rank[:], scalar=TOP - 0.5, in1=ex[:],
                                                      op0=ALU.is_lt, op1=ALU.mult))
                        link(dve.tensor_reduce(top[:], ex[:], AX.X, ALU.add))
                        link(dve.reciprocal(top[:], top[:]))
                        link(dve.tensor_tensor(ex[:], ex[:], top[:].unsqueeze(2).to_broadcast([P, TT, NE]),
                                               ALU.mult))
                        link(dve.memset(ex[:, :, N:N + 1], 1.0))
                        link(dve.memset(ex[:, :, N + 1:NE], 0.0))
                        link(dve.tensor_copy(gw[:, :, 0:NE].bitcast(F32R), ex[:]))
                        link(dve.tensor_tensor(gw[:, :, NE:2 * NE], ex[:], gw[:, :, 0:NE], ALU.subtract))
                        dve.tensor_copy(gw[:, :, 16:32], gw[:, :, 0:16]).then_inc(s_gw, 1)

                    for u in range(UNITS):
                        split_h(u)
                        if u == 0:
                            logits()
                        gated(u)
                        if u == 0:
                            gate_softmax()

                    if j == 0:
                        for m in range(KT):
                            dve.wait_ge(s_acc, (i * C + j) * KT + m + 1)
                            tmp = h[:, m % ET, :]
                            link(dve.tensor_tensor(tmp, xt[0][:, m, :].bitcast(F32), acc[m][:], ALU.add))
                            link(dve.tensor_tensor(tmp, tmp, xt[1][:, m, :].bitcast(F32), ALU.add))
                            link(dve.tensor_copy(xt[0][:, m, :], tmp))
                            dve.tensor_tensor(xt[1][:, m, :], tmp, xt[0][:, m, :].bitcast(F32),
                                              ALU.subtract).then_inc(s_xt, 1)
                        dve.wait_ge(s_xt, i * KT + KT)
                    else:
                        def add(t):
                            k = t % STAGES
                            dve.wait_ge(s_acc, (i * C + j) * KT + t + 1)
                            dve.wait_ge(s_res[k], 16 * (i * (TT // STAGES) + t // STAGES + 1))
                            dve.tensor_tensor(stage[:, k, :], stage[:, k, :], acc[t][:],
                                              ALU.add).then_inc(s_accfree, 1)
                            dve.wait_ge(s_accfree, KT + i * TT + t + 1)
                            dve.bn_stats(stats[:, k, :], stage[:, k, :]).then_inc(s_stats, 1)
                            apart(dve, s_stats, i * TT + t + 1, s_passed["dve"])
                            dve.bn_aggr(mv[:, k, :], stats[:, k, :]).then_inc(s_var, 1)

                        def norm(t):
                            k = t % STAGES
                            dve.wait_ge(s_var, i * TT + t + 1)
                            dve.wait_ge(s_pow, i * TT + t + 1)
                            dve.tensor_scalar(stage[:, k, :], stage[:, k, :], mv[:, k, 0:1], rstd[:, k, 1:2],
                                              ALU.subtract, ALU.mult).then_inc(s_y, 1)

                        for t in range(TT):
                            add(t)
                            if t:
                                norm(t - 1)
                        norm(TT - 1)
                assert count[0] == FFN_LINKS + s0, count[0] - s0


def lay_out_attention(x, ctx, Wqkv, bqkv, Wo, bo, Wq, bq, Wk, bk):
    import numpy as np
    tiles = lambda a: np.ascontiguousarray(a.reshape(a.shape[0], a.shape[1], -1, P).transpose(0, 3, 2, 1))
    return dict(
        x=x.reshape(-1, H), xt=tiles(x), ctxt=tiles(ctx),
        w_qkv=np.ascontiguousarray(Wqkv.reshape(KT, P, 3, H).transpose(2, 1, 0, 3)),
        qk_bias=np.ascontiguousarray(bqkv[:2 * H].reshape(2, KT, P).transpose(2, 0, 1)),
        v_bias=np.ascontiguousarray(bqkv[2 * H:].reshape(KT, P).T), Wo=Wo, bo=bo,
        w_x=np.ascontiguousarray(np.stack([Wq, Wk]).reshape(2, 128, -1, P).transpose(3, 0, 2, 1)),
        x_bias=np.ascontiguousarray(np.stack([bq, bk], 1)))


def lay_out_ffn(Wg, bg, Wup, bup, Wsw, bsw, Wdn, bdn, Wsu, bsu, Wsa, bsa, Wsd, bsd):
    import numpy as np
    cols = lambda *v: np.ascontiguousarray(
        np.concatenate([a.reshape(-1, 2, P) for a in v]).transpose(2, 0, 1))
    return dict(
        b_up=cols(bsu, bup), b_sw=cols(bsa, bsw), bg=bg,
        w_gate=np.ascontiguousarray(Wg.reshape(2, 4, P, 8).transpose(2, 0, 1, 3).reshape(P, 64)),
        b_out=np.concatenate([bdn, bsd[None], np.zeros_like(bsd)[None]]),
        Wup=Wup, Wsw=Wsw, Wdn=Wdn, Wsu=Wsu, Wsa=Wsa, Wsd=Wsd)


def decoder_layer(nc, io, out):
    x2 = nc.dram_tensor("x2_rows", [B * S, H], F32).ap()
    x2t = nc.dram_tensor("x2_transposed", [2, B, P, KT, S], F32R).ap()
    with ExitStack() as sems:
        attention(nc, sems, io, x2, x2t)
        feed_forward(nc, sems, io | {"out": out}, x2, x2t)


def kernel(x, ctx_1024, L0_attn_Wqkv, L0_attn_bqkv, L0_attn_Wo, L0_attn_bo, L0_xattn_Wq, L0_xattn_bq,
           L0_xattn_Wk, L0_xattn_bk, L0_ffn_Wg, L0_ffn_bg, L0_ffn_Wup, L0_ffn_bup, L0_ffn_Wsw, L0_ffn_bsw,
           L0_ffn_Wdn, L0_ffn_bdn, L0_ffn_Wsu, L0_ffn_bsu, L0_ffn_Wsa, L0_ffn_bsa, L0_ffn_Wsd, L0_ffn_bsd):
    import numpy as np
    import concourse.bacc as bacc
    from concourse.bass_utils import run_bass_kernel_spmd

    attn = [np.asarray(a) for a in (x, ctx_1024, L0_attn_Wqkv, L0_attn_bqkv, L0_attn_Wo, L0_attn_bo,
                                    L0_xattn_Wq, L0_xattn_bq, L0_xattn_Wk, L0_xattn_bk)]
    ffn = [np.asarray(a) for a in (L0_ffn_Wg, L0_ffn_bg, L0_ffn_Wup, L0_ffn_bup, L0_ffn_Wsw, L0_ffn_bsw,
                                   L0_ffn_Wdn, L0_ffn_bdn, L0_ffn_Wsu, L0_ffn_bsu, L0_ffn_Wsa, L0_ffn_bsa,
                                   L0_ffn_Wsd, L0_ffn_bsd)]
    laid = lay_out_attention(*attn) | lay_out_ffn(*ffn)
    nc = bacc.Bacc("TRN2", target_bir_lowering=False, num_devices=1)
    arrays, io = {}, {}
    for name, a in laid.items():
        arrays["in_" + name] = np.ascontiguousarray(a)
        io[name] = nc.dram_tensor("in_" + name, a.shape, mybir.dt.from_np(a.dtype), kind="ExternalInput").ap()
    out = nc.dram_tensor("out_rows", [B * S, H], F32, kind="ExternalOutput").ap()
    decoder_layer(nc, io, out)
    result = run_bass_kernel_spmd(nc, [arrays], core_ids=[0])
    return result.results[0]["out_rows"].reshape(B, S, H)
```

```python
import math
from contextlib import ExitStack

import concourse.bass as bass
from concourse import mybir

F32 = mybir.dt.float32
F32R = mybir.dt.float32r
ALU = mybir.AluOpType
ACT = mybir.ActivationFunctionType
AX = mybir.AxisListType

P = 128
B, S, H = 4, 512, 512
KT = H // P
TT = S // P
EPS = 1e-5
PARTS = [(0, 0), (0, 1), (1, 0)]
ATT_LINKS = 11
FFN_LINKS = 94


def apart(eng, sem, value, passed):
    eng.wait_ge(sem, value)
    eng.sem_inc(passed, 1)


def attention(nc, sems, io, x2_dram, x2t_dram, att):
    NH, D = 16, 32
    G = P // D
    NG = NH // G
    DX, CT = 128, 2
    LAG = 2
    SCALE = 1.0 / math.sqrt(D)
    MASKED = -1e30
    slope = [1.0 / 2 ** (n / 2) for n in range(NH)]
    SEEN = TT * (TT + 1) // 2 * P
    ROW = [t * (t + 1) // 2 * P for t in range(TT)]
    ORDER = [3, 2, 0, 1]
    COL = {0: 0, 1: TT * P, 3: TT * P + 3 * P, 2: TT * P + 4 * P}
    RING = 4
    NP = 3
    with ExitStack() as ctx:
        def sb(name, shape, dt=F32):
            return ctx.enter_context(nc.sbuf_tensor("a_" + name, shape, dt))

        def sem(name):
            return sems.enter_context(nc.semaphore("a_" + name))

        def bank(name):
            return ctx.enter_context(nc.psum_tensor("a_" + name, [P, S], F32))

        HL = ("hi", "lo")
        w_qkv = [sb(f"w_qkv_{s}", [P, 3, KT, H], F32R) for s in HL]
        w_o = [sb(f"w_o_{s}", [P, KT, H], F32R) for s in HL]
        w_x = [sb(f"w_x_{s}", [P, 2, CT, DX], F32R) for s in HL]
        dist = sb("dist", [P, S])
        o_bias = sb("o_bias", [P, H])
        xt = [sb(f"xt_{s}", [P, KT, S], F32R) for s in HL]
        raw = sb("raw", [P, 2, S])
        inv_sb = sb("inv_sb", [P, S])
        inv_wide = inv_sb[:].rearrange("p (t g d) -> p t g d", t=TT, g=G)
        nat = sb("nat", [P, 4, S], F32R)
        stack = [[sb(f"stack{n}_{s}", [P, G, S], F32R) for s in ("q", "k")] for n in range(2)]
        ct = [stack[0][0][:, CT * a:CT * (a + 1), :] for a in range(2)]
        crosst = stack[1]
        v = sb("v", [P, TT, H])
        probs = sb("probs", [P, RING, SEEN])
        probs_t = sb("probs_t", [P, G, SEEN])
        x = sb("x", [P, TT, H])
        ident = sb("ident", [P, P])
        q_scale = sb("q_scale", [P, NG])
        qk_bias = sb("qk_bias", [P, 2, NG])
        v_bias = sb("v_bias", [P, KT])
        x_bias = sb("x_bias", [P, 2])
        top = sb("top", [P, 2, TT])
        ntop = sb("ntop", [P, 2, TT])
        total = sb("total", [P, G, TT])
        inv = sb("inv", [P, TT, G])
        stats = sb("stats", [P, TT, 6])
        mv = sb("mv", [P, TT, 2])
        var = sb("var", [P, TT])
        rstd = sb("rstd", [P, TT])
        half = sb("half", [P, 1])
        parts_dram = nc.dram_tensor("qk_parts", [2, P, 4, S], F32).ap()

        ab = [bank(f"proj{n}") for n in range(2)]
        s3, s20, s1 = bank("s3"), bank("s20"), bank("s1")
        tb = [bank(f"turn{n}") for n in range(2)]
        av = bank("av")
        scores = {3: s3[:, 0:4 * P], 2: s20[:, 0:3 * P], 0: s20[:, 3 * P:4 * P], 1: s1[:, 0:2 * P]}

        STEPS = range(NH + LAG + 2)
        QK_AT = {0: [(0, 2, k) for k in range(KT)], 1: [(1, 2, k) for k in range(KT)],
                 2: [(0, 3, 0), (0, 3, 1)], 3: [(0, 3, 2), (0, 3, 3)], 4: [(1, 3, k) for k in range(KT)]}
        COPY_QK_AT = {st: (w, g) for st, tiles in QK_AT.items() for w, g, k in tiles if k == KT - 1}
        SPLIT_QK_AT = {1: (0, 2), 2: (1, 2), 4: (0, 3), 5: (1, 3), 15: (0, NG), 16: (1, NG)}
        SPLIT_CONTEXT_AT, XQK_AT = 12, {14: 0, 15: 1}
        SUMS_AT = {G * (g + 1): g for g in range(NG)}
        SPREAD_AT = {G * (g + 1) + 1: g for g in range(NG)}
        USE_AT = {G * g + G - 1 + LAG + 1: g for g in range(NG)}
        ATT_AT = {st + 1: g for st, g in USE_AT.items()}

        def fillings(last):
            keys = []
            for st in STEPS:
                if st in COPY_QK_AT:
                    w, g = COPY_QK_AT[st]
                    keys.append(("qk"[w], g))
                if st in XQK_AT:
                    keys.append(("x", XQK_AT[st]))
                if st in SPREAD_AT:
                    keys.append(("inv", SPREAD_AT[st]))
            keys += [("wo", t) for t in range(TT)]
            keys += [] if last else [("next", w, g) for g in range(2) for w in "qk"]
            keys += [("xm", t) for t in range(TT)]
            keys += [] if last else [("next", "v", t) for t in range(TT)]
            return keys

        AHEAD = [("next", w, g) for g in range(2) for w in "qk"] + [("next", "v", t) for t in range(TT)]
        NA = len(fillings(False))
        NEXT_QK = [(w, g) for g in range(2) for w in range(2)]
        T = {}
        for hd in range(NH):
            for n in range(3):
                T["p", hd, n] = len(T)
        for what in ("at", "x1t", "x2t"):
            for n in range(KT):
                T[what, n] = len(T)
        NT = len(T)
        assert (NA - fillings(False).index(("wo", 0))) % 2 == 0 and NT % 2 == 0 and len(AHEAD) % 2 == 0

        ENERGY_AT = {NH + LAG - 1: (0, 1, 2), NH + LAG: (3,)}
        EXP_ENERGY_AT = {NH + LAG: (0, 1, 2), NH + LAG + 1: (3,)}
        energy = [s3, s20, s1, s3]
        HEADS = fillings(True).index(("wo", 0))

        class Slots:

            def __init__(self, i, last=False):
                self.i = i
                self.keys = AHEAD if i is None else fillings(last)
                self.heads = 0 if i is None else HEADS

            def bank(self, key):
                n = self.keys.index(key) - self.heads
                return ab[0] if n < 0 else ab[(n + 1) % 2]

            def filled(self, key):
                n = self.keys.index(key) + 1
                return n if self.i is None else len(AHEAD) + self.i * NA + n

            def before(self, key):
                n = self.keys.index(key)
                if n < self.heads:
                    return self.keys[n - 1] if n else ("v", TT - 1)
                if self.heads and n == self.heads:
                    return ("p", NH - 1)
                n = max(n - 2, self.heads - 1)
                return self.keys[n] if n >= 0 else None

        s_win = [sem(f"win{n}") for n in range(5)]
        s_cst = sem("cst")
        s_prep = sem("prep")
        s_wq = sem("wq")
        s_vb, s_vwo = sem("vb"), sem("vwo")
        s_link, s_plink = sem("link"), sem("plink")
        s_xraw, s_craw, s_xin = sem("xraw"), sem("craw"), sem("xin")
        s_xhi, s_xlo = sem("xhi"), sem("xlo")
        s_chi, s_clo = sem("chi"), sem("clo")
        s_xb = sem("xb")
        s_a, s_t, s_s, s_av = sem("a"), sem("t"), sem("s"), sem("av")
        s_rawqk = sem("rawqk")
        s_nathi, s_nat = sem("nathi"), sem("nat")
        s_natout = [sem("natout_q"), sem("natout_k")]
        s_stack = [sem(f"stack{n}") for n in range(2)]
        s_v = sem("v")
        s_ttr = sem("ttr")
        s_ntop = sem("ntop")
        s_exp = sem("exp")
        s_rcp = sem("rcp")
        s_inv = sem("inv")
        s_invc = sem("invc")
        s_pt0 = sem("pt0")
        s_pt1 = sem("pt1")
        s_atm, s_ath, s_atl = sem("atm"), sem("ath"), sem("atl")
        s_e = sem("e")
        s_emax = sem("emax")
        s_en = sem("en")
        s_px = sem("px")
        s_hi = sem("hi")
        s_lo = sem("lo")
        s_wo, s_xm = sem("wo"), sem("xm")
        s_stats = sem("stats")
        s_var = sem("var")
        s_pow0, s_pow = sem("pow0"), sem("pow")
        s_norm = sem("norm")
        s_x2out, s_x2tout = sem("x2out"), [sem("x2tout0"), sem("x2tout1")]
        s_passed = {eng: sem(f"passed_{eng}") for eng in ("sp", "pool", "dve")}

        LOADS = 16 * 2 * NP

        def turn_bank(key):
            if key[0] == "p":
                return (tb[0][:], tb[1][:], ab[1][:])[key[2]]
            return (tb[0], tb[1], s3, s20)[key[1]][:]

        def turned(i, key):
            return i * NT + T[key] + 1

        def split_tile(i, what, n):
            return i * 3 * KT + {"at": 0, "x1t": 1, "x2t": 2}[what] * KT + n + 1

        def qk_tile(e, g, w):
            return (2 * NG + 2) * e + 2 * g + w + 1

        def in_stack(e, g):
            return LOADS * (2 * e + g // 2 + 1)

        flat = probs[:].rearrange("p r n -> p (r n)")
        flat_t = probs_t[:].rearrange("p g n -> p (g n)")
        x_staged = flat_t[:, 0:KT * S].rearrange("p (k n) -> p k n", k=KT)
        wq_staged = flat_t[:, KT * S:2 * KT * S].rearrange("p (k n) -> p k n", k=KT)
        wv_staged = flat[:, 0:KT * H].rearrange("p (k n) -> p k n", k=KT)
        wx_staged = flat[:, KT * H:KT * H + 2 * CT * DX].rearrange("p (w c d) -> p w c d", w=2, c=CT)

        def cross(t):
            return flat[:, t * S:(t + 1) * S]

        block = ctx.enter_context(nc.Block())

        @block.sync
        def _(sp):
            sp.dma_start(wq_staged, io["w_qkv"][0]).then_inc(s_win[0], 16)
            sp.dma_start(x_staged, io["xt"][0]).then_inc(s_xraw, 16)
            for dst, src in [(qk_bias[:], io["qk_bias"]), (x_bias[:], io["x_bias"]), (v_bias[:], io["v_bias"]),
                             (o_bias[:], io["bo"].unsqueeze(0).to_broadcast([P, H]))]:
                sp.dma_start(dst, src).then_inc(s_cst, 16)
            sp.dma_start(v[:], io["w_qkv"][1]).then_inc(s_win[1], 16)
            sp.dma_start(wv_staged, io["w_qkv"][2]).then_inc(s_win[2], 16)
            sp.dma_start(wx_staged, io["w_x"]).then_inc(s_win[3], 16)
            sp.dma_start(x[:], io["Wo"].rearrange("(k p) n -> p k n", p=P)).then_inc(s_win[4], 16)

            def store_parts(e, g, w, first=False):
                apart(sp, s_nat, qk_tile(e, g, w), s_passed["sp"])
                if not first:
                    apart(sp, s_stack[g % 2], in_stack(e, g) - LOADS, s_passed["sp"])
                sp.dma_start(parts_dram[g % 2, :, 2 * w:2 * w + 2, :],
                             nat[:, 2 * w:2 * w + 2, :].bitcast(F32)).then_inc(s_natout[w], 16)

            def load_parts(e, g, w):
                apart(sp, s_natout[w], 16 * (NG * e + g + 1), s_passed["sp"])
                for r in range(NP):
                    part = ((0, 0, 1), (0, 1, 0))[w][r]
                    sp.dma_start(stack[g % 2][w][D * r:D * (r + 1), :, :].bitcast(F32),
                                 parts_dram[g % 2, :, 2 * w + part, :].rearrange("(h d) n -> d h n", d=D)
                                 ).then_inc(s_stack[g % 2], 16)

            for g in range(2):
                for w in range(2):
                    store_parts(0, g, w, first=True)
                for w in range(2):
                    load_parts(0, g, w)
            sp.wait_ge(s_wq, 7)

            def entry(i, last):
                apart(sp, s_x2out, 16 * TT * i + 16, s_passed["sp"])
                sp.dma_start(x[:], io["x"][bass.ds(i * S, S), :].rearrange("(t p) n -> p t n", p=P)
                             ).then_inc(s_xin, 16)
                for g in range(2, NG):
                    for w in range(2):
                        store_parts(i, g, w)
                    apart(sp, s_s, 3 * (NH * i + G * (g - 1)), s_passed["sp"])
                    for w in range(2):
                        load_parts(i, g, w)
                sp.dma_start(raw[:], io["ctxt"][bass.ds(i, 1)].rearrange("o p k n -> (o p) k n")
                             ).then_inc(s_craw, 16)
                if not last:
                    apart(sp, s_av, NG * i + NG, s_passed["sp"])
                    sp.dma_start(x_staged, io["xt"][bass.ds(i + 1, 1)].rearrange("o p k n -> (o p) k n")
                                 ).then_inc(s_xraw, 16)
                    slots = Slots(i)
                    for w in range(2):
                        store_parts(i + 1, 0, w)
                    apart(sp, s_a, slots.filled(("x", 1)), s_passed["sp"])
                    for w in range(2):
                        load_parts(i + 1, 0, w)
                    for w in range(2):
                        store_parts(i + 1, 1, w)
                    apart(sp, s_a, slots.filled(("xm", TT - 1)), s_passed["sp"])
                    for w in range(2):
                        load_parts(i + 1, 1, w)
                for t in range(TT):
                    apart(sp, s_norm, 2 * TT * i + TT + t + 1, s_passed["sp"])
                    sp.dma_start(x2_dram[bass.ds(i * S + t * P, P), :], x[:, t, :]).then_inc(s_x2out, 16)
                if not last:
                    for part in range(2):
                        apart(sp, (s_hi, s_lo)[part], split_tile(i, "x2t", KT - 1) + part, s_passed["sp"])
                        dst = x2t_dram[part, bass.ds(i, 1)].rearrange("o p k n -> (o p) k n")
                        sp.dma_start(dst.bitcast(F32), att[part][:].bitcast(F32)).then_inc(s_x2tout[part], 16)

            with sp.Fori(0, B - 1) as i:
                entry(i, False)
            entry(B - 1, True)
            sp.wait_ge(s_x2out, 16 * TT * B + 16)
            for part in range(2):
                sp.wait_ge(s_x2tout[part], 16 * (B - 1) + 16)

        @block.gpsimd
        def _(pool):
            done = [0]

            def step(ins):
                done[0] += 1
                ins.then_inc(s_plink, 1)
                pool.wait_ge(s_plink, done[0])

            for g in range(NG):
                for r in range(G):
                    ins = pool.memset(q_scale[D * r:D * (r + 1), g:g + 1], SCALE / slope[G * g + r])
                    if (g, r) == (NG - 1, G - 1):
                        ins.then_inc(s_prep, 1)
                        pool.wait_ge(s_prep, 1)
                    else:
                        step(ins)
            step(pool.memset(half[:], -0.5))
            step(pool.memset(ident[:], 0.0))
            pool.affine_select(out=ident[:], in_=ident[:], compare_op=ALU.not_equal, fill=1.0,
                               base=0, pattern=[[-1, P]], channel_multiplier=1).then_inc(s_prep, 1)
            pool.wait_ge(s_prep, 2)
            scratch = inv_sb[:].bitcast(mybir.dt.int32)
            step(pool.iota(scratch, pattern=[[1, S]], base=-(TT - 1) * P, channel_multiplier=-1))
            step(pool.tensor_copy(dist[:], scratch))
            pool.affine_select(out=dist[:], in_=dist[:], compare_op=ALU.is_ge, fill=MASKED,
                               base=(TT - 1) * P, pattern=[[-1, S]], channel_multiplier=1).then_inc(s_prep, 1)
            pool.wait_ge(s_prep, 3)

            def low_qk(e, g, w):
                pool.wait_ge(s_nathi, qk_tile(e, g, w))
                pool.tensor_tensor(nat[:, 2 * w + 1, :], raw[:, w, :], nat[:, 2 * w, :].bitcast(F32),
                                   ALU.subtract).then_inc(s_nat, 1)

            def rstds(n):
                apart(pool, s_var, n + 1, s_passed["pool"])
                pool.tensor_scalar(var[:], mv[:, :, 1], EPS, None, ALU.add).then_inc(s_pow0, 1)
                pool.wait_ge(s_pow0, n + 1)
                pool.tensor_tensor(rstd[:], var[:], half[:].to_broadcast([P, TT]), ALU.pow).then_inc(s_pow, 1)

            def entry(i, last):
                for st in STEPS:
                    if st in SPLIT_QK_AT:
                        w, g = SPLIT_QK_AT[st]
                        low_qk(i, g, w)
                    if st == G + 2:
                        pool.wait_ge(s_xin, 16 * i + 16)
                        for t in range(TT):
                            pool.tensor_tensor(x[:, t, :], x[:, t, :], o_bias[:], ALU.add).then_inc(s_xb, 1)
                    if st == SPLIT_CONTEXT_AT:
                        for c in range(CT):
                            pool.wait_ge(s_chi, CT * i + c + 1)
                            pool.tensor_tensor(ct[1][:, c, :], raw[:, c, :], ct[0][:, c, :].bitcast(F32),
                                               ALU.subtract).then_inc(s_clo, 1)
                    if st in ATT_AT:
                        g = ATT_AT[st]
                        if g == 0:
                            pool.wait_ge(s_x2tout[1], 16 * i + 16)
                        pool.wait_ge(s_ath, NG * i + g + 1)
                        pool.tensor_tensor(att[1][:, g, :], inv_sb[:], att[0][:, g, :].bitcast(F32),
                                           ALU.subtract).then_inc(s_atl, 1)
                rstds(2 * i)
                if not last:
                    for g in range(2):
                        for w in range(2):
                            low_qk(i + 1, g, w)
                rstds(2 * i + 1)

            for g in range(2):
                for w in range(2):
                    low_qk(0, g, w)
            pool.wait_ge(s_wq, 7)
            with pool.Fori(0, B - 1) as i:
                entry(i, False)
            entry(B - 1, True)

        @block.scalar
        def _(act):
            def split_x(e):
                act.wait_ge(s_xraw, 16 * e + 16)
                for k in range(KT):
                    act.activation(xt[0][:, k, :], x_staged[:, k, :], ACT.Copy).then_inc(s_xhi, 1)

            def copy_qk(e, g, w, slots, key):
                act.wait_ge(s_a, slots.filled(key))
                if g == NG:
                    act.wait_ge(s_clo, CT * e + CT)
                    bias, scale = x_bias[:, w:w + 1], 1.0
                else:
                    if not (slots.i is None and g == 0):
                        act.wait_ge(s_nat, qk_tile(e, g, w) - 2)
                    bias, scale = qk_bias[:, w, g:g + 1], q_scale[:, g:g + 1] if w == 0 else 1.0
                act.activation(raw[:, w, :], slots.bank(key)[:], ACT.Identity, bias=bias,
                               scale=scale).then_inc(s_rawqk, 1)

            def copy_v(slots, tiles):
                for t in tiles:
                    act.wait_ge(s_a, slots.filled(("next", "v", t)))
                    act.activation(v[:, t, :], slots.bank(("next", "v", t))[:], ACT.Copy).then_inc(s_v, 1)

            def entry(i, last):
                slots = Slots(i, last)

                def high(what, dst):
                    for n in range(KT):
                        act.wait_ge(s_t, turned(i, (what, n)))
                        act.activation(dst[0][:, n, :], turn_bank((what, n)), ACT.Copy).then_inc(s_hi, 1)

                def exponentials(hd):
                    act.wait_ge(s_ntop, NH * i + hd + 1)
                    if hd % G == 0 and hd:
                        act.wait_ge(s_rcp, NG * i + hd // G)
                    for t in ORDER:
                        at = probs[:, hd % RING, ROW[t]:ROW[t] + (t + 1) * P]
                        act.activation(at, at, ACT.Exp, bias=ntop[:, hd % 2, t:t + 1], scale=slope[hd],
                                       accum_out=total[:, hd % G, t:t + 1]).then_inc(s_exp, 1)

                def copy_turned(hd, n):
                    at, width = ((COL[1], 4 * P), (COL[2], 2 * P))[n - 1]
                    act.wait_ge(s_t, turned(i, ("p", hd, n)))
                    if hd == 0 and n == 1:
                        act.wait_ge(s_xlo, KT * i + KT)
                    elif hd % G == 0 and n == 1:
                        act.wait_ge(s_av, NG * i + hd // G)
                    act.activation(probs_t[:, hd % G, at:at + width], turn_bank(("p", hd, n))[:, 0:width],
                                   ACT.Copy).then_inc(s_pt1, 1)

                for st in STEPS:
                    turns = LAG <= st < NH + LAG
                    if turns and st not in USE_AT:
                        copy_turned(st - LAG, 1)
                        copy_turned(st - LAG, 2)
                    if st < NH:
                        exponentials(st)
                    if turns and st in USE_AT:
                        copy_turned(st - LAG, 1)
                        copy_turned(st - LAG, 2)
                    if st in SUMS_AT:
                        act.wait_ge(s_rcp, NG * i + SUMS_AT[st] + 1)
                        if SUMS_AT[st]:
                            act.wait_ge(s_atl, NG * i + SUMS_AT[st])
                        act.activation(inv_wide, inv[:].unsqueeze(3).to_broadcast([P, TT, G, D]),
                                       ACT.Copy).then_inc(s_inv, 1)
                    if st in COPY_QK_AT:
                        w, g = COPY_QK_AT[st]
                        copy_qk(i, g, w, slots, ("qk"[w], g))
                    if st in XQK_AT:
                        copy_qk(i, NG, XQK_AT[st], slots, ("x", XQK_AT[st]))
                    if st in SPREAD_AT:
                        g = SPREAD_AT[st]
                        act.wait_ge(s_a, slots.filled(("inv", g)))
                        act.activation(inv_sb[:], slots.bank(("inv", g))[:], ACT.Copy).then_inc(s_invc, 1)
                    for t in EXP_ENERGY_AT.get(st, ()):
                        act.wait_ge(s_emax, TT * i + t + 1)
                        act.activation(cross(t), energy[t][:], ACT.Exp, bias=ntop[:, 0, t:t + 1],
                                       accum_out=total[:, 0, t:t + 1]).then_inc(s_en, 1)
                if not last:
                    split_x(i + 1)
                    copy_qk(i + 1, 0, 0, slots, ("next", "q", 0))
                high("at", crosst)
                if not last:
                    for w, g in NEXT_QK[1:]:
                        copy_qk(i + 1, g, w, slots, ("next", "qk"[w], g))
                high("x1t", att)
                if not last:
                    copy_v(slots, range(TT - 1))
                high("x2t", att)
                if not last:
                    copy_v(slots, range(TT - 1, TT))

            split_x(0)
            act.wait_ge(s_wq, 2)
            slots = Slots(None)
            for g in range(2):
                for w in range(2):
                    copy_qk(0, g, w, slots, ("next", "qk"[w], g))
            copy_v(slots, range(TT))
            with act.Fori(0, B - 1) as i:
                entry(i, False)
            entry(B - 1, True)

        @block.tensor
        def _(pe):
            def product(out, pairs):
                for n, (lhs, rhs) in enumerate(pairs):
                    mm = pe.matmul(out, lhs, rhs, start=(n == 0), stop=(n == len(pairs) - 1))
                return mm

            def add_tile(out, k, lhs, rhs, t):
                for n, (a, b) in enumerate(PARTS):
                    mm = pe.matmul(out[:], lhs[b][:, k, t * P:(t + 1) * P], rhs[a][:, k, :],
                                   start=(k == 0 and n == 0), stop=(k == KT - 1 and n == len(PARTS) - 1))
                return mm

            def free_a(slots, key):
                old = slots.before(key)
                if old is None:
                    return
                e = 0 if slots.i is None else slots.i
                ahead = 0 if slots.i is None else 1
                what, n = old[0], old[-1]
                if what == "next" and old[1] == "v":
                    pe.wait_ge(s_v, TT * (e + ahead) + n + 1)
                elif what == "next":
                    pe.wait_ge(s_rawqk, qk_tile(e + ahead, n, "qk".index(old[1])))
                elif what in ("q", "k"):
                    pe.wait_ge(s_rawqk, qk_tile(e, n, "qk".index(what)))
                elif what == "x":
                    pe.wait_ge(s_rawqk, qk_tile(e, NG, n))
                elif what == "p":
                    pe.wait_ge(s_pt1, 2 * (NH * e + NH))
                else:
                    per = NG if what == "inv" else TT
                    pe.wait_ge({"v": s_v, "inv": s_invc, "wo": s_wo, "xm": s_xm}[what],
                               per * e + n + 1)

            def project_qk_tile(slots, key, w, g, k):
                if k == 0:
                    free_a(slots, key)
                for n, (a, b) in enumerate(PARTS):
                    mm = pe.matmul(slots.bank(key)[:], w_qkv[a][:, w, k, g * P:(g + 1) * P], xt[b][:, k, :],
                                   start=(k == 0 and n == 0), stop=(k == KT - 1 and n == len(PARTS) - 1))
                if k == KT - 1:
                    mm.then_inc(s_a, 1)

            def project_next_qk(e, slots, tiles):
                for w, g in tiles:
                    if slots.i is None and g == 0:
                        pe.wait_ge(s_wq, (1, 3)[w])
                    for k in range(KT):
                        if (w, g) == (0, 0):
                            pe.wait_ge(s_xlo, KT * e + k + 1)
                        project_qk_tile(slots, ("next", "qk"[w], g), w, g, k)

            def project_v(slots, tiles):
                for t in tiles:
                    key = ("next", "v", t)
                    free_a(slots, key)
                    product(slots.bank(key)[:], [(xt[b][:, k, t * P:(t + 1) * P], w_qkv[a][:, 2, k, :])
                                                 for k in range(KT) for a, b in PARTS]).then_inc(s_a, 1)

            def entry(i, last):
                slots = Slots(i, last)

                def free_t(key):
                    what, n = key[0], key[-1]
                    heads = key[1] if what == "p" else NH
                    if what == "p" and heads == 0:
                        if n == 2:
                            pe.wait_ge(s_v, TT * i + TT - 1)
                        return
                    if what in ("x1t", "x2t"):
                        pe.wait_ge(s_lo, split_tile(i, what, n) - KT + 1)
                    elif what == "at" and n > 1:
                        pe.wait_ge(s_en, TT * i + TT)
                    elif n == 0:
                        pe.wait_ge(s_pt0, NH * i + heads)
                    else:
                        pe.wait_ge(s_pt1, 2 * (NH * i + heads - 1) + n)

                def turn_probs(hd, n):
                    if n == 0:
                        pe.wait_ge(s_exp, TT * (NH * i + hd + 1))
                    free_t(("p", hd, n))
                    out = turn_bank(("p", hd, n))
                    at = 0
                    for c in ((0,), (1, 3), (2,))[n]:
                        for t in range(c, TT):
                            mm = pe.transpose(out[:, at:at + P],
                                              probs[:, hd % RING, ROW[t] + c * P:ROW[t] + (c + 1) * P],
                                              ident[:])
                            at += P
                    mm.then_inc(s_t, 1)

                def turn(what, src):
                    for n in range(KT):
                        free_t((what, n))
                        for t in range(TT):
                            mm = pe.transpose(turn_bank((what, n))[:, t * P:(t + 1) * P], src(t, n), ident[:])
                        mm.then_inc(s_t, 1)

                for st in STEPS:
                    if st < NH:
                        hd, g = st, st // G
                        if hd % G == 0:
                            pe.wait_ge(s_stack[g % 2], in_stack(i, g))
                        if hd == 0:
                            pe.wait_ge(s_lo, 3 * KT * i + 1)
                        for t in ORDER:
                            if hd:
                                pe.wait_ge(s_ttr, TT * (NH * i + hd - 1) + {3: 1, 2: 3, 0: 3, 1: 4}[t])
                            mm = pe.matmul(scores[t], stack[g % 2][0][0:NP * D, hd % G, t * P:(t + 1) * P],
                                           stack[g % 2][1][0:NP * D, hd % G, 0:(t + 1) * P],
                                           start=True, stop=True)
                            if t != 2:
                                mm.then_inc(s_s, 1)
                    if st in USE_AT:
                        g = USE_AT[st]
                        pe.wait_ge(s_pt0, NH * i + G * g + G)
                        pe.wait_ge(s_pt1, 2 * (NH * i + G * g + G))
                        if g:
                            pe.wait_ge(s_atm, NG * i + g)
                        else:
                            pe.wait_ge(s_v, TT * i + TT)
                        for c in range(TT):
                            for hh in range(G):
                                mm = pe.matmul(av[D * hh:D * (hh + 1), c * P:S],
                                               v[:, c, (G * g + hh) * D:(G * g + hh + 1) * D],
                                               probs_t[:, hh, COL[c]:COL[c] + S - c * P],
                                               start=(c == 0), stop=(c == TT - 1), skip_group_check=True)
                        mm.then_inc(s_av, 1)
                    if LAG <= st < NH + LAG:
                        turn_probs(st - LAG, 0)
                        turn_probs(st - LAG, 1)
                    if LAG <= st < NH + LAG:
                        turn_probs(st - LAG, 2)
                    for w, g, k in QK_AT.get(st, ()):
                        project_qk_tile(slots, ("qk"[w], g), w, g, k)
                    if st in XQK_AT:
                        w = XQK_AT[st]
                        free_a(slots, ("x", w))
                        if w == 0:
                            pe.wait_ge(s_clo, CT * i + CT)
                        product(slots.bank(("x", w))[:], [(w_x[a][:, w, c, :], ct[b][:, c, :])
                                                          for c in range(CT) for a, b in PARTS]).then_inc(s_a, 1)
                    if st in SPREAD_AT:
                        g = SPREAD_AT[st]
                        free_a(slots, ("inv", g))
                        pe.wait_ge(s_inv, NG * i + g + 1)
                        for t in range(TT):
                            mm = pe.matmul(slots.bank(("inv", g))[:, t * P:(t + 1) * P],
                                           inv_sb[:, t * P:(t + 1) * P], ident[:],
                                           start=True, stop=True)
                        mm.then_inc(s_a, 1)
                    for t in ENERGY_AT.get(st, ()):
                        if t == 0:
                            pe.wait_ge(s_nat, qk_tile(i, NG, 1))
                            pe.wait_ge(s_ttr, TT * (NH * i + NH))
                        elif t == TT - 1:
                            pe.wait_ge(s_en, TT * i + 1)
                        product(energy[t][:], [(nat[:, a, t * P:(t + 1) * P], nat[:, 2 + b, :])
                                               for a, b in PARTS]).then_inc(s_e, 1)
                for t in range(TT):
                    free_a(slots, ("wo", t))
                    for k in range(KT):
                        if t == 0:
                            pe.wait_ge(s_atl, NG * i + k + 1)
                        mm = add_tile(slots.bank(("wo", t)), k, att, w_o, t)
                    mm.then_inc(s_a, 1)
                if not last:
                    project_next_qk(i + 1, slots, NEXT_QK[:1])
                pe.wait_ge(s_px, TT * i + TT)
                turn("at", lambda t, n: cross(t)[:, n * P:(n + 1) * P])
                if not last:
                    project_next_qk(i + 1, slots, NEXT_QK[1:])
                pe.wait_ge(s_norm, 2 * TT * i + TT)
                turn("x1t", lambda t, n: x[:, t, n * P:(n + 1) * P])
                for t in range(TT):
                    free_a(slots, ("xm", t))
                    for k in range(KT):
                        if t == 0:
                            pe.wait_ge(s_lo, split_tile(i, "x1t", k) + 1)
                        mm = add_tile(slots.bank(("xm", t)), k, att, crosst, t)
                    mm.then_inc(s_a, 1)
                if not last:
                    project_v(slots, range(TT - 1))
                pe.wait_ge(s_norm, 2 * TT * i + 2 * TT)
                turn("x2t", lambda t, n: x[:, t, n * P:(n + 1) * P])
                if not last:
                    project_v(slots, range(TT - 1, TT))

            slots = Slots(None)
            project_next_qk(0, slots, NEXT_QK)
            pe.wait_ge(s_wq, 4)
            project_v(slots, range(TT))
            pe.wait_ge(s_prep, 3)
            pe.wait_ge(s_vb, 1)
            pe.wait_ge(s_win[4], 16)
            for k in range(KT):
                mm = pe.matmul(av[:], inv_sb[:, k * P:(k + 1) * P], x[:, k, :], start=(k == 0),
                               stop=(k == KT - 1))
            mm.then_inc(s_vwo, 1)
            pe.wait_ge(s_wq, 7)
            with pe.Fori(0, B - 1) as i:
                entry(i, False)
            entry(B - 1, True)

        @block.vector
        def _(dve):
            count = [0]
            base = [0]

            def link(ins):
                count[0] += 1
                ins.then_inc(s_link, 1)
                dve.wait_ge(s_link, base[0] + count[0])

            def split_weight(parts, src, s):
                dve.wait_ge(s_win[s], 16)
                link(dve.tensor_copy(parts[0], src))
                dve.tensor_tensor(parts[1], src, parts[0].bitcast(F32), ALU.subtract).then_inc(s_wq, 1)

            def split_x(e):
                for k in range(KT):
                    dve.wait_ge(s_xhi, KT * e + k + 1)
                    dve.tensor_tensor(xt[1][:, k, :], x_staged[:, k, :], xt[0][:, k, :].bitcast(F32),
                                      ALU.subtract).then_inc(s_xlo, 1)

            def high_qk(e, g, w):
                dve.wait_ge(s_rawqk, qk_tile(e, g, w))
                if g:
                    dve.wait_ge(s_natout[w], 16 * (NG * e + g))
                dve.tensor_copy(nat[:, 2 * w, :], raw[:, w, :]).then_inc(s_nathi, 1)

            def entry(i, last):
                slots = Slots(i, last)
                base[0] = i * ATT_LINKS
                count[0] = s0

                for st in STEPS:
                    if st < NH:
                        hd = st
                        if hd >= RING:
                            dve.wait_ge(s_t, turned(i, ("p", hd - RING, 2)))
                        if hd >= 2:
                            dve.wait_ge(s_exp, TT * (NH * i + hd - 1))
                        for t in ORDER:
                            if t != 0:
                                apart(dve, s_s, 3 * (NH * i + hd) + {3: 1, 2: 2, 1: 3}[t], s_passed["dve"])
                            dve.tensor_tensor_reduce(probs[:, hd % RING, ROW[t]:ROW[t] + (t + 1) * P],
                                                     scores[t], dist[:, S - (t + 1) * P:S], 1.0, -3e38,
                                                     ALU.add, ALU.max, top[:, hd % 2, t:t + 1]).then_inc(s_ttr, 1)
                        dve.wait_ge(s_ttr, TT * (NH * i + hd + 1))
                        dve.tensor_scalar(ntop[:, hd % 2, :], top[:, hd % 2, :], -slope[hd], None,
                                          ALU.mult).then_inc(s_ntop, 1)
                    if st in SUMS_AT:
                        g = SUMS_AT[st]
                        dve.wait_ge(s_exp, TT * (NH * i + G * g + G))
                        if g:
                            dve.wait_ge(s_inv, NG * i + g)
                        dve.reciprocal(inv[:].rearrange("p t g -> p g t"), total[:]).then_inc(s_rcp, 1)
                    if LAG <= st < NH + LAG:
                        hd = st - LAG
                        dve.wait_ge(s_t, turned(i, ("p", hd, 0)))
                        if hd % G == 0 and hd:
                            dve.wait_ge(s_av, NG * i + hd // G)
                        dve.tensor_copy(probs_t[:, hd % G, 0:S], turn_bank(("p", hd, 0))).then_inc(s_pt0, 1)
                    if st in ATT_AT:
                        g = ATT_AT[st]
                        if g == 0:
                            dve.wait_ge(s_x2tout[0], 16 * i + 16)
                        dve.wait_ge(s_av, NG * i + g + 1)
                        dve.wait_ge(s_invc, NG * i + g + 1)
                        dve.tensor_tensor(inv_sb[:], av[:], inv_sb[:], ALU.mult).then_inc(s_atm, 1)
                        dve.wait_ge(s_atm, NG * i + g + 1)
                        dve.tensor_copy(att[0][:, g, :], inv_sb[:]).then_inc(s_ath, 1)
                    if st == SPLIT_CONTEXT_AT:
                        dve.wait_ge(s_s, 3 * (NH * i + 3 * G))
                        dve.wait_ge(s_craw, 16 * i + 16)
                        for c in range(CT):
                            dve.tensor_copy(ct[0][:, c, :], raw[:, c, :]).then_inc(s_chi, 1)
                    if st in SPLIT_QK_AT:
                        w, g = SPLIT_QK_AT[st]
                        high_qk(i, g, w)

                    for t in EXP_ENERGY_AT.get(st, ()):
                        dve.wait_ge(s_e, TT * i + t + 1)
                        link(dve.tensor_reduce(top[:, 0, t:t + 1], energy[t][:], AX.X, ALU.max))
                        dve.tensor_scalar(ntop[:, 0, t:t + 1], top[:, 0, t:t + 1], -1.0, None,
                                          ALU.mult).then_inc(s_emax, 1)

                dve.wait_ge(s_en, TT * i + TT)
                dve.wait_ge(s_inv, NG * i + NG)
                link(dve.reciprocal(inv[:, :, 0], total[:, 0, :]))
                for t in range(TT):
                    dve.tensor_scalar(cross(t), cross(t), inv[:, t, 0:1], None, ALU.mult).then_inc(s_px, 1)

                def add(what, t, s):
                    dve.wait_ge(s_a, slots.filled((what, t)))
                    dve.tensor_tensor(x[:, t, :], x[:, t, :], slots.bank((what, t))[:], ALU.add).then_inc(s, 1)
                    dve.wait_ge(s, TT * i + t + 1)
                    dve.bn_stats(stats[:, t, :], x[:, t, :]).then_inc(s_stats, 1)
                    apart(dve, s_stats, 2 * TT * i + (TT if what == "xm" else 0) + t + 1, s_passed["dve"])
                    ins = dve.bn_aggr(mv[:, t, :], stats[:, t, :])
                    ins.then_inc(s_var, 1) if t == TT - 1 else link(ins)

                def norm(n):
                    dve.wait_ge(s_pow, 2 * i + n + 1)
                    for t in range(TT):
                        dve.tensor_scalar(x[:, t, :], x[:, t, :], mv[:, t, 0:1], rstd[:, t:t + 1],
                                          ALU.subtract, ALU.mult).then_inc(s_norm, 1)

                def lows(what, dst):
                    for n in range(KT):
                        dve.wait_ge(s_hi, split_tile(i, what, n))
                        dve.tensor_tensor(dst[1][:, n, :], turn_bank((what, n)), dst[0][:, n, :].bitcast(F32),
                                          ALU.subtract).then_inc(s_lo, 1)

                dve.wait_ge(s_xb, TT * i + TT)
                for t in range(TT):
                    add("wo", t, s_wo)
                    if t == 1 and not last:
                        split_x(i + 1)
                norm(0)
                if not last:
                    high_qk(i + 1, 0, 0)
                lows("at", crosst)
                if not last:
                    for w, g in NEXT_QK[1:]:
                        high_qk(i + 1, g, w)
                lows("x1t", att)
                for t in range(TT):
                    add("xm", t, s_xm)
                norm(1)
                lows("x2t", att)
                if not last:
                    assert count[0] == ATT_LINKS + s0, count[0] - s0

            split_weight([part[:, 0] for part in w_qkv], wq_staged, 0)
            split_x(0)
            dve.wait_ge(s_prep, 1)
            dve.wait_ge(s_cst, 16 * 4)
            dve.tensor_tensor(qk_bias[:, 0, :], qk_bias[:, 0, :], q_scale[:], ALU.mult).then_inc(s_wq, 1)
            dve.wait_ge(s_prep, 3)
            dve.tensor_copy(inv_sb[:].rearrange("p (k n) -> p k n", k=KT),
                            v_bias[:].unsqueeze(2).to_broadcast([P, KT, P])).then_inc(s_vb, 1)
            split_weight([part[:, 1] for part in w_qkv], v[:], 1)
            for w in range(2):
                high_qk(0, 0, w)
            split_weight([part[:, 2] for part in w_qkv], wv_staged, 2)
            for w in range(2):
                high_qk(0, 1, w)
            split_weight([part[:] for part in w_x], wx_staged, 3)
            split_weight([part[:] for part in w_o], x[:], 4)
            dve.wait_ge(s_vwo, 1)
            dve.tensor_tensor(o_bias[:], o_bias[:], av[:], ALU.add).then_inc(s_wq, 1)
            link(dve.memset(stats[:], 0.0))
            dve.memset(mv[:, 0, :], 0.0).then_inc(s_x2out, 16)
            dve.memset(mv[:, 1, :], 0.0).then_inc(s_x2tout[0], 16)
            dve.memset(mv[:, 2, :], 0.0).then_inc(s_x2tout[1], 16)
            dve.memset(mv[:, 3, :], 0.0).then_inc(s_lo, 1)
            s0 = count[0]
            with dve.Fori(0, B - 1) as i:
                entry(i, False)
            entry(B - 1, True)


def feed_forward(nc, sems, io, x2_dram, x2t_dram, xt):
    N, C, E, NE = 6, 2, 256, 8
    SH = 2
    UNITS = SH + N
    TOP = N
    ET = E // P
    PIECE = 512
    STAGES = 2
    ctx = ExitStack()
    with ctx:
        def sb(name, shape, dt=F32):
            return ctx.enter_context(nc.sbuf_tensor(name, shape, dt))

        def sem(name):
            return sems.enter_context(nc.semaphore("f_" + name))

        w_up = [sb(f"w_up_{s}", [P, UNITS, KT, E], F32R) for s in ("hi", "lo")]
        w_sw = [sb(f"w_sw_{s}", [P, 1 + N, ET, E], F32R) for s in ("hi", "lo")]
        w_dn = [sb(f"w_dn_{s}", [P, UNITS, ET, H], F32R) for s in ("hi", "lo")]
        w_gate = sb("w_gate", [P, KT * C * 16 + 112], F32R)
        rows = sb("rows", [64, N * P], F32R)
        wt = sb("wt", [64, S], F32R)
        h = sb("h", [P, ET, S])
        hp = [sb(f"h_{s}", [P, ET, S], F32R) for s in ("hi", "lo")]
        gp = [sb(f"g_{s}", [P, ET, S], F32R) for s in ("hi", "lo")]
        stage = sb("stage", [P, STAGES, PIECE])
        ident = sb("ident", [P, P], F32R)
        gate_t = sb("gate_t", [16, S])
        fold = sb("fold", [16, 8])
        b_up = sb("b_up", [P, UNITS, ET])
        b_sw = sb("b_sw", [P, 1 + N, ET])
        b_gate = sb("b_gate", [P, C, NE])
        before = sb("before", [P, NE, NE])
        lg = sb("lg", [P, TT, NE])
        cmp_gt = sb("cmp_gt", [P, TT, NE, NE])
        rank = sb("rank", [P, TT, NE])
        top = sb("top", [P, TT])
        ex = sb("ex", [P, TT, NE])
        gw = sb("gw", [P, TT, 32])
        stats = sb("stats", [P, 2, 6])
        mv = sb("mv", [P, 2, 2])
        rstd = sb("rstd", [P, 2, 2])
        half = sb("half", [P, 1])
        zero = sb("zero", [P, 1])
        pick = sb("pick", [64, 2])

        acc = [ctx.enter_context(nc.psum_tensor(f"acc{m}", [P, S], F32)) for m in range(KT)]
        ring = [ctx.enter_context(nc.psum_tensor(f"ring{m}", [P, S], F32)) for m in range(4)]

        SLOT = {"gate": 0}
        n_slots = 1
        for u in range(UNITS):
            if u == SH:
                SLOT["wt"] = n_slots
                n_slots += 1
            for what in ("h0", "h1", *(("wb",) if u >= SH else ()), "z0", "z1"):
                SLOT[what, u] = n_slots
                n_slots += 1
        assert n_slots % len(ring) == 0

        def bank(key):
            return ring[SLOT[key] % len(ring)]

        def filled(i, j, key):
            return i * (C * n_slots) + j * n_slots + SLOT[key] + 1

        def units(i, j, u):
            return i * (C * UNITS) + j * UNITS + u

        s_const = sem("s_const")
        s_bout = sem("s_bout")
        s_prep = sem("s_prep")
        s_staged = [sem(f"s_staged{k}") for k in range(STAGES)]
        s_wsplit = sem("s_wsplit")
        s_whi = sem("s_whi")
        s_firsthi, s_first = sem("s_firsthi"), sem("s_first")
        s_gatew = sem("s_gatew")
        s_small = sem("s_small")
        s_slot = sem("s_slot")
        s_tok = sem("s_tok")
        s_dn = sem("s_dn")
        s_acc = sem("s_acc")
        s_gatecopy = sem("s_gatecopy")
        s_exp = sem("s_exp")
        s_wt = sem("s_wt")
        s_h = sem("s_h")
        s_silu = sem("s_silu")
        s_lg = sem("s_lg")
        s_dif = sem("s_dif")
        s_gw = sem("s_gw")
        s_hsplit = sem("s_hsplit")
        s_wb = sem("s_wb")
        s_zread = sem("s_zread")
        s_gsplit = sem("s_gsplit")
        s_xhi = sem("s_xhi")
        s_xt = sem("s_xt")
        s_accfree = sem("s_accfree")
        s_xload = [sem("s_xload_hi"), sem("s_xload_lo")]
        s_res = [sem("s_res0"), sem("s_res1")]
        s_late = [sem("s_late0"), sem("s_late1")]
        s_stats = sem("s_stats")
        s_var = sem("s_var")
        s_pow0 = sem("s_pow0")
        s_pow = sem("s_pow")
        s_y = sem("s_y")
        s_out = [sem("s_out0"), sem("s_out1")]
        s_link = sem("s_link")
        s_pl = sem("s_pl")

        pieces, need = [], {}
        for u in range(UNITS):
            e = u - SH
            up_src = io["Wsu"][:, u * E:(u + 1) * E] if u < SH else io["Wup"][e]
            sw_src = io["Wsa"] if u < SH else io["Wsw"][e]
            dn_src = io["Wsd"][u * E:(u + 1) * E, :] if u < SH else io["Wdn"][e]
            for k in range(0, KT, 2):
                pieces.append(([w[:, u, k:k + 2, :] for w in w_up],
                               up_src[k * P:(k + 2) * P, :].rearrange("(k p) e -> p k e", p=P), 2))
            need["up", u] = len(pieces)
            if u != 1:
                s = max(u - 1, 0)
                pieces.append(([w[:, s, :, :] for w in w_sw], sw_src.rearrange("(k p) e -> p k e", p=P), 2))
            need["sw", u] = len(pieces)
            for k in range(ET):
                pieces.append(([w[:, u, k:k + 1, :] for w in w_dn],
                               dn_src[k * P:(k + 1) * P, :].rearrange("(k p) e -> p k e", p=P), 1))
            need["dn", u] = len(pieces)

        FIRST = need["dn", 0]

        def wait_split(eng, n):
            if n <= FIRST:
                eng.wait_ge(s_first, n)
            else:
                eng.wait_ge(s_wsplit, n - FIRST)

        def piece(n):
            k = pieces[n][2]
            return stage[:, n % STAGES, :].rearrange("p (k e) -> p k e", k=k)

        def rows_tile(t, last):
            return h[:, t - STAGES, :] if last and t >= STAGES else stage[:, t % STAGES, :]

        def sw_of(u):
            return max(u - 1, 0)

        def selectors():
            split = S // P
            return [(h[0:32, 1, :].rearrange("p (n c) -> p n c", c=P), split, 0),
                    (h[0:32, 0, P:P + (N - split) * P].rearrange("p (n c) -> p n c", c=P), N - split, split)]

        s_passed = {eng: sem(f"passed_{eng}") for eng in ("sp", "pool", "dve")}

        block = ctx.enter_context(nc.Block())

        @block.sync
        def _(sp):
            def load_x(e):
                for part in range(2):
                    sp.dma_start(xt[part][:].bitcast(F32),
                                 x2t_dram[part, e].bitcast(F32)).then_inc(s_xload[part], 16)

            for dst, src in [(h[:, 0, 0:C * KT * NE], io["w_gate"]), (b_up[:], io["b_up"]), (b_sw[:], io["b_sw"]),
                             (b_gate[:], io["bg"].unsqueeze(0).to_broadcast([P, C, NE]))]:
                sp.dma_start(dst, src).then_inc(s_const, 16)
            for n, (_, src, k) in enumerate(pieces):
                if n == STAGES:
                    sp.dma_start(h[32:64, 1, :], io["b_out"]).then_inc(s_bout, 16)
                if n >= STAGES:
                    wait_split(sp, n - STAGES + 1)
                sp.dma_start(piece(n), src).then_inc(s_staged[n % STAGES], 16)
            wait_split(sp, len(pieces))

            def chunk(i, e, last):
                if not last:
                    apart(sp, s_slot, filled(i, C - 1, ("h1", UNITS - 1)), s_passed["sp"])
                    load_x(i)
                for first in range(0, TT, STAGES):
                    for t in range(first, first + STAGES):
                        k = t % STAGES
                        if last and first:
                            apart(sp, s_gsplit, ET * units(i, C - 1, UNITS - 1) + ET, s_passed["sp"])
                        else:
                            apart(sp, s_out[k], 16 * (i * TT // STAGES + t // STAGES) + 16, s_passed["sp"])
                        sp.dma_start(rows_tile(t, last), x2_dram[bass.ds(e * S + t * P, P), :]
                                     ).then_inc(s_late[k] if last and first else s_res[k], 16)
                    if not last:
                        for t in range(first, first + STAGES):
                            store(i, e, t, last)
                if last:
                    for t in range(TT):
                        store(i, e, t, last)

            def store(i, e, t, last):
                apart(sp, s_y, i * TT + t + 1, s_passed["sp"])
                sp.dma_start(io["out"][bass.ds(e * S + t * P, P), :], rows_tile(t, last)
                             ).then_inc(s_out[t % STAGES], 16)

            chunk(0, B - 1, False)
            with sp.Fori(1, B - 1) as i:
                chunk(i, i - 1, False)
            chunk(B - 1, B - 2, True)
            for k in range(STAGES):
                sp.wait_ge(s_out[k], 16 * (1 + B * TT // STAGES))

        @block.gpsimd
        def _(pool):
            done = [0]

            def step(ins):
                done[0] += 1
                ins.then_inc(s_pl, 1)
                pool.wait_ge(s_pl, done[0])

            def mark(t, op, base, pattern, channel):
                step(pool.affine_select(out=t, in_=t, compare_op=op, fill=1.0, base=base,
                                        pattern=pattern, channel_multiplier=channel))

            scratch = cmp_gt[:].rearrange("p a b c -> p (a b c)")[:, 0:P]
            for t, value in ((half[:], -0.5), (zero[:], 0.0), (scratch, 0.0), (fold[:], 0.0), (before[:], 0.0),
                             (pick[:], 0.0), (gate_t[:], 0.0)):
                step(pool.memset(t, value))
            mark(scratch, ALU.not_equal, 0, [[-1, P]], 1)
            pool.memset(half[:], -0.5).then_inc(s_prep, 1)
            mark(fold[:], ALU.not_equal, 0, [[-1, NE]], 1)
            mark(fold[:], ALU.not_equal, -NE, [[-1, NE]], 1)
            mark(before[:], ALU.is_ge, 0, [[-1, NE], [1, NE]], 0)
            mark(pick[:, 0:1], ALU.is_ge, -48, [[0, 1]], 1)
            for at, experts, first in selectors():
                step(pool.memset(at, 0.0))
                mark(at, ALU.not_equal, -first, [[-1, experts], [0, P]], 1)
                mark(at, ALU.not_equal, -(first + NE), [[-1, experts], [0, P]], 1)
            pool.memset(half[:], -0.5).then_inc(s_prep, 1)
            for n, (dst, _, k) in enumerate(pieces):
                if n < FIRST:
                    continue
                pool.wait_ge(s_staged[n % STAGES], 16 * (n // STAGES + 1))
                pool.tensor_tensor(dst[0], piece(n), zero[:].unsqueeze(2).to_broadcast([P, k, PIECE // k]),
                                   ALU.add).then_inc(s_whi, 1)
                pool.wait_ge(s_whi, n - FIRST + 1)
                pool.tensor_tensor(dst[1], piece(n), dst[0].bitcast(F32), ALU.subtract).then_inc(s_wsplit, 1)
            with pool.Fori(0, B) as i:
                for t in range(TT):
                    k = t % STAGES
                    apart(pool, s_var, i * TT + t + 1, s_passed["pool"])
                    pool.tensor_scalar(rstd[:, k, 0:1], mv[:, k, 1:2], EPS, None, ALU.add).then_inc(s_pow0, 1)
                    pool.wait_ge(s_pow0, i * TT + t + 1)
                    pool.tensor_tensor(rstd[:, k, 1:2], rstd[:, k, 0:1], half[:], ALU.pow).then_inc(s_pow, 1)

        @block.scalar
        def _(act):
            for n in range(FIRST):
                act.wait_ge(s_staged[n % STAGES], 16 * (n // STAGES + 1))
                act.activation(pieces[n][0][0], piece(n), ACT.Copy).then_inc(s_firsthi, 1)
            act.wait_ge(s_const, 16 * 4)
            act.wait_ge(s_small, 3)
            with act.Fori(0, B) as i:
                for j in range(C):
                    act.wait_ge(s_slot, filled(i, j, "gate"))
                    act.activation(gate_t[:], bank("gate")[0:16, :], ACT.Copy).then_inc(s_gatecopy, 1)
                    for u in range(UNITS):
                        if u == SH:
                            act.wait_ge(s_slot, filled(i, j, "wt"))
                            act.activation(wt[0:32, :], bank("wt")[0:32, :], ACT.Copy)
                            act.activation(wt[32:64, :], bank("wt")[0:32, :], ACT.Copy).then_inc(s_wt, 1)
                        for m in range(ET):
                            act.wait_ge(s_slot, filled(i, j, (f"h{m}", u)))
                            if u:
                                act.wait_ge(s_gsplit, ET * units(i, j, u - 1) + m + 1)
                            act.activation(h[:, m, :], bank((f"h{m}", u))[:], ACT.Identity,
                                           bias=b_up[:, u, m:m + 1]).then_inc(s_h, 1)
                        if u == 0:
                            act.wait_ge(s_dif, i * C + j + 1)
                            act.activation(ex[:], lg[:], ACT.Exp).then_inc(s_exp, 1)
                        for m in range(ET):
                            z = bank((f"z{m}", u))
                            act.wait_ge(s_slot, filled(i, j, (f"z{m}", u)))
                            act.activation(z[:], z[:], ACT.Silu,
                                           bias=b_sw[:, sw_of(u), m:m + 1]).then_inc(s_silu, 1)
                    if j == 0:
                        for m in range(KT):
                            act.wait_ge(s_acc, i * C * KT + m + 1)
                            act.activation(xt[0][:, m, :], acc[m][:], ACT.Copy).then_inc(s_xhi, 1)

        @block.tensor
        def _(pe):
            def product(out, pairs):
                for n, (lhs, rhs) in enumerate(pairs):
                    mm = pe.matmul(out, lhs, rhs, start=(n == 0), stop=(n == len(pairs) - 1))
                return mm

            pe.wait_ge(s_gatew, 1)
            with pe.Fori(0, B) as i:
                for j in range(C):
                    def up(u):
                        wait_split(pe, need["up", u])
                        for m in range(ET):
                            out = bank((f"h{m}", u))
                            s = SLOT[f"h{m}", u] - len(ring)
                            if u >= 1:
                                free(s)
                            product(out[:], [(w_up[a][:, u, k, m * P:(m + 1) * P], xt[b][:, k, :])
                                             for k in range(KT) for a, b in PARTS]).then_inc(s_slot, 1)

                    def free(s):
                        key = next(k for k, v in SLOT.items() if v == s)
                        if key == "gate":
                            pe.wait_ge(s_lg, i * C + j + 1)
                        elif key == "wt":
                            pe.wait_ge(s_wt, i * C + j + 1)
                        elif key[0][0] == "h":
                            pe.wait_ge(s_h, ET * units(i, j, key[1]) + int(key[0][1]) + 1)
                        elif key[0] == "wb":
                            pe.wait_ge(s_wb, (i * C + j) * N + key[1] - SH + 1)
                        else:
                            pe.wait_ge(s_zread, ET * units(i, j, key[1]) + int(key[0][1]) + 1)

                    def gate_weights_by_token():
                        pe.wait_ge(s_small, 3)
                        pe.wait_ge(s_gatecopy, i * C + j + 1)
                        for t in range(TT):
                            mm = pe.matmul(bank("gate")[:, t * NE:(t + 1) * NE], gate_t[:, t * P:(t + 1) * P],
                                           fold[:], start=True, stop=True)
                        mm.then_inc(s_tok, 1)

                    def broadcast(u):
                        free(SLOT["wb", u] - len(ring))
                        if u == SH:
                            pe.wait_ge(s_wt, i * C + j + 1)
                        pe.matmul(bank(("wb", u))[:], rows[0:32, (u - SH) * P:(u - SH + 1) * P], wt[0:32, :],
                                  start=True, stop=True).then_inc(s_slot, 1)

                    def sw(u):
                        wait_split(pe, need["sw", u])
                        tiles = [(m, k) for m in range(ET) for k in range(ET)]
                        if u == 0:
                            tiles.sort(key=lambda tile: tile[1])
                        waited = -1
                        for m, k in tiles:
                            if k > waited:
                                waited = k
                                pe.wait_ge(s_hsplit, ET * units(i, j, u) + k + 1)
                            slot = SLOT[f"z{m}", u] - len(ring)
                            if k == 0 and slot >= 0:
                                free(slot)
                            for n, (a, b) in enumerate(PARTS):
                                mm = pe.matmul(bank((f"z{m}", u))[:], w_sw[a][:, sw_of(u), k, m * P:(m + 1) * P],
                                               hp[b][:, k, :], start=(k == 0 and n == 0),
                                               stop=(k == ET - 1 and n == len(PARTS) - 1))
                            if k == ET - 1:
                                mm.then_inc(s_slot, 1)

                    def dn(u, k):
                        wait_split(pe, need["dn", u])
                        pe.wait_ge(s_gsplit, ET * units(i, j, u) + k + 1)
                        for m in range(KT):
                            if j == 0 and u == 0 and k == 0:
                                pe.wait_ge(s_accfree, i * KT + m + 1)
                            for a, b in PARTS:
                                if j == 0:
                                    lhs, rhs = w_dn[a][:, u, k, m * P:(m + 1) * P], gp[b][:, k, :]
                                else:
                                    lhs, rhs = gp[b][:, k, m * P:(m + 1) * P], w_dn[a][:, u, k, :]
                                mm = pe.matmul(acc[m][:], lhs, rhs,
                                               start=(u == 0 and k == 0 and (a, b) == (0, 0)), stop=False)
                        mm.then_inc(s_dn, 1)

                    def out_bias():
                        for m in range(KT):
                            if j == 0:
                                lhs, rhs = rows[32:64, m * P:(m + 1) * P], wt[32:64, :]
                            else:
                                lhs, rhs = wt[32:64, m * P:(m + 1) * P], rows[32:64, 0:H]
                            pe.matmul(acc[m][:], lhs, rhs, start=False, stop=True).then_inc(s_acc, 1)

                    if j == 0:
                        for part in range(2):
                            pe.wait_ge(s_xload[part], 16 * i + 16)
                    gate_pairs = []
                    for k in range(KT):
                        if j == 1:
                            pe.wait_ge(s_xt, i * KT + k + 1)
                        at = (j * KT + k) * 16
                        for b in range(2):
                            mm = pe.matmul(bank("gate")[:], w_gate[:, at:at + P], xt[b][:, k, :],
                                           start=(k == 0 and b == 0), stop=(k == KT - 1 and b == 1))
                    mm.then_inc(s_slot, 1)
                    for u in range(UNITS):
                        up(u)
                        if u == 0:
                            gate_weights_by_token()
                        if u:
                            dn(u - 1, 0)
                        if 0 < u < UNITS - 1:
                            dn(u - 1, 1)
                        if u >= SH:
                            broadcast(u)
                        sw(u)
                        if u == UNITS - 1:
                            dn(u - 1, 1)
                        if u == SH - 1:
                            free(SLOT["wt"] - len(ring))
                            pe.wait_ge(s_gw, i * C + j + 1)
                            for t in range(TT):
                                mm = pe.transpose(bank("wt")[0:32, t * P:(t + 1) * P], gw[:, t, :],
                                                  ident[:].bitcast(F32))
                            mm.then_inc(s_slot, 1)
                    if j == 0:
                        for m in range(KT):
                            for part in range(2):
                                pe.matmul(acc[m][:], ident[:], xt[part][:, m, :], start=False, stop=False)
                    for k in range(ET):
                        dn(UNITS - 1, k)
                    out_bias()

        @block.vector
        def _(dve):
            count = [0]
            base = [0]

            def link(ins):
                count[0] += 1
                ins.then_inc(s_link, 1)
                dve.wait_ge(s_link, base[0] + count[0])

            for part in range(2):
                dve.memset(lg[:, part, :], 0.0).then_inc(s_xload[part], 16)
            link(dve.memset(w_gate[:].bitcast(mybir.dt.uint32), 0))
            dve.wait_ge(s_const, 16 * 4)
            wg = w_gate[:, 0:C * KT * 16].rearrange("p (a n) -> p a n", n=16)
            raw = h[:, 0, 0:C * KT * NE].rearrange("p (a n) -> p a n", n=NE)
            link(dve.tensor_copy(wg[:, :, 0:NE], raw))
            dve.tensor_tensor(wg[:, :, NE:16], raw, wg[:, :, 0:NE].bitcast(F32), ALU.subtract).then_inc(s_gatew, 1)
            dve.wait_ge(s_gatew, 1)

            def split_first(n):
                dve.wait_ge(s_firsthi, n + 1)
                dst = pieces[n][0]
                dve.tensor_tensor(dst[1], piece(n), dst[0].bitcast(F32), ALU.subtract).then_inc(s_first, 1)

            for n in range(FIRST - 1):
                split_first(n)
            dve.wait_ge(s_prep, 1)
            link(dve.tensor_copy(ident[:], cmp_gt[:].rearrange("p a b c -> p (a b c)")[:, 0:P]))
            dve.wait_ge(s_prep, 2)
            for at, experts, first in selectors():
                dst = rows[0:32, first * P:(first + experts) * P]
                link(dve.tensor_copy(dst.rearrange("p (n c) -> p n c", c=P), at))
            bd = rows[32:64, 0:H]
            raw = h[32:64, 1, :]
            low = h[32:64, 0, :]
            dve.wait_ge(s_bout, 16)
            link(dve.tensor_copy(bd, raw))
            link(dve.tensor_tensor(low, raw, bd.bitcast(F32), ALU.subtract))
            link(dve.tensor_scalar(pick[32:64, 1:2], pick[32:64, 0:1], -1.0, 1.0, ALU.mult, ALU.add))
            link(dve.tensor_scalar(low, low, pick[32:64, 1:2], None, ALU.mult))
            link(dve.scalar_tensor_tensor(out=bd, in0=bd.bitcast(F32), scalar=pick[32:64, 0:1], in1=low,
                                          op0=ALU.mult, op1=ALU.add))
            dve.memset(gw[:], 0.0).then_inc(s_small, 1)
            dve.memset(stats[:], 0.0).then_inc(s_small, 1)
            dve.memset(mv[:], 0.0).then_inc(s_small, 1)
            link(dve.memset(top[:], 0.0))
            dve.memset(rank[:], 0.0).then_inc(s_accfree, KT)
            dve.memset(rstd[:, 0, :], 0.0).then_inc(s_out[0], 16)
            dve.memset(rstd[:, 1, :], 0.0).then_inc(s_out[1], 16)
            split_first(FIRST - 1)
            def split_h(i, j, u):
                for m in range(ET):
                    dve.wait_ge(s_h, ET * units(i, j, u) + m + 1)
                    link(dve.tensor_copy(hp[0][:, m, :], h[:, m, :]))
                    dve.tensor_tensor(hp[1][:, m, :], h[:, m, :], hp[0][:, m, :].bitcast(F32),
                                      ALU.subtract).then_inc(s_hsplit, 1)

            def gated(i, j, u):
                if u >= SH:
                    dve.wait_ge(s_slot, filled(i, j, ("wb", u)))
                    for m in range(ET):
                        ins = dve.tensor_tensor(h[:, m, :], h[:, m, :], bank(("wb", u))[:], ALU.mult)
                        if m == ET - 1:
                            ins.then_inc(s_wb, 1)
                    dve.wait_ge(s_wb, (i * C + j) * N + u - SH + 1)
                for m in range(ET):
                    dve.wait_ge(s_silu, ET * units(i, j, u) + m + 1)
                    dve.tensor_tensor(h[:, m, :], h[:, m, :], bank((f"z{m}", u))[:],
                                      ALU.mult).then_inc(s_zread, 1)
                    dve.wait_ge(s_zread, ET * units(i, j, u) + m + 1)
                    if u:
                        dve.wait_ge(s_dn, ET * units(i, j, u - 1) + m + 1)
                    link(dve.tensor_copy(gp[0][:, m, :], h[:, m, :]))
                    dve.tensor_tensor(gp[1][:, m, :], h[:, m, :], gp[0][:, m, :].bitcast(F32),
                                      ALU.subtract).then_inc(s_gsplit, 1)

            def logits(i, j):
                dve.wait_ge(s_tok, i * C + j + 1)
                dve.tensor_tensor(lg[:], bank("gate")[:, 0:TT * NE].rearrange("p (t n) -> p t n", t=TT),
                                  b_gate[:, j, :].unsqueeze(1).to_broadcast([P, TT, NE]),
                                  ALU.add).then_inc(s_lg, 1)
                dve.wait_ge(s_lg, i * C + j + 1)
                own = lg[:].unsqueeze(3).to_broadcast([P, TT, NE, NE])
                other = lg[:].unsqueeze(2).to_broadcast([P, TT, NE, NE])
                link(dve.tensor_tensor(cmp_gt[:], other, own, ALU.is_equal))
                link(dve.tensor_tensor(cmp_gt[:], cmp_gt[:],
                                       before[:].unsqueeze(1).to_broadcast([P, TT, NE, NE]), ALU.mult))
                link(dve.tensor_reduce(rank[:], cmp_gt[:], AX.X, ALU.add))
                link(dve.tensor_tensor(cmp_gt[:], other, own, ALU.is_gt))
                link(dve.tensor_reduce(ex[:], cmp_gt[:], AX.X, ALU.add))
                link(dve.tensor_tensor(rank[:], rank[:], ex[:], ALU.add))
                link(dve.tensor_reduce(top[:], lg[:], AX.X, ALU.max))
                dve.tensor_tensor(lg[:], lg[:], top[:].unsqueeze(2).to_broadcast([P, TT, NE]),
                                  ALU.subtract).then_inc(s_dif, 1)

            def gate_softmax(i, j):
                dve.wait_ge(s_exp, i * C + j + 1)
                link(dve.scalar_tensor_tensor(out=ex[:], in0=rank[:], scalar=TOP - 0.5, in1=ex[:],
                                              op0=ALU.is_lt, op1=ALU.mult))
                link(dve.tensor_reduce(top[:], ex[:], AX.X, ALU.add))
                link(dve.reciprocal(top[:], top[:]))
                link(dve.tensor_tensor(ex[:], ex[:], top[:].unsqueeze(2).to_broadcast([P, TT, NE]),
                                       ALU.mult))
                link(dve.memset(ex[:, :, N:N + 1], 1.0))
                link(dve.memset(ex[:, :, N + 1:NE], 0.0))
                link(dve.tensor_copy(gw[:, :, 0:NE].bitcast(F32R), ex[:]))
                link(dve.tensor_tensor(gw[:, :, NE:2 * NE], ex[:], gw[:, :, 0:NE], ALU.subtract))
                dve.tensor_copy(gw[:, :, 16:32], gw[:, :, 0:16]).then_inc(s_gw, 1)

            def add(i, t, last=False):
                k, y = t % STAGES, rows_tile(t, last)
                dve.wait_ge(s_acc, (i * C + C - 1) * KT + t + 1)
                if last:
                    dve.wait_ge(s_late[k], 16)
                else:
                    dve.wait_ge(s_res[k], 16 * (i * (TT // STAGES) + t // STAGES + 1))
                dve.tensor_tensor(y, y, acc[t][:], ALU.add).then_inc(s_accfree, 1)
                dve.wait_ge(s_accfree, KT + i * TT + t + 1)
                dve.bn_stats(stats[:, k, :], y).then_inc(s_stats, 1)
                apart(dve, s_stats, i * TT + t + 1, s_passed["dve"])
                dve.bn_aggr(mv[:, k, :], stats[:, k, :]).then_inc(s_var, 1)

            def norm(i, t, last=False):
                k, y = t % STAGES, rows_tile(t, last)
                dve.wait_ge(s_var, i * TT + t + 1)
                dve.wait_ge(s_pow, i * TT + t + 1)
                dve.tensor_scalar(y, y, mv[:, k, 0:1], rstd[:, k, 1:2], ALU.subtract, ALU.mult).then_inc(s_y, 1)

            def first_unit(i, j):
                split_h(i, j, 0)
                logits(i, j)
                if j == 0 and i is not first:
                    for t in range(STAGES, TT):
                        add(i - 1, t)
                gated(i, j, 0)
                if j == 0 and i is not first:
                    for t in range(STAGES, TT):
                        norm(i - 1, t)
                gate_softmax(i, j)

            def chunk(i, last):
                base[0] = i * FFN_LINKS
                count[0] = s0
                for j in range(C):
                    if j:
                        first_unit(i, j)
                    for u in range(1, UNITS):
                        split_h(i, j, u)
                        gated(i, j, u)
                    if j == 0:
                        for m in range(KT):
                            dve.wait_ge(s_xhi, i * KT + m + 1)
                            dve.tensor_tensor(xt[1][:, m, :], acc[m][:], xt[0][:, m, :].bitcast(F32),
                                              ALU.subtract).then_inc(s_xt, 1)
                for t in range(STAGES):
                    add(i, t)
                for t in range(STAGES):
                    norm(i, t)
                if last:
                    for t in range(STAGES, TT):
                        add(i, t, last)
                    for t in range(STAGES, TT):
                        norm(i, t, last)
                else:
                    first_unit(i + 1, 0)
                    assert count[0] == FFN_LINKS + s0, count[0] - s0

            first = 0
            first_unit(first, 0)
            s0 = count[0]
            with dve.Fori(0, B - 1) as i:
                chunk(i, False)
            chunk(B - 1, True)


def lay_out_attention(x, ctx, Wqkv, bqkv, Wo, bo, Wq, bq, Wk, bk):
    import numpy as np
    tiles = lambda a: np.ascontiguousarray(a.reshape(a.shape[0], a.shape[1], -1, P).transpose(0, 3, 2, 1))
    return dict(
        x=x.reshape(-1, H), xt=tiles(x), ctxt=tiles(ctx),
        w_qkv=np.ascontiguousarray(Wqkv.reshape(KT, P, 3, H).transpose(2, 1, 0, 3)),
        qk_bias=np.ascontiguousarray(bqkv[:2 * H].reshape(2, KT, P).transpose(2, 0, 1)),
        v_bias=np.ascontiguousarray(bqkv[2 * H:].reshape(KT, P).T), Wo=Wo, bo=bo,
        w_x=np.ascontiguousarray(np.stack([Wq, Wk]).reshape(2, 128, -1, P).transpose(3, 0, 2, 1)),
        x_bias=np.ascontiguousarray(np.stack([bq, bk], 1)))


def lay_out_ffn(Wg, bg, Wup, bup, Wsw, bsw, Wdn, bdn, Wsu, bsu, Wsa, bsa, Wsd, bsd):
    import numpy as np
    cols = lambda *v: np.ascontiguousarray(
        np.concatenate([a.reshape(-1, 2, P) for a in v]).transpose(2, 0, 1))
    return dict(
        b_up=cols(bsu, bup), b_sw=cols(bsa, bsw), bg=bg,
        w_gate=np.ascontiguousarray(Wg.reshape(2, 4, P, 8).transpose(2, 0, 1, 3).reshape(P, 64)),
        b_out=np.tile(np.concatenate([bdn, bsd[None], np.zeros_like(bsd)[None]]), (4, 1)),
        Wup=Wup, Wsw=Wsw, Wdn=Wdn, Wsu=Wsu, Wsa=Wsa, Wsd=Wsd)


def decoder_layer(nc, io, out):
    x2 = nc.dram_tensor("x2_rows", [B * S, H], F32).ap()
    x2t = nc.dram_tensor("x2_transposed", [2, B, P, KT, S], F32R).ap()
    with ExitStack() as sems:
        xt = [sems.enter_context(nc.sbuf_tensor(f"x_parts_{s}", [P, KT, S], F32R)) for s in ("hi", "lo")]
        attention(nc, sems, io, x2, x2t, xt)
        feed_forward(nc, sems, io | {"out": out}, x2, x2t, xt)


def kernel(x, ctx_1024, L0_attn_Wqkv, L0_attn_bqkv, L0_attn_Wo, L0_attn_bo, L0_xattn_Wq, L0_xattn_bq,
           L0_xattn_Wk, L0_xattn_bk, L0_ffn_Wg, L0_ffn_bg, L0_ffn_Wup, L0_ffn_bup, L0_ffn_Wsw, L0_ffn_bsw,
           L0_ffn_Wdn, L0_ffn_bdn, L0_ffn_Wsu, L0_ffn_bsu, L0_ffn_Wsa, L0_ffn_bsa, L0_ffn_Wsd, L0_ffn_bsd):
    import numpy as np
    import concourse.bacc as bacc
    from concourse.bass_utils import run_bass_kernel_spmd

    attn = [np.asarray(a) for a in (x, ctx_1024, L0_attn_Wqkv, L0_attn_bqkv, L0_attn_Wo, L0_attn_bo,
                                    L0_xattn_Wq, L0_xattn_bq, L0_xattn_Wk, L0_xattn_bk)]
    ffn = [np.asarray(a) for a in (L0_ffn_Wg, L0_ffn_bg, L0_ffn_Wup, L0_ffn_bup, L0_ffn_Wsw, L0_ffn_bsw,
                                   L0_ffn_Wdn, L0_ffn_bdn, L0_ffn_Wsu, L0_ffn_bsu, L0_ffn_Wsa, L0_ffn_bsa,
                                   L0_ffn_Wsd, L0_ffn_bsd)]
    laid = lay_out_attention(*attn) | lay_out_ffn(*ffn)
    nc = bacc.Bacc("TRN2", target_bir_lowering=False, num_devices=1)
    arrays, io = {}, {}
    for name, a in laid.items():
        arrays["in_" + name] = np.ascontiguousarray(a)
        io[name] = nc.dram_tensor("in_" + name, a.shape, mybir.dt.from_np(a.dtype), kind="ExternalInput").ap()
    out = nc.dram_tensor("out_rows", [B * S, H], F32, kind="ExternalOutput").ap()
    decoder_layer(nc, io, out)
    result = run_bass_kernel_spmd(nc, [arrays], core_ids=[0])
    return result.results[0]["out_rows"].reshape(B, S, H)
```
